# Optimizing a Trainium2 kernel written in Bass

```python
import numpy as np
import jax
import jax.numpy as jnp

def _softmax(x, axis=-1):
    return jax.nn.softmax(x, axis=axis)

def _gelu(x):
    return jax.nn.gelu(x, approximate=True)

def _silu(x):
    return jax.nn.silu(x)

def _sigmoid(x):
    return jax.nn.sigmoid(x)

def _layernorm(x, axis=-1, eps=1e-05):
    m = jnp.mean(x, axis=axis, keepdims=True)
    v = jnp.var(x, axis=axis, keepdims=True)
    return (x - m) / jnp.sqrt(v + eps)

def _scatter_add(tgt, idx, src, axis=0):
    return tgt.at[idx].add(src)

def _segment_sum(src, seg, n):
    return jax.ops.segment_sum(src, seg, n)
kernel_name = 'mk_gnn_preln_d4_gnn_r8_815775'

def setup_inputs(seed: int=0):
    np.random.seed(seed)
    _w = jnp.asarray

    def _rec_inputs():
        import jax
        import jax.numpy as jnp
        _gk = jax.random.key(seed)
        x = -0.0003019 + 1 * jax.random.normal(jax.random.fold_in(_gk, 1), (1250, 1024), jnp.float32)
        src = jax.random.randint(jax.random.fold_in(_gk, 2), (20000,), 0, 1250, jnp.int32)
        dst = jax.random.randint(jax.random.fold_in(_gk, 3), (20000,), 0, 1250, jnp.int32)
        _o = jnp.argsort(dst, stable=True)
        src = src[_o]
        dst = dst[_o]
        edge_type_8 = jax.random.randint(jax.random.fold_in(_gk, 13), (20000,), 0, 8, jnp.int32)
        return (x, src, dst, edge_type_8)
    x, src, dst, edge_type_8 = _rec_inputs()

    def _L0_gnn_setup():
        import jax, jax.numpy as jnp
        import numpy as np
        N = 2500
        E = 40000
        IN = 1024
        HID = 256
        H = 4
        D = HID // H
        OUT = 1024
        EPS = 1e-06
        NEG_SLOPE = 0.2
        key = jax.random.key(seed)
        ks = jax.random.split(key, 8)
        x = jax.random.normal(ks[0], (N, IN), dtype=jnp.float32)
        edge_index = jax.random.randint(ks[1], (2, E), 0, N, dtype=jnp.int64)
        s = 0.02
        return {'x': x, 'edge_index': edge_index, 'rms_w': jnp.ones((IN,), dtype=jnp.float32), 'W_down': jax.random.normal(ks[2], (IN, HID), dtype=jnp.float32) * s, 'Wl': jax.random.normal(ks[3], (HID, HID), dtype=jnp.float32) * s, 'Wr': jax.random.normal(ks[4], (HID, HID), dtype=jnp.float32) * s, 'att': jax.random.normal(ks[5], (H, D), dtype=jnp.float32) * s, 'W_up': jax.random.normal(ks[6], (HID, OUT), dtype=jnp.float32) * s}
    _L0_gnn_all = _L0_gnn_setup()
    _L0_gnn_in = {k: v for k, v in _L0_gnn_all.items() if k in ('rms_w', 'W_down', 'Wl', 'Wr', 'att', 'W_up')}
    del _L0_gnn_all

    def _L1_gnn_setup():
        import jax, jax.numpy as jnp
        import numpy as np
        NEG_SLOPE = 0.1
        EPS = 1e-05
        key = jax.random.key(seed)
        k1, k2, k3, k4, k5 = jax.random.split(key, 5)
        N, E, DIN, DOUT = (1250, 20000, 1024, 1024)
        x = jax.random.normal(k1, (N, DIN), dtype=jnp.float32)
        W = jax.random.normal(k2, (DIN, DOUT), dtype=jnp.float32) * 0.02
        a = jax.random.normal(k3, (1, 2 * DOUT), dtype=jnp.float32) * 0.02
        src = jax.random.randint(k4, (E,), 0, N, dtype=jnp.int64)
        dst = jax.random.randint(k5, (E,), 0, N, dtype=jnp.int64)
        return {'x': x, 'W': W, 'a': a, 'src': src, 'dst': dst}
    _L1_gnn_all = _L1_gnn_setup()
    _L1_gnn_in = {k: v for k, v in _L1_gnn_all.items() if k in ('W', 'a')}
    del _L1_gnn_all

    def _L2_gnn_setup():
        import jax, jax.numpy as jnp
        import numpy as np
        N, D, R, E = (1250, 1024, 8, 10000)

        def _rgcn(x, edge_index, edge_type, weight, root, bias):
            src, dst = (edge_index[0], edge_index[1])
            msgs = x[src]
            out = x @ root + bias
            n = x.shape[0]
            for r in range(weight.shape[0]):
                mask = (edge_type == r).astype(x.dtype)
                sums = jax.ops.segment_sum(msgs * mask[:, None], dst, num_segments=n)
                cnt = jax.ops.segment_sum(mask, dst, num_segments=n)
                mean = sums / jnp.maximum(cnt, 1.0)[:, None]
                out = out + mean @ weight[r]
            return out
        key = jax.random.key(seed)
        ks = jax.random.split(key, 8)
        s = 1.0 / np.sqrt(D)
        x = jax.random.normal(ks[0], (N, D), dtype=jnp.float32)
        edge_index = jax.random.randint(ks[1], (2, E), 0, N, dtype=jnp.int64)
        edge_type = jax.random.randint(ks[2], (E,), 0, R, dtype=jnp.int64)
        weight = jax.random.normal(ks[3], (R, D, D), dtype=jnp.float32) * s
        root = jax.random.normal(ks[4], (D, D), dtype=jnp.float32) * s
        bias = jnp.zeros((D,), dtype=jnp.float32)
        w_gate = jax.random.normal(ks[5], (2 * D, D), dtype=jnp.float32) * (1.0 / np.sqrt(2 * D))
        b_gate = jnp.zeros((D,), dtype=jnp.float32)
        return {'x': x, 'edge_index': edge_index, 'edge_type': edge_type, 'weight': weight, 'root': root, 'bias': bias, 'w_gate': w_gate, 'b_gate': b_gate}
    _L2_gnn_all = _L2_gnn_setup()
    _L2_gnn_in = {k: v for k, v in _L2_gnn_all.items() if k in ('weight', 'root', 'bias', 'w_gate', 'b_gate')}
    del _L2_gnn_all

    def _L3_gnn_setup():
        import jax, jax.numpy as jnp
        import numpy as np
        N = 2500
        E = 40000
        D_IN = 1024
        D_OUT = 1024
        key = jax.random.key(seed)
        k1, k2, k3, k4 = jax.random.split(key, 4)
        x = jax.random.normal(k1, (N, D_IN), dtype=jnp.float32)
        edge_index = jax.random.randint(k2, (2, E), 0, N, dtype=jnp.int64)
        W = jax.random.normal(k3, (D_OUT, D_IN), dtype=jnp.float32) * (1.0 / np.sqrt(D_IN))
        b = jax.random.normal(k4, (D_OUT,), dtype=jnp.float32) * 0.01
        return {'x': x, 'edge_index': edge_index, 'W': W, 'b': b}
    _L3_gnn_all = _L3_gnn_setup()
    _L3_gnn_in = {k: v for k, v in _L3_gnn_all.items() if k in ('W', 'b')}
    del _L3_gnn_all
    return {'x': x, 'src': src, 'dst': dst, 'edge_type_8': edge_type_8, 'L0_gnn_rms_w': _L0_gnn_in['rms_w'], 'L0_gnn_W_down': _L0_gnn_in['W_down'], 'L0_gnn_Wl': _L0_gnn_in['Wl'], 'L0_gnn_Wr': _L0_gnn_in['Wr'], 'L0_gnn_att': _L0_gnn_in['att'], 'L0_gnn_W_up': _L0_gnn_in['W_up'], 'L1_gnn_W': _L1_gnn_in['W'], 'L1_gnn_a': _L1_gnn_in['a'], 'L2_gnn_weight': _L2_gnn_in['weight'], 'L2_gnn_root': _L2_gnn_in['root'], 'L2_gnn_bias': _L2_gnn_in['bias'], 'L2_gnn_w_gate': _L2_gnn_in['w_gate'], 'L2_gnn_b_gate': _L2_gnn_in['b_gate'], 'L3_gnn_W': _L3_gnn_in['W'], 'L3_gnn_b': _L3_gnn_in['b']}

def reference(x, src, dst, edge_type_8, L0_gnn_rms_w, L0_gnn_W_down, L0_gnn_Wl, L0_gnn_Wr, L0_gnn_att, L0_gnn_W_up, L1_gnn_W, L1_gnn_a, L2_gnn_weight, L2_gnn_root, L2_gnn_bias, L2_gnn_w_gate, L2_gnn_b_gate, L3_gnn_W, L3_gnn_b):
    import jax
    import jax.numpy as jnp

    def _L0_gnn_ref(x, edge_index, rms_w, W_down, Wl, Wr, att, W_up):
        import jax, jax.numpy as jnp
        import numpy as np
        N = 2500
        E = 40000
        IN = 1024
        HID = 256
        H = 4
        D = HID // H
        OUT = 1024
        EPS = 1e-06
        NEG_SLOPE = 0.2
        n = x.shape[0]
        ms = jnp.mean(jnp.square(x), axis=-1, keepdims=True)
        x = x * jax.lax.rsqrt(ms + EPS) * rms_w
        x = x @ W_down
        loop = jnp.arange(n, dtype=edge_index.dtype)
        src = jnp.concatenate([edge_index[0], loop])
        dst = jnp.concatenate([edge_index[1], loop])
        xl = (x @ Wl).reshape(n, H, D)
        xr = (x @ Wr).reshape(n, H, D)
        msg = xl[src] + xr[dst]
        act = jnp.where(msg > 0, msg, NEG_SLOPE * msg)
        e = jnp.einsum('ehd,hd->eh', act, att)
        m = jax.ops.segment_max(e, dst, num_segments=n)
        p = jnp.exp(e - m[dst])
        denom = jax.ops.segment_sum(p, dst, num_segments=n)
        alpha = p / (denom[dst] + 1e-16)
        out = jax.ops.segment_sum(alpha[..., None] * xl[src], dst, num_segments=n)
        out = out.reshape(n, HID)
        return out @ W_up

    def _L1_gnn_ref(x, W, a, src, dst):
        import jax, jax.numpy as jnp
        import numpy as np
        NEG_SLOPE = 0.1
        EPS = 1e-05
        N = x.shape[0]
        d = W.shape[1]
        h = x @ W
        a_l, a_r = (a[0, :d], a[0, d:])
        al = h @ a_l
        ar = h @ a_r
        e = jnp.exp(-jax.nn.leaky_relu(al[src] + ar[dst], negative_slope=NEG_SLOPE))
        rowsum = jax.ops.segment_sum(e, src, num_segments=N)
        h_prime = jax.ops.segment_sum(e[:, None] * h[dst], src, num_segments=N)
        h_prime = h_prime / (rowsum[:, None] + EPS)
        return jax.nn.elu(h_prime)

    def _L2_gnn_ref(x, edge_index, edge_type, weight, root, bias, w_gate, b_gate):
        import jax, jax.numpy as jnp
        import numpy as np
        N, D, R, E = (1250, 1024, 8, 10000)

        def _rgcn(x, edge_index, edge_type, weight, root, bias):
            src, dst = (edge_index[0], edge_index[1])
            msgs = x[src]
            out = x @ root + bias
            n = x.shape[0]
            for r in range(weight.shape[0]):
                mask = (edge_type == r).astype(x.dtype)
                sums = jax.ops.segment_sum(msgs * mask[:, None], dst, num_segments=n)
                cnt = jax.ops.segment_sum(mask, dst, num_segments=n)
                mean = sums / jnp.maximum(cnt, 1.0)[:, None]
                out = out + mean @ weight[r]
            return out
        u = _rgcn(x, edge_index, edge_type, weight, root, bias)
        z = jnp.concatenate([u, x], axis=1) @ w_gate + b_gate
        h = jnp.tanh(u) * z + x * (1.0 - z)
        return h

    def _L3_gnn_ref(x, edge_index, W, b):
        import jax, jax.numpy as jnp
        import numpy as np
        N = 2500
        E = 40000
        D_IN = 1024
        D_OUT = 1024
        num_nodes = x.shape[0]
        self_idx = jnp.arange(num_nodes, dtype=edge_index.dtype)
        ei = jnp.concatenate([edge_index, jnp.stack([self_idx, self_idx], axis=0)], axis=1)
        row, col = (ei[0], ei[1])
        h = jnp.einsum('nd,od->no', x, W) + b
        deg = jnp.zeros((num_nodes,), dtype=h.dtype).at[row].add(1.0)
        deg_inv_sqrt = deg ** (-0.5)
        norm = deg_inv_sqrt[row] * deg_inv_sqrt[col]
        msg = norm[:, None] * h[col]
        out = jax.ops.segment_sum(msg, row, num_segments=num_nodes)
        return out
    edge_index = jnp.stack([src, dst])
    h = jnp.maximum(_layernorm(x, axis=-1), 0.0)
    x = x + _L0_gnn_ref(h, edge_index, L0_gnn_rms_w, L0_gnn_W_down, L0_gnn_Wl, L0_gnn_Wr, L0_gnn_att, L0_gnn_W_up)
    h = jnp.maximum(_layernorm(x, axis=-1), 0.0)
    x = x + _L1_gnn_ref(h, L1_gnn_W, L1_gnn_a, src, dst)
    h = jnp.maximum(_layernorm(x, axis=-1), 0.0)
    x = x + _L2_gnn_ref(h, edge_index, edge_type_8, L2_gnn_weight, L2_gnn_root, L2_gnn_bias, L2_gnn_w_gate, L2_gnn_b_gate)
    h = jnp.maximum(_layernorm(x, axis=-1), 0.0)
    x = x + _L3_gnn_ref(h, edge_index, L3_gnn_W, L3_gnn_b)
    return x

_drawn_inputs = setup_inputs


def setup_inputs(seed=0):
    import zlib

    import numpy as np

    out = dict(_drawn_inputs(seed))
    spreads = {'L0_gnn_rms_w': (1.0, 0.6), 'L2_gnn_bias': (0.0, 0.1), 'L2_gnn_b_gate': (0.0, 0.1)}
    factors = {'L0_gnn_Wr': 64.0, 'L0_gnn_att': 64.0, 'L1_gnn_a': 3.731, 'L3_gnn_b': 8.0}
    for name, (base, spread) in spreads.items():
        noise = np.random.default_rng([zlib.crc32(name.encode()), seed]).standard_normal(out[name].shape)
        drawn = base * np.exp(spread * noise) if base else spread * noise
        out[name] = jnp.asarray(drawn.astype(out[name].dtype))
    for name, factor in factors.items():
        out[name] = (out[name] * factor).astype(out[name].dtype)
    return out
```

```python
import concourse.bass as bass
from concourse import mybir
from contextlib import ExitStack

F32 = mybir.dt.float32
F32R = mybir.dt.float32r
F16 = mybir.dt.float16
I32 = mybir.dt.int32
ALU = mybir.AluOpType
ACT = mybir.ActivationFunctionType
AX = mybir.AxisListType

P = 128
N = 1250
D = 1024
E = 20000
NT = -(-N // P)
NP = NT * P
TAIL = N - (NT - 1) * P
KD = D // P
HALF = 512
R = 8
HID, H, DH = 256, 4, 64
HK = HID // P
EP = 125
EC = E // EP
G = 4
CH = EC // G
CE = G * P
PAY = 1 + H
LATER = 1024.0
FAR = 1.0e30
DCH = [(0, 512), (512, 512), (1024, 256)]
LN_EPS = 1e-5


class Phase(ExitStack):

    def __init__(self, nc):
        super().__init__()
        self.nc, self.sems = nc, []
        self.callback(self.clear)

    def sem(self, name):
        self.sems.append(self.nc.alloc_semaphore(name))
        return self.sems[-1]

    def clear(self):
        self.nc.clear_and_free_semaphores(self.sems)
        self.nc.all_engine_barrier()


class Count:

    def __init__(self, sem):
        self.sem, self.n = sem, 0

    def up(self, instruction, by=1):
        instruction.then_inc(self.sem, by)
        self.n += by
        return self.n


class LayerNormRelu:

    def __init__(self, ctx, nc, tag, ps, src_tiles=None):
        def sem(name):
            return ctx.sem(f"{tag}_{name}")

        def sb(name, shape, dt):
            return ctx.enter_context(nc.sbuf_tensor(f"{tag}_{name}", shape, dt))

        self.nc, self.ps = nc, ps
        self.h = sb("h", [P, 2, D], F32)
        self.hi = sb("hi", [P, 2, KD, P], F32R)
        self.lo = sb("lo", [P, 2, KD, P], F32R)
        self.h_ready = sem("h_ready")
        self.turned = sem("turned")
        self.hi_ready = sem("hi_ready")
        self.lo_ready = sem("lo_ready")
        self.used = sem("used")
        self.h_read = sem("h_read")

    def turn(self, pe, ident, b):
        pe.wait_ge(self.h_ready, b + 1)
        for half in range(2):
            if b >= 2:
                pe.wait_ge(self.lo_ready, 2 * (b - 2) + half + 1)
            for k in range(4):
                last = self.nc.tensor.transpose(self.ps[2 * (b % 2) + half][:, k * P:(k + 1) * P],
                                                self.h[:, b % 2, (4 * half + k) * P:(4 * half + k + 1) * P], ident)
            last.then_inc(self.turned, 1)

    def part_hi(self, act, b):
        for half in range(2):
            act.wait_ge(self.turned, 2 * b + half + 1)
            if b >= 2 and half == 0:
                act.wait_ge(self.used, b - 1)
            self.nc.scalar.activation(self.hi[:, b % 2, 4 * half:4 * half + 4, :].rearrange("p k n -> p (k n)"),
                                      self.ps[2 * (b % 2) + half][:, :], ACT.Copy).then_inc(self.hi_ready, 1)

    def part_lo(self, dve, b):
        for half in range(2):
            dve.wait_ge(self.hi_ready, 2 * b + half + 1)
            self.nc.vector.tensor_tensor(self.lo[:, b % 2, 4 * half:4 * half + 4, :].rearrange("p k n -> p (k n)"),
                                         self.ps[2 * (b % 2) + half][:, :],
                                         self.hi[:, b % 2, 4 * half:4 * half + 4, :].rearrange("p k n -> p (k n)").bitcast(F32),
                                         ALU.subtract).then_inc(self.lo_ready, 1)

    def product(self, pe, b, w_hi, w_lo, banks, width=D):
        cuts = [(c, min(HALF, width - c)) for c in range(0, width, HALF)]
        for k in range(KD):
            if k % 4 == 0:
                pe.wait_ge(self.lo_ready, 2 * b + k // 4 + 1)
            for a, w, first, end in ((self.hi, w_hi, k == 0, False), (self.hi, w_lo, False, False),
                                     (self.lo, w_hi, False, k == KD - 1)):
                for bank, (c, n) in zip(banks, cuts):
                    last = self.nc.tensor.matmul(bank[:, 0:n], a[:, b % 2, k, :], w[:, k, c:c + n],
                                                 start=first, stop=end)
        last.then_inc(self.used, 1)
        return last


def norm_stats(nc, ctx, tag):
    def sb(name, shape, dt=F32):
        return ctx.enter_context(nc.sbuf_tensor(f"{tag}_{name}", shape, dt))
    s = {"parts": sb("parts", [P, NT, 2, 6]), "mv": sb("mv", [P, NT, 2]), "var": sb("var", [P, NT]),
         "std": sb("std", [P, NT]), "rstd": sb("rstd", [P, NT]), "shift": sb("shift", [P, NT])}
    for name in ("stat", "std_ready", "norm_ready"):
        s["s_" + name] = ctx.sem(f"{tag}_{name}")
    return s


def dve_stats(nc, dve, X, s, wait_tile=None):
    stat = Count(s["s_stat"])
    for b in range(NT):
        if wait_tile is not None:
            wait_tile(b)
        for half in range(2):
            stat.up(nc.vector.bn_stats(s["parts"][:, b, half, :], X[:, b, half * HALF:(half + 1) * HALF]))
    for b in range(NT):
        dve.wait_ge(stat.sem, 2 * b + 2)
        nc.vector.bn_aggr(s["mv"][:, b, :], s["parts"][:, b, :, :].rearrange("p a c -> p (a c)")).then_inc(stat.sem, 1)
        stat.n += 1
    dve.wait_ge(stat.sem, stat.n)
    stat.up(nc.vector.tensor_scalar_add(s["var"][:, :], s["mv"][:, :, 1], LN_EPS))
    dve.wait_ge(s["s_std_ready"], 1)
    stat.up(nc.vector.reciprocal(s["rstd"][:, :], s["std"][:, :]))
    dve.wait_ge(stat.sem, stat.n)
    nc.vector.scalar_tensor_tensor(out=s["shift"][:, :], in0=s["mv"][:, :, 0], scalar=-1.0, in1=s["rstd"][:, :],
                                   op0=ALU.mult, op1=ALU.mult).then_inc(s["s_norm_ready"], 1)


STATS = 3 * NT + 1


def act_std(nc, act, s):
    act.wait_ge(s["s_stat"], STATS)
    nc.scalar.activation(s["std"][:, :], s["var"][:, :], ACT.Sqrt).then_inc(s["s_std_ready"], 1)
    act.wait_ge(s["s_norm_ready"], 1)


def act_h(nc, act, ln, X, s, b):
    if b >= 2:
        act.wait_ge(ln.turned, 2 * (b - 2) + 2)
    nc.scalar.activation(ln.h[:, b % 2, :], X[:, b, :], ACT.Relu, bias=s["shift"][:, b:b + 1],
                         scale=s["rstd"][:, b:b + 1]).then_inc(ln.h_ready, 1)


class Weights:

    def __init__(self, ctx, nc, tag, dram, width=D):
        def sem(name):
            return ctx.sem(f"{tag}_{name}")
        self.nc, self.dram, self.width = nc, dram, width
        self.stage = ctx.enter_context(nc.sbuf_tensor(f"{tag}_stage", [P, 2, width], F32))
        self.hi = ctx.enter_context(nc.sbuf_tensor(f"{tag}_hi", [P, KD, width], F32R))
        self.lo = ctx.enter_context(nc.sbuf_tensor(f"{tag}_lo", [P, KD, width], F32R))
        self.loaded = [sem("loaded0"), sem("loaded1")]
        self.hi_out = sem("hi_out")
        self.lo_out = sem("lo_out")

    def load(self, sp):
        for k in range(KD):
            if k >= 2:
                sp.wait_ge(self.lo_out, k - 1)
            sp.dma_start(self.stage[:, k % 2, :], self.dram[k * P:(k + 1) * P, :]).then_inc(self.loaded[k % 2], 16)

    def part_hi(self, act, k):
        act.wait_ge(self.loaded[k % 2], 16 * (k // 2 + 1))
        self.nc.scalar.activation(self.hi[:, k, :], self.stage[:, k % 2, :], ACT.Copy).then_inc(self.hi_out, 1)

    def part_lo(self, dve, k):
        dve.wait_ge(self.hi_out, k + 1)
        self.nc.vector.tensor_tensor(self.lo[:, k, :], self.stage[:, k % 2, :], self.hi[:, k, :].bitcast(F32),
                                     ALU.subtract).then_inc(self.lo_out, 1)


def row_broadcast(dram_row, width):
    return dram_row.rearrange("(a n) -> a n", a=1).to_broadcast([P, width])


def edge_phase(nc, a, t, cst, X, ps, keep):
    with Phase(nc) as ctx:
        def sb(name, shape, dt=F32):
            return ctx.enter_context(nc.sbuf_tensor("e_" + name, shape, dt))

        def sem(name):
            return ctx.sem("e_" + name)

        ident, tri, ones_w = cst["ident"], cst["tri"], cst["weigh"]
        ln = LayerNormRelu(ctx, nc, "n0", ps)
        st = norm_stats(nc, ctx, "s0")
        wd = Weights(ctx, nc, "wd", a["L0_gnn_W_down"], HID)
        rms = sb("rms", [P, KD])
        wlr = sb("wlr", [P, HK, 2 * HID])
        wlr_hi, wlr_lo = sb("wlr_hi", [P, HK, 2 * HID], F32R), sb("wlr_lo", [P, HK, 2 * HID], F32R)
        att = sb("att", [P, HID])
        zero = sb("zero", [P, 6400])
        sumsq, meansq, rroot, rrms = sb("sumsq", [P, NT]), sb("meansq", [P, NT]), sb("rroot", [P, NT]), sb("rrms", [P, NT])
        sq = sb("sq", [P, D])
        xd = sb("xd", [P, 2, HID])
        xd_hi, xd_lo = sb("xd_hi", [P, 2, HK, P], F32R), sb("xd_lo", [P, 2, HK, P], F32R)
        xlr = sb("xlr", [P, 2, 2 * HID])
        sg, sv, sw = sb("sg", [P, HID]), sb("sv", [P, HID]), sb("sw", [P, HID])
        self_pay = sb("self_pay", [P, NT, PAY])
        node_i, node_f, self_idx = sb("node_i", [P, NT], I32), sb("node_f", [P, NT]), sb("self_idx", [P, NT], I32)
        src, dst, typ = sb("src", [P, EC + G], I32), sb("dst", [P, EC + G], I32), sb("typ", [P, EC], I32)
        slot_i, slot = sb("slot_i", [P, G], I32), sb("slot", [P, G])
        live = sb("live", [P, 1])
        key = [sb(f"key{q}", [P, EC + G]) for q in range(2)]
        kcol = [sb(f"kcol{q}", [P, G]) for q in range(2)]
        rel = [sb(f"rel{q}", [P, EC]) for q in range(2)]
        spill = [sb(f"spill{q}", [P, G]) for q in range(2)]
        krow = [sb(f"krow{q}", [P, CE]) for q in range(2)]
        eq = [sb(f"eq{q}", [P, G, CE], F16) for q in range(2)]
        eqd = [sb(f"eqd{q}", [P, G, P], F16) for q in range(2)]
        mult = [sb(f"mult{q}", [P, G]) for q in range(2)]
        lead = [sb(f"lead{q}", [P, G]) for q in range(2)]
        row_f = [sb(f"row_f{q}", [P, G]) for q in range(2)]
        pair_idx = [sb(f"pair_idx{u}", [P, G], I32) for u in range(2)]
        idx_s = [sb(f"idx_s{u}", [P, G], I32) for u in range(2)]
        idx_d = [sb(f"idx_d{u}", [P, G], I32) for u in range(2)]
        gl = [sb(f"gl{u}", [P, G, HID]) for u in range(2)]
        gr = [sb(f"gr{u}", [P, G, HID]) for u in range(2)]
        gv = sb("gv", [P, G, HID])
        logit = sb("logit", [P, G, H])
        pay = [sb(f"pay{u}", [P, G, PAY]) for u in range(2)]

        s_x = [sem(f"x_in{i}") for i in range(NT)]
        s_w, s_edges, s_rms = sem("w_in"), sem("edges_in"), sem("rms_in")
        s_xtail = sem("x_tail_zero")
        s_zero, s_cleared = sem("zero_ready"), [sem("pairs_cleared"), sem("typed_cleared")]
        s_rms_done = sem("wd_scaled")
        s_ss, s_ms, s_rr, s_rrms = sem("sumsq"), sem("meansq"), sem("rroot"), sem("rrms")
        s_xd, s_xdT, s_xdhi, s_xdlo, s_xlmm, s_xl = (sem(n) for n in (
            "xd_ready", "xd_turned", "xd_hi", "xd_lo", "lr_done", "xlr_ready"))
        s_wl_hi, s_wl_lo = sem("wlr_hi_out"), sem("wlr_lo_out")
        s_tab, s_xa = [sem("tab0"), sem("tab1")], sem("xl_kept")
        s_chain, s_self, s_iota, s_selfidx = sem("v_chain"), sem("self_pay_ready"), sem("iota"), sem("self_idx_ready")
        s_keys = sem("keys_ready")
        s_krow, s_krow_out, s_eq, s_mult = sem("krow_turned"), sem("krow_out"), sem("eq_ready"), sem("mult_done")
        s_idx, s_gl, s_gr, s_pay = sem("idx_ready"), [sem("gl0"), sem("gl1")], [sem("gr0"), sem("gr1")], sem("pay_ready")
        s_put = sem("pairs_put")
        s_free, s_landed, s_begun = sem("gathered_read"), sem("puts_landed"), sem("gather_begun")

        xl_dram, xr_dram, pairs, typed = t["xl"], t["xr"], t["pairs"], t["typed"]
        keep_xl, mult8, idx8 = keep["xl"], keep["mult8"], keep["idx8"]
        n_zero = [(pairs, NP * NP * PAY), (typed, R * NP * NP)]
        block = ctx.enter_context(nc.Block())

        @block.sync
        def _(sp):
            for b in range(NT):
                rows = P if b < NT - 1 else TAIL
                if b == NT - 1:
                    sp.wait_ge(s_xtail, 1)
                sp.dma_start(X[0:rows, b, :], a["x"][b * P:b * P + rows, :]).then_inc(s_x[b], 16)
            with nc.allow_non_contiguous_dma(reason="1024 scales, one per partition and tile"):
                sp.dma_start(rms[:, :], a["L0_gnn_rms_w"].rearrange("(k p) -> p k", p=P)).then_inc(s_rms, 16)
            wd.load(sp)
            for j, w in enumerate(("L0_gnn_Wl", "L0_gnn_Wr")):
                sp.dma_start(wlr[:, :, j * HID:(j + 1) * HID], a[w].rearrange("(k p) n -> p k n", p=P)).then_inc(s_w, 16)
            sp.dma_start(att[:, :], row_broadcast(a["L0_gnn_att"].rearrange("h d -> (h d)"), HID)).then_inc(s_w, 16)
            for b in range(NT):
                sp.wait_ge(s_xl, b + 1)
                sp.dma_start(xl_dram[b * P:(b + 1) * P, :], xlr[:, b % 2, 0:HID]).then_inc(s_tab[b % 2], 16)
                sp.dma_start(xr_dram[b * P:(b + 1) * P, :], xlr[:, b % 2, HID:2 * HID]).then_inc(s_tab[b % 2], 16)

        @block.gpsimd
        def _(pool):
            nc.gpsimd.iota(node_i[:, :], pattern=[[P, NT]], base=0, channel_multiplier=1).then_inc(s_iota, 1)
            nc.gpsimd.iota(slot_i[:, :], pattern=[[P, G]], base=0, channel_multiplier=1).then_inc(s_iota, 1)
            pool.wait_ge(s_cleared[0], 16 * (NP * NP * PAY // (P * 6400) + 1))
            pool.wait_ge(s_selfidx, 1)
            for b in range(NT):
                pool.wait_ge(s_self, b + 1)
                pool.indirect_dma_start(out=pairs[:, :], out_offset=bass.IndirectOffsetOnAxis(ap=self_idx[:, b:b + 1], axis=0),
                                        in_=self_pay[:, b, :], in_offset=None, compute_op=ALU.add).then_inc(s_put, 16)
            pool.wait_ge(s_tab[0], 16 * NT)
            pool.wait_ge(s_tab[1], 16 * NT)
            pool.wait_ge(s_put, 16 * NT)
            nc.gpsimd.sem_inc(s_landed, 1)

            def gather(i, u):
                pool.wait_ge(s_idx, 2 * i + u + 1)
                pool.wait_ge(s_free, 2 * i + u + 1)
                nc.gpsimd.sem_inc(s_begun, 1)
                for j in range(G):
                    pool.indirect_dma_start(out=gl[u][:, j, :], out_offset=None, in_=xl_dram[:, :],
                                            in_offset=bass.IndirectOffsetOnAxis(ap=idx_s[u][:, j:j + 1], axis=0)).then_inc(s_gl[u], 16)
                    pool.indirect_dma_start(out=gr[u][:, j, :], out_offset=None, in_=xr_dram[:, :],
                                            in_offset=bass.IndirectOffsetOnAxis(ap=idx_d[u][:, j:j + 1], axis=0)).then_inc(s_gr[u], 16)

            def put(i, u):
                pool.wait_ge(s_pay, 2 * i + u + 1)
                pool.wait_ge(s_put, (2 * i + u) * 16 * G + 16 * NT)
                nc.gpsimd.sem_inc(s_landed, 1)
                for j in range(G):
                    pool.indirect_dma_start(out=pairs[:, :], out_offset=bass.IndirectOffsetOnAxis(ap=pair_idx[u][:, j:j + 1], axis=0),
                                            in_=pay[u][:, j, :], in_offset=None, compute_op=ALU.add).then_inc(s_put, 16)

            gather(0, 0)
            with pool.Fori(0, CH // 2 - 1) as i:
                gather(i, 1)
                put(i, 0)
                gather(i + 1, 0)
                put(i, 1)
            gather(CH // 2 - 1, 1)
            put(CH // 2 - 1, 0)
            put(CH // 2 - 1, 1)
            pool.wait_ge(s_put, CH * G * 16 + 16 * NT)
            pool.wait_ge(s_cleared[1], 16 * (R * NP * NP // (P * 6400) + 1))

        @block.scalar
        def _(act):
            for name, tile in (("src", src), ("dst", dst), ("edge_type_8", typ)):
                act.wait_ge(s_xtail, 2)
                act.dma_start(tile[0:EP, 0:EC], a[name].rearrange("(p c) -> p c", c=EC)).then_inc(s_edges, 16)
            act.wait_ge(s_zero, 1)
            act.wait_ge(s_x[NT - 1], 16)
            for (tab, size), s_zeroed in zip(n_zero, s_cleared):
                tail = tab[size // tab.shape[1]:size // tab.shape[1] + CE, :].rearrange("(p n) w -> p (n w)", p=P)
                act.dma_start(tail, zero[:, 0:CE * tab.shape[1] // P]).then_inc(s_zeroed, 16)
                flat = tab[0:size // tab.shape[1], :].rearrange("a b -> (a b)").rearrange("(c p n) -> c p n", p=P, n=6400)
                for c in range(flat.shape[0]):
                    act.dma_start(flat[c], zero[:, :]).then_inc(s_zeroed, 16)
            act.wait_ge(s_rms, 16)
            for k in range(KD):
                act.wait_ge(s_rms_done, k + 1)
                nc.scalar.activation(wd.hi[:, k, :], wd.stage[:, k % 2, :], ACT.Copy).then_inc(wd.hi_out, 1)
            act.wait_ge(s_w, 48)
            nc.scalar.activation(wlr_hi[:, :, :], wlr[:, :, :], ACT.Copy).then_inc(s_wl_hi, 1)
            act_std(nc, act, st)
            for b in range(NT + 1):
                if b < NT:
                    act_h(nc, act, ln, X, st, b)
                    act.wait_ge(ln.h_ready, b + 1)
                    nc.scalar.activation(sq[:, :], ln.h[:, b % 2, :], ACT.Square, accum_out=sumsq[:, b:b + 1]).then_inc(s_ss, 1)
                    ln.part_hi(act, b)
                    act.wait_ge(s_ms, b + 1)
                    nc.scalar.activation(rroot[:, b:b + 1], meansq[:, b:b + 1], ACT.Sqrt).then_inc(s_rr, 1)
                if b >= 1:
                    c = b - 1
                    act.wait_ge(ln.used, c + 1)
                    act.wait_ge(s_rrms, c + 1)
                    if c >= 2:
                        act.wait_ge(s_xdT, c - 1)
                    nc.scalar.activation(xd[:, c % 2, :], ps[4][:, 0:HID], ACT.Copy, scale=rrms[:, c:c + 1]).then_inc(s_xd, 1)
                    act.wait_ge(s_xdT, c + 1)
                    if c >= 2:
                        act.wait_ge(s_xlmm, c - 1)
                    nc.scalar.activation(xd_hi[:, c % 2, :, :].rearrange("p k n -> p (k n)"), ps[5][:, 0:HID], ACT.Copy).then_inc(s_xdhi, 1)
                    act.wait_ge(s_xlmm, c + 1)
                    if c >= 2:
                        act.wait_ge(s_tab[c % 2], 32 * (c // 2))
                        act.wait_ge(s_self, c - 1)
                        act.wait_ge(s_xa, c - 1)
                    nc.scalar.activation(xlr[:, c % 2, :], ps[6 + c % 2][:, :], ACT.Copy).then_inc(s_xl, 1)

            def keys_out(n, q):
                act.wait_ge(s_krow, n + 1)
                act.wait_ge(s_eq, n + 1)
                nc.scalar.activation(krow[q][:, :], ps[q][:, :], ACT.Copy).then_inc(s_krow_out, 1)

            nc.scalar.sem_inc(s_krow_out, 2)
            with act.Fori(0, CH) as i:
                keys_out(2 * i, 0)
                keys_out(2 * i + 1, 1)

        @block.vector
        def _(dve):
            chain = Count(s_chain)

            def link(ins):
                chain.up(ins)
                dve.wait_ge(s_chain, chain.n)

            link(nc.vector.memset(X[:, NT - 1, :], 0.0))
            nc.vector.sem_inc(s_xtail, 1)
            for tile in (src, dst, typ):
                last = nc.vector.memset(tile[:, :], 0)
            link(last)
            nc.vector.sem_inc(s_xtail, 1)
            nc.vector.memset(zero[:, :], 0.0).then_inc(s_zero, 1)
            dve.wait_ge(s_rms, 16)
            for k in range(KD):
                dve.wait_ge(wd.loaded[k % 2], 16 * (k // 2 + 1))
                nc.vector.tensor_scalar(wd.stage[:, k % 2, :], wd.stage[:, k % 2, :], rms[:, k:k + 1], None, ALU.mult).then_inc(s_rms_done, 1)
                wd.part_lo(dve, k)
            dve.wait_ge(s_wl_hi, 1)
            nc.vector.tensor_tensor(wlr_lo[:, :, :], wlr[:, :, :], wlr_hi[:, :, :].bitcast(F32), ALU.subtract).then_inc(s_wl_lo, 1)
            dve_stats(nc, dve, X, st, lambda b: dve.wait_ge(s_x[b], 16))
            dve.wait_ge(s_iota, 2)
            link(nc.vector.tensor_copy(node_f[:, :], node_i[:, :]))
            link(nc.vector.tensor_scalar(node_f[:, :], node_f[:, :], float(NP + 1), None, ALU.mult))
            nc.vector.tensor_copy(self_idx[:, :], node_f[:, :]).then_inc(s_selfidx, 1)
            link(nc.vector.tensor_copy(slot[:, :], slot_i[:, :]))
            link(nc.vector.tensor_scalar(live[:, :], slot[:, 0:1], float(EP), None, ALU.is_lt))
            link(nc.vector.tensor_scalar(spill[0][:, :], slot[:, :], float(NP * NP), None, ALU.add))
            link(nc.vector.tensor_scalar(spill[1][:, :], slot[:, :], float(R * NP * NP), None, ALU.add))
            dve.wait_ge(s_edges, 48)
            link(nc.vector.scalar_tensor_tensor(out=key[0][:, 0:EC], in0=dst[:, 0:EC], scalar=float(NP), in1=src[:, 0:EC], op0=ALU.mult, op1=ALU.add))
            link(nc.vector.scalar_tensor_tensor(out=key[1][:, 0:EC], in0=typ[:, :], scalar=float(NP), in1=src[:, 0:EC], op0=ALU.mult, op1=ALU.add))
            link(nc.vector.scalar_tensor_tensor(out=key[1][:, 0:EC], in0=key[1][:, 0:EC], scalar=float(NP), in1=dst[:, 0:EC], op0=ALU.mult, op1=ALU.add))
            for q in range(2):
                link(nc.vector.memset(key[q][:, EC:EC + G], 0.0))
                sp_all = spill[q][:, :].unsqueeze(1).to_broadcast([P, CH, G])
                k3, r3 = (v[q][:, 0:EC].rearrange("p (c g) -> p c g", g=G) for v in (key, rel))
                link(nc.vector.tensor_tensor(r3, k3, sp_all, ALU.subtract))
                link(nc.vector.tensor_scalar(rel[q][:, :], rel[q][:, :], live[:, 0:1], None, ALU.mult))
                link(nc.vector.tensor_tensor(k3, r3, sp_all, ALU.add))
                link(nc.vector.tensor_copy(kcol[q][:, :], key[q][:, 0:G]))
            nc.vector.sem_inc(s_keys, 1)

            def self_loops(c):
                dve.wait_ge(s_xl, c + 1)
                nc.vector.tensor_copy(keep_xl[:, c, :, 0:DH], xlr[:, c % 2, 0:HID].rearrange("p (h d) -> p h d", d=DH)).then_inc(s_xa, 1)
                link(nc.vector.tensor_tensor(sg[:, :], xlr[:, c % 2, 0:HID], xlr[:, c % 2, HID:2 * HID], ALU.add))
                link(nc.vector.scalar_tensor_tensor(out=sv[:, :], in0=sg[:, :], scalar=0.2, in1=sg[:, :], op0=ALU.mult, op1=ALU.max))
                link(nc.vector.tensor_tensor(sw[:, :], sv[:, :], att[:, :], ALU.mult))
                nc.vector.tensor_reduce(self_pay[:, c, 1:PAY], sw[:, :].rearrange("p (h d) -> p h d", d=DH), axis=AX.X, op=ALU.add).then_inc(s_self, 1)

            link(nc.vector.memset(keep_xl[:, :, :, DH:DH + 2], 1.0))
            link(nc.vector.memset(self_pay[:, :, 0:1], 1.0))
            for b in range(NT + 1):
                if b < NT:
                    ln.part_lo(dve, b)
                    dve.wait_ge(s_ss, b + 1)
                    nc.vector.tensor_scalar(meansq[:, b:b + 1], sumsq[:, b:b + 1], 1.0 / D, 1e-6, ALU.mult, ALU.add).then_inc(s_ms, 1)
                    dve.wait_ge(s_rr, b + 1)
                    nc.vector.reciprocal(rrms[:, b:b + 1], rroot[:, b:b + 1]).then_inc(s_rrms, 1)
                if b >= 1:
                    dve.wait_ge(s_xdhi, b)
                    nc.vector.tensor_tensor(xd_lo[:, (b - 1) % 2, :, :].rearrange("p k n -> p (k n)"), ps[5][:, 0:HID],
                                            xd_hi[:, (b - 1) % 2, :, :].rearrange("p k n -> p (k n)").bitcast(F32), ALU.subtract).then_inc(s_xdlo, 1)
                    self_loops(b - 1)

            nc.vector.tensor_copy(idx_s[0][:, :], src[:, 0:G])
            link(nc.vector.tensor_copy(idx_d[0][:, :], dst[:, 0:G]))
            nc.vector.sem_inc(s_idx, 1)
            before = chain.n
            nc.vector.sem_inc(s_eq, 2)
            nc.vector.sem_inc(s_free, 2)

            def chunk(i, u, at):
                steps = [0]

                def step(ins):
                    ins.then_inc(s_chain, 1)
                    steps[0] += 1
                    dve.wait_ge(s_chain, at + steps[0])

                n = 2 * i + u
                cols = bass.ds(n * G, G)
                after = bass.ds(n * G + G, G)
                nc.vector.tensor_copy(idx_s[1 - u][:, :], src[:, after])
                step(nc.vector.tensor_copy(idx_d[1 - u][:, :], dst[:, after]))
                nc.vector.sem_inc(s_idx, 1)
                for q in range(2):
                    dve.wait_ge(s_krow_out, 2 * n + q + 3)
                    dve.wait_ge(s_mult, 2 * n + q + 1)
                    for g in range(G):
                        ins = nc.vector.tensor_scalar(eq[q][:, g, :], krow[q][:, :], key[q][:, bass.ds(n * G + g, 1)], None, ALU.is_equal)
                    step(ins)
                    diagonal = eq[q][:, :, :].rearrange("p g (c e) -> p (g c) e", e=P)[:, 0:G * G:G + 1, :]
                    nc.vector.tensor_tensor(eqd[q][:, :, :], diagonal, tri[:, :].unsqueeze(1).to_broadcast([P, G, P]), ALU.mult).then_inc(s_eq, 1)
                nc.vector.tensor_copy(kcol[0][:, :], key[0][:, after])
                step(nc.vector.tensor_copy(kcol[1][:, :], key[1][:, after]))
                nc.vector.sem_inc(s_keys, 1)
                dve.wait_ge(s_gl[u], (i + 1) * 16 * G)
                dve.wait_ge(s_gr[u], (i + 1) * 16 * G)
                step(nc.vector.tensor_tensor(gl[u][:, :, :], gl[u][:, :, :], gr[u][:, :, :], ALU.add))
                step(nc.vector.scalar_tensor_tensor(out=gv[:, :, :], in0=gl[u][:, :, :], scalar=0.2, in1=gl[u][:, :, :], op0=ALU.mult, op1=ALU.max))
                nc.vector.sem_inc(s_free, 1)
                step(nc.vector.tensor_tensor(gv[:, :, :], gv[:, :, :], att[:, :].unsqueeze(1).to_broadcast([P, G, HID]), ALU.mult))
                step(nc.vector.tensor_reduce(logit[:, :, :].rearrange("p g h -> p (g h)"), gv[:, :, :].rearrange("p g (h d) -> p (g h) d", d=DH), axis=AX.X, op=ALU.add))
                dve.wait_ge(s_landed, n + 1)
                for q in range(2):
                    dve.wait_ge(s_mult, 2 * n + q + 3)
                    m = mult[q][:, :] if q == 0 else mult8[:, cols]
                    step(nc.vector.tensor_copy(m, ps[2 + q][:, 0:G]))
                    step(nc.vector.tensor_scalar(lead[q][:, :], m, LATER, None, ALU.is_lt))
                    step(nc.vector.tensor_tensor(row_f[q][:, :], lead[q][:, :], rel[q][:, cols], ALU.mult))
                    step(nc.vector.tensor_tensor(pair_idx[u][:, :] if q == 0 else idx8[:, cols], row_f[q][:, :], spill[q][:, :], ALU.add))
                step(nc.vector.tensor_tensor(pay[u][:, :, 1:PAY], logit[:, :, :], mult[0][:, :].unsqueeze(2).to_broadcast([P, G, H]), ALU.mult))
                step(nc.vector.tensor_copy(pay[u][:, :, 0:1], mult[0][:, :].unsqueeze(2)))
                nc.vector.sem_inc(s_pay, 1)
                return steps[0]

            per = 18
            with dve.Fori(0, CH // 2) as i:
                got = chunk(i, 0, i * (2 * per) + before)
                assert got == per, got
                chunk(i, 1, i * (2 * per) + (before + per))

        @block.tensor
        def _(pe):
            pe.wait_ge(wd.lo_out, KD)
            pe.wait_ge(s_wl_lo, 1)
            for b in range(NT + 1):
                if b < NT:
                    ln.turn(pe, ident[:, :], b)
                    if b >= 1:
                        pe.wait_ge(s_xd, b)
                    ln.product(pe, b, wd.hi, wd.lo, [ps[4]], HID)
                if b >= 1:
                    c = b - 1
                    pe.wait_ge(s_xd, c + 1)
                    if c >= 1:
                        pe.wait_ge(s_xdlo, c)
                    for k in range(HK):
                        last = nc.tensor.transpose(ps[5][:, k * P:(k + 1) * P], xd[:, c % 2, k * P:(k + 1) * P], ident[:, :])
                    last.then_inc(s_xdT, 1)
                    pe.wait_ge(s_xdlo, c + 1)
                    if c >= 2:
                        pe.wait_ge(s_xl, c - 1)
                    for k in range(HK):
                        for x_, w_, first, end in ((xd_hi, wlr_hi, k == 0, False), (xd_hi, wlr_lo, False, False), (xd_lo, wlr_hi, False, k == HK - 1)):
                            last = nc.tensor.matmul(ps[6 + c % 2][:, :], x_[:, c % 2, k, :], w_[:, k, :], start=first, stop=end)
                    last.then_inc(s_xlmm, 1)
            pe.wait_ge(ln.lo_ready, 2 * NT)
            nc.tensor.sem_inc(s_mult, 2)
            with pe.Fori(0, CH) as i:
                pe.wait_ge(s_keys, i + 1)
                for q in range(2):
                    pe.wait_ge(s_krow_out, 2 * i + 2)
                    for g in range(G):
                        last = nc.tensor.transpose(ps[q][:, g * P:(g + 1) * P],
                                                   kcol[q][:, g:g + 1].to_broadcast([P, P]), ident[:, :])
                    last.then_inc(s_krow, 1)
                for q in range(2):
                    pe.wait_ge(s_eq, 2 * i + q + 3)
                    for j in range(G):
                        for g in range(G):
                            nc.tensor.matmul(ps[2 + q][:, j:j + 1], eq[q][:, g, j * P:(j + 1) * P],
                                             ones_w[:, (1 if g < j else 0):(2 if g < j else 1)], start=(g == 0), stop=False)
                        last = nc.tensor.matmul(ps[2 + q][:, j:j + 1], eqd[q][:, j, :], ones_w[:, 2:3], start=False, stop=True)
                    last.then_inc(s_mult, 1)




def pair_phase(nc, a, t, cst, X, ps, keep):
    with Phase(nc) as ctx:
        def sb(name, shape, dt=F32):
            return ctx.enter_context(nc.sbuf_tensor("p_" + name, shape, dt))

        def sem(name):
            return ctx.sem("p_" + name)

        ident = cst["ident"]
        row = [sb(f"row{u}", [P, NP, PAY]) for u in range(2)]
        cnt = [sb(f"cnt{u}", [P, NP]) for u in range(2)]
        inv, off = sb("inv", [P, NP]), sb("off", [P, NP])
        lg, pr, pc = sb("lg", [P, NP]), sb("pr", [P, 2, NP]), sb("pc", [P, 2, NP])
        top, neg = sb("top", [P, NT, H]), sb("neg", [P, NT, H])
        pT = sb("pT", [P, 2, NT, P])
        den, iden = sb("den", [P, H]), sb("iden", [P, H])
        agg = sb("agg", [P, HID])
        agg_hi, agg_lo = sb("agg_hi", [P, HK, P], F32R), sb("agg_lo", [P, HK, P], F32R)
        wu, wu_hi, wu_lo = sb("wu", [P, HK, D]), sb("wu_hi", [P, HK, D], F32R), sb("wu_lo", [P, HK, D], F32R)
        s_row = [sem("row_in0"), sem("row_in1")]
        s_w, s_whi, s_wlo = sem("wu_in"), sem("wu_hi_out"), sem("wu_lo_out")
        s_cnt, s_cntout = sem("cnt_ready"), [sem("cnt_out0"), sem("cnt_out1")]
        s_row_free = sem("row_read")
        s_chain, s_top, s_neg, s_exp, s_pc = sem("v_chain"), sem("top_ready"), sem("neg_ready"), sem("exp_ready"), sem("pc_ready")
        s_turn, s_pT, s_head = sem("p_turned"), sem("pT_ready"), sem("head_done")
        s_norm, s_aggT, s_ahi, s_alo, s_up, s_xadd = (sem(n) for n in (
            "agg_normed", "agg_turned", "agg_hi_out", "agg_lo_out", "up_done", "x_added"))
        s_typed = sem("typed_put")
        rows_dram, counts, typed = t["pairs"], t["counts"], t["typed"]
        keep_xl, mult8, idx8 = keep["xl"], keep["mult8"], keep["idx8"]
        block = ctx.enter_context(nc.Block())
        CUTS = [(0, 4), (4, 4), (8, 2)]

        @block.sync
        def _(sp):
            sp.dma_start(wu[:, :, :], a["L0_gnn_W_up"].rearrange("(k p) n -> p k n", p=P)).then_inc(s_w, 16)
            for b in range(NT):
                if b >= 2:
                    sp.wait_ge(s_row_free, b - 1)
                sp.dma_start(row[b % 2][:, :, :], rows_dram[b * P * NP:(b + 1) * P * NP, :].rearrange("(p n) w -> p n w", p=P)).then_inc(s_row[b % 2], 16)
                if b >= 1:
                    sp.wait_ge(s_cnt, b)
                    sp.dma_start(counts[(b - 1) * P:b * P, :], cnt[(b - 1) % 2][:, :]).then_inc(s_cntout[(b - 1) % 2], 16)
            sp.wait_ge(s_cnt, NT)
            sp.dma_start(counts[(NT - 1) * P:NT * P, :], cnt[(NT - 1) % 2][:, :]).then_inc(s_cntout[(NT - 1) % 2], 16)
            for u in range(2):
                sp.wait_ge(s_cntout[u], 16 * (NT // 2))

        @block.gpsimd
        def _(pool):
            for c in range(CH):
                if c >= 1:
                    pool.wait_ge(s_typed, 16 * G * c)
                for j in range(G):
                    e = c * G + j
                    pool.indirect_dma_start(out=typed[:, :], out_offset=bass.IndirectOffsetOnAxis(ap=idx8[:, e:e + 1], axis=0),
                                            in_=mult8[:, e:e + 1], in_offset=None, compute_op=ALU.add).then_inc(s_typed, 16)
            pool.wait_ge(s_typed, 16 * G * CH)

        @block.vector
        def _(dve):
            chain = Count(s_chain)

            def link(ins):
                chain.up(ins)
                dve.wait_ge(s_chain, chain.n)

            def up_add(b):
                dve.wait_ge(s_up, b + 1)
                for n in range(2):
                    last = nc.vector.tensor_tensor(X[:, b, n * HALF:(n + 1) * HALF], X[:, b, n * HALF:(n + 1) * HALF], ps[6 + n][:, :], ALU.add)
                last.then_inc(s_xadd, 1)

            def finish(b):
                dve.wait_ge(s_head, H * (b + 1))
                sums = ps[4][:, 0:H * (DH + 2)].rearrange("p (h d) -> p h d", d=DH + 2)
                link(nc.vector.tensor_scalar_add(den[:, :].unsqueeze(2), sums[:, :, DH:DH + 1], 1e-16))
                link(nc.vector.reciprocal(iden[:, :], den[:, :]))
                nc.vector.tensor_tensor(agg[:, :].rearrange("p (h d) -> p h d", d=DH), sums[:, :, 0:DH],
                                        iden[:, :].unsqueeze(2).to_broadcast([P, H, DH]), ALU.mult).then_inc(s_norm, 1)
                dve.wait_ge(s_ahi, b + 1)
                nc.vector.tensor_tensor(agg_lo[:, :, :].rearrange("p k n -> p (k n)"), ps[5][:, 0:HID],
                                        agg_hi[:, :, :].rearrange("p k n -> p (k n)").bitcast(F32), ALU.subtract).then_inc(s_alo, 1)

            dve.wait_ge(s_whi, 1)
            nc.vector.tensor_tensor(wu_lo[:, :, :], wu[:, :, :], wu_hi[:, :, :].bitcast(F32), ALU.subtract).then_inc(s_wlo, 1)
            def prepare(n):
                b, h = n // H, n % H
                u = b % 2
                if h == 0:
                    dve.wait_ge(s_row[u], 16 * (b // 2 + 1))
                    if b >= 2:
                        dve.wait_ge(s_cntout[u], 16 * (b // 2))
                    link(nc.vector.tensor_copy(cnt[u][:, :].unsqueeze(2), row[u][:, :, 0:1]))
                    nc.vector.sem_inc(s_cnt, 1)
                    nc.vector.tensor_scalar(off[:, :], cnt[u][:, :], 0.5, -FAR, ALU.is_lt, ALU.mult)
                    link(nc.vector.tensor_scalar_max(inv[:, :], cnt[u][:, :], 1.0))
                    link(nc.vector.reciprocal(inv[:, :], inv[:, :]))
                link(nc.vector.tensor_tensor(lg[:, :].unsqueeze(2), row[u][:, :, 1 + h:2 + h], inv[:, :].unsqueeze(2), ALU.mult))
                if h == H - 1:
                    nc.vector.sem_inc(s_row_free, 1)
                link(nc.vector.tensor_tensor(pr[:, n % 2, :], lg[:, :], off[:, :], ALU.add))
                link(nc.vector.tensor_reduce(top[:, b, h:h + 1], pr[:, n % 2, :], axis=AX.X, op=ALU.max))
                nc.vector.tensor_scalar(neg[:, b, h:h + 1], top[:, b, h:h + 1], -1.0, None, ALU.mult).then_inc(s_neg, 1)

            def weigh(n):
                dve.wait_ge(s_exp, n + 1)
                if n >= 2:
                    dve.wait_ge(s_turn, 3 * (n - 1))
                nc.vector.tensor_tensor(pc[:, n % 2, :], pr[:, n % 2, :], cnt[n // H % 2][:, :], ALU.mult).then_inc(s_pc, 1)

            prepare(0)
            for n in range(NT * H):
                if n + 1 < NT * H:
                    if n >= 1:
                        dve.wait_ge(s_pc, n)
                    prepare(n + 1)
                weigh(n)
                if n % H == 1 and n > H:
                    finish(n // H - 1)
                if n % H == 3 and n > H:
                    up_add(n // H - 1)
            finish(NT - 1)
            up_add(NT - 1)
            dve.wait_ge(s_xadd, NT)

        @block.scalar
        def _(act):
            act.wait_ge(s_w, 16)
            nc.scalar.activation(wu_hi[:, :, :], wu[:, :, :], ACT.Copy).then_inc(s_whi, 1)

            def evac(n):
                for c, (k0, kn) in enumerate(CUTS):
                    act.wait_ge(s_turn, 3 * n + c + 1)
                    if n >= 2 and c == 0:
                        act.wait_ge(s_head, n - 1)
                    nc.scalar.activation(pT[:, n % 2, k0:k0 + kn, :].rearrange("p k n -> p (k n)"), ps[(3 * n + c) % 4][:, 0:kn * P], ACT.Copy).then_inc(s_pT, 1)

            def agg_hi_out(b):
                act.wait_ge(s_aggT, b + 1)
                if b >= 1:
                    act.wait_ge(s_up, b)
                nc.scalar.activation(agg_hi[:, :, :].rearrange("p k n -> p (k n)"), ps[5][:, 0:HID], ACT.Copy).then_inc(s_ahi, 1)

            for b in range(NT):
                for h in range(H):
                    n = b * H + h
                    act.wait_ge(s_neg, n + 1)
                    nc.scalar.activation(pr[:, n % 2, :], pr[:, n % 2, :], ACT.Exp, bias=neg[:, b, h:h + 1]).then_inc(s_exp, 1)
                    if n >= 1:
                        evac(n - 1)
                    if h == 1 and b >= 1:
                        agg_hi_out(b - 1)
            evac(NT * H - 1)
            agg_hi_out(NT - 1)

        @block.tensor
        def _(pe):
            def turn_up(b):
                pe.wait_ge(s_norm, b + 1)
                if b >= 1:
                    pe.wait_ge(s_alo, b)
                for k in range(HK):
                    last = nc.tensor.transpose(ps[5][:, k * P:(k + 1) * P], agg[:, k * P:(k + 1) * P], ident[:, :])
                last.then_inc(s_aggT, 1)
                pe.wait_ge(s_alo, b + 1)
                if b >= 1:
                    pe.wait_ge(s_xadd, b)
                for k in range(HK):
                    for x_, w_, first, end in ((agg_hi, wu_hi, k == 0, False), (agg_hi, wu_lo, False, False), (agg_lo, wu_hi, False, k == HK - 1)):
                        for n in range(2):
                            last = nc.tensor.matmul(ps[6 + n][:, :], x_[:, k, :], w_[:, k, n * HALF:(n + 1) * HALF], start=first, stop=end)
                last.then_inc(s_up, 1)

            def turn_p(n):
                pe.wait_ge(s_pc, n + 1)
                for c, (k0, kn) in enumerate(CUTS):
                    g = 3 * n + c
                    if g >= 4:
                        pe.wait_ge(s_pT, g - 3)
                    for k in range(kn):
                        last = nc.tensor.transpose(ps[g % 4][:, k * P:(k + 1) * P], pc[:, n % 2, (k0 + k) * P:(k0 + k + 1) * P], ident[:, :])
                    last.then_inc(s_turn, 1)

            def weigh(n):
                b, h = n // H, n % H
                pe.wait_ge(s_pT, 3 * n + 3)
                if h == 0 and b >= 1:
                    pe.wait_ge(s_norm, b)
                for k in range(NT):
                    last = nc.tensor.matmul(ps[4][:, h * (DH + 2):(h + 1) * (DH + 2)], pT[:, n % 2, k, :], keep_xl[:, k, h, :], start=(k == 0), stop=(k == NT - 1))
                last.then_inc(s_head, 1)

            pe.wait_ge(s_wlo, 1)
            for n in range(NT * H):
                turn_p(n)
                if n >= 1:
                    weigh(n - 1)
                    if n % H == 1 and n > H:
                        turn_up(n // H - 1)
            weigh(NT * H - 1)
            turn_up(NT - 1)


def product_phase(nc, a, t, cst, X, ps, tag, weight, finish):
    with Phase(nc) as ctx:
        ln = LayerNormRelu(ctx, nc, tag, ps)
        st = norm_stats(nc, ctx, tag + "s")
        w = Weights(ctx, nc, tag + "w", weight)
        done = ctx.sem(tag + "_read")
        f = finish(ctx, ln, done)
        block = ctx.enter_context(nc.Block())

        @block.sync
        def _(sp):
            w.load(sp)
            f.sync(sp)

        @block.gpsimd
        def _(pool):
            f.gpsimd(pool)

        @block.scalar
        def _(act):
            w.part_hi(act, 0)
            w.part_hi(act, 1)
            act_std(nc, act, st)
            for k in range(2, KD):
                w.part_hi(act, k)
            for b in range(NT + 1):
                if b < NT:
                    f.before_h(act, b)
                    act_h(nc, act, ln, X, st, b)
                    ln.part_hi(act, b)
                if b >= 1:
                    f.scalar(act, b - 1)

        @block.vector
        def _(dve):
            w.part_lo(dve, 0)
            w.part_lo(dve, 1)
            dve_stats(nc, dve, X, st)
            for k in range(2, KD):
                w.part_lo(dve, k)
            for b in range(NT + 1):
                if b < NT:
                    ln.part_lo(dve, b)
                if b >= 1:
                    f.vector(dve, b - 1)
            f.vector_end(dve)

        @block.tensor
        def _(pe):
            ln.turn(pe, cst["ident"][:, :], 0)
            pe.wait_ge(w.lo_out, KD)
            for b in range(NT):
                if b + 1 < NT:
                    ln.turn(pe, cst["ident"][:, :], b + 1)
                if b >= 2:
                    pe.wait_ge(done, b - 1)
                ln.product(pe, b, w.hi, w.lo, [ps[4 + 2 * (b % 2)], ps[5 + 2 * (b % 2)]])


class Finish:

    def __init__(self, nc, ctx, ln, done, ps, X):
        self.nc, self.ln, self.done, self.ps, self.X = nc, ln, done, ps, X
        self.make(ctx)

    def make(self, ctx):
        pass

    def bank(self, b, n):
        return self.ps[4 + 2 * (b % 2) + n]

    def sync(self, sp):
        pass

    def gpsimd(self, pool):
        pass

    def before_h(self, act, b):
        pass

    def scalar(self, act, b):
        pass

    def vector(self, dve, b):
        pass

    def vector_end(self, dve):
        pass


def attention_phase(nc, a, t, cst, X, ps, h1, al, ar):
    a_row = a["L1_gnn_a"].rearrange("a n -> (a n)")

    class F(Finish):
        def make(self, ctx):
            def sem(name):
                return ctx.sem("a_" + name)
            self.vec = ctx.enter_context(nc.sbuf_tensor("a_vec", [P, 2 * D], F32))
            self.prod = ctx.enter_context(nc.sbuf_tensor("a_prod", [P, D], F32))
            self.vec_in, self.chain = sem("vec_in"), sem("v_chain")

        def sync(self, sp):
            sp.dma_start(self.vec[:, :], row_broadcast(a_row, 2 * D)).then_inc(self.vec_in, 16)

        def scalar(self, act, b):
            act.wait_ge(self.ln.used, b + 1)
            for n in range(2):
                last = nc.scalar.activation(h1[:, b, n * HALF:(n + 1) * HALF], self.bank(b, n)[:, :], ACT.Copy)
            last.then_inc(self.done, 1)

        def vector(self, dve, b):
            if b == 0:
                dve.wait_ge(self.vec_in, 16)
            dve.wait_ge(self.done, b + 1)
            for j, out in enumerate((al, ar)):
                if 2 * b + j > 0:
                    dve.wait_ge(self.chain, 2 * b + j)
                nc.vector.tensor_tensor_reduce(out=self.prod[:, :], in0=h1[:, b, :], in1=self.vec[:, j * D:(j + 1) * D], scale=1.0, scalar=0.0,
                                               op0=ALU.mult, op1=ALU.add, accum_out=out[:, b:b + 1]).then_inc(self.chain, 1)

        def vector_end(self, dve):
            dve.wait_ge(self.chain, 2 * NT)

    product_phase(nc, a, t, cst, X, ps, "a1", a["L1_gnn_W"], lambda ctx, ln, done: F(nc, ctx, ln, done, ps, X))


def neighbour_phase(nc, a, t, cst, X, ps, h1, al, ar, dinv):
    with Phase(nc) as ctx:
        def sb(name, shape, dt=F32):
            return ctx.enter_context(nc.sbuf_tensor("q_" + name, shape, dt))

        def sem(name):
            return ctx.sem("q_" + name)

        ident, ones = cst["ident"], cst["ones"]
        p = sb("p", [P, NT, NP])
        al_row = sb("al_row", [P, NP])
        u1, u2, ex = sb("u1", [P, 2, NP]), sb("u2", [P, 2, NP]), sb("ex", [P, 2, NP])
        root = sb("root", [P, NT])
        rs = sb("rs", [P, NT])
        irs = sb("irs", [P, NT])
        neg, pos, en = sb("neg", [P, 2, D]), sb("pos", [P, 2, D]), sb("en", [P, 2, D])
        s_p = [sem(f"p_in{u}") for u in range(2)]
        s_deg, s_root, s_dinv = sem("deg_done"), sem("deg_root"), sem("dinv_ready")
        s_row, s_rowout = sem("al_turned"), sem("al_row_out")
        s_chain, s_u, s_ex, s_pr = sem("v_chain"), sem("u_ready"), sem("ex_ready"), sem("p_ready")
        s_agg, s_neg, s_en, s_x, s_out = sem("agg_done"), sem("neg_ready"), sem("exp_ready"), sem("x_ready"), sem("x_out")
        s_bank = sem("banks_read")
        block = ctx.enter_context(nc.Block())

        @block.sync
        def _(sp):
            for k in range(NT):
                sp.dma_start(p[:, k, :], t["counts"][k * P:(k + 1) * P, :]).then_inc(s_p[k // 5], 16)
            for b in range(NT):
                sp.wait_ge(s_x, b + 1)
                sp.dma_start(t["x2"][b * P:(b + 1) * P, :], X[:, b, :]).then_inc(s_out, 16)
            sp.wait_ge(s_out, 16 * NT)

        @block.scalar
        def _(act):
            for c in range(3):
                n = min(4, NT - 4 * c)
                act.wait_ge(s_row, c + 1)
                nc.scalar.activation(al_row[:, 4 * c * P:(4 * c + n) * P], ps[c][:, 0:n * P], ACT.Copy).then_inc(s_rowout, 1)
            act.wait_ge(s_deg, 1)
            nc.scalar.activation(root[:, :], ps[3][:, 0:NT], ACT.Sqrt).then_inc(s_root, 1)
            for k in range(NT):
                act.wait_ge(s_u, k + 1)
                if k >= 2:
                    act.wait_ge(s_pr, k - 1)
                nc.scalar.activation(ex[:, k % 2, :], u2[:, k % 2, :], ACT.Exp, scale=-1.0).then_inc(s_ex, 1)
            for b in range(NT):
                act.wait_ge(s_neg, b + 1)
                if b >= 2:
                    act.wait_ge(s_x, b - 1)
                nc.scalar.activation(en[:, b % 2, :], neg[:, b % 2, :], ACT.Exp).then_inc(s_en, 1)

        @block.vector
        def _(dve):
            chain = Count(s_chain)

            def link(ins):
                chain.up(ins)
                dve.wait_ge(s_chain, chain.n)

            dve.wait_ge(s_root, 1)
            nc.vector.reciprocal(dinv[:, :], root[:, :]).then_inc(s_dinv, 1)
            dve.wait_ge(s_rowout, 3)
            for k in range(NT):
                link(nc.vector.tensor_tensor(p[:, k, k * P:(k + 1) * P], p[:, k, k * P:(k + 1) * P], ident[:, :], ALU.subtract))
                link(nc.vector.tensor_scalar(u1[:, k % 2, :], al_row[:, :], ar[:, k:k + 1], None, ALU.add))
                if k >= 2:
                    dve.wait_ge(s_ex, k - 1)
                nc.vector.scalar_tensor_tensor(out=u2[:, k % 2, :], in0=u1[:, k % 2, :], scalar=0.1, in1=u1[:, k % 2, :], op0=ALU.mult, op1=ALU.max).then_inc(s_u, 1)
                if k >= 1:
                    dve.wait_ge(s_ex, k)
                    nc.vector.tensor_tensor(p[:, k - 1, :], p[:, k - 1, :], ex[:, (k - 1) % 2, :], ALU.mult).then_inc(s_pr, 1)
            dve.wait_ge(s_ex, NT)
            nc.vector.tensor_tensor(p[:, NT - 1, :], p[:, NT - 1, :], ex[:, (NT - 1) % 2, :], ALU.mult).then_inc(s_pr, 1)

            def start(b):
                dve.wait_ge(s_agg, b + 1)
                link(nc.vector.tensor_scalar_add(rs[:, b:b + 1], ps[6 + b % 2][:, 0:1], 1e-5))
                link(nc.vector.reciprocal(irs[:, b:b + 1], rs[:, b:b + 1]))
                if b >= 2:
                    dve.wait_ge(s_en, b - 1)
                for n in range(2):
                    last = nc.vector.tensor_scalar(neg[:, b % 2, n * HALF:(n + 1) * HALF], ps[2 * (b % 2) + n][:, :], irs[:, b:b + 1], 0.0, ALU.mult, ALU.min)
                last.then_inc(s_neg, 1)
                for n in range(2):
                    last = nc.vector.tensor_scalar(pos[:, b % 2, n * HALF:(n + 1) * HALF], ps[2 * (b % 2) + n][:, :], irs[:, b:b + 1], 0.0, ALU.mult, ALU.max)
                last.then_inc(s_bank, 1)

            def end(b):
                dve.wait_ge(s_bank, b + 1)
                link(nc.vector.tensor_tensor(X[:, b, :], X[:, b, :], pos[:, b % 2, :], ALU.add))
                dve.wait_ge(s_en, b + 1)
                nc.vector.scalar_tensor_tensor(out=X[:, b, :], in0=en[:, b % 2, :], scalar=-1.0, in1=X[:, b, :], op0=ALU.add, op1=ALU.add).then_inc(s_x, 1)

            for b in range(NT):
                start(b)
                if b >= 1:
                    end(b - 1)
            end(NT - 1)

        @block.tensor
        def _(pe):
            for c in range(3):
                for k in range(min(4, NT - 4 * c)):
                    last = nc.tensor.transpose(ps[c][:, k * P:(k + 1) * P], al[:, 4 * c + k:4 * c + k + 1].to_broadcast([P, P]), ident[:, :])
                last.then_inc(s_row, 1)
            for u in range(2):
                pe.wait_ge(s_p[u], 16 * 5)
            for b in range(NT):
                for k in range(NT):
                    last = nc.tensor.matmul(ps[3][:, b:b + 1], p[:, k, b * P:(b + 1) * P], ones[:, 0:1], start=(k == 0), stop=(k == NT - 1))
            last.then_inc(s_deg, 1)
            pe.wait_ge(s_root, 1)
            for b in range(NT):
                if b >= 2:
                    pe.wait_ge(s_bank, b - 1)
                for k in range(NT):
                    if b == 0:
                        pe.wait_ge(s_pr, k + 1)
                    first, end = k == 0, k == NT - 1
                    for n in range(2):
                        nc.tensor.matmul(ps[2 * (b % 2) + n][:, :], p[:, k, b * P:(b + 1) * P], h1[:, k, n * HALF:(n + 1) * HALF], start=first, stop=end)
                    last = nc.tensor.matmul(ps[6 + b % 2][:, 0:1], p[:, k, b * P:(b + 1) * P], ones[:, 0:1], start=first, stop=end)
                last.then_inc(s_agg, 1)


def gate_x_phase(nc, a, t, cst, X, ps, h16):
    class F(Finish):
        def make(self, ctx):
            def sem(name):
                return ctx.sem("g_" + name)
            self.bias = ctx.enter_context(nc.sbuf_tensor("g_bias", [P, D], F32))
            self.z = ctx.enter_context(nc.sbuf_tensor("g_z", [P, 2, D], F32))
            self.bias_in, self.h_out, self.z_out = sem("bias_in"), [sem("h_out0"), sem("h_out1")], [sem("z_out0"), sem("z_out1")]
            self.h_hi, self.h_lo = sem("h16_hi"), sem("h16_lo")

        def sync(self, sp):
            sp.dma_start(self.bias[:, :], row_broadcast(a["L2_gnn_b_gate"], D)).then_inc(self.bias_in, 16)
            for b in range(NT + 1):
                if b < NT:
                    sp.wait_ge(self.ln.h_ready, b + 1)
                    sp.dma_start(t["h2"][b * P:(b + 1) * P, :], self.ln.h[:, b % 2, :]).then_inc(self.h_out[b % 2], 16)
                if b >= 1:
                    sp.wait_ge(self.done, b)
                    sp.dma_start(t["zx"][(b - 1) * P:b * P, :], self.z[:, (b - 1) % 2, :]).then_inc(self.z_out[(b - 1) % 2], 16)
            for u in range(2):
                sp.wait_ge(self.z_out[u], 16 * (NT // 2))
                sp.wait_ge(self.h_out[u], 16 * (NT // 2))

        def gpsimd(self, pool):
            for b in range(NT):
                pool.wait_ge(self.ln.h_ready, b + 1)
                nc.gpsimd.tensor_copy(h16[:, 0, b, :], self.ln.h[:, b % 2, :]).then_inc(self.h_hi, 1)
                pool.wait_ge(self.h_hi, b + 1)
                nc.gpsimd.tensor_tensor(h16[:, 1, b, :], self.ln.h[:, b % 2, :], h16[:, 0, b, :], ALU.subtract).then_inc(self.h_lo, 1)

        def before_h(self, act, b):
            if b >= 2:
                act.wait_ge(self.h_lo, b - 1)
                act.wait_ge(self.h_out[b % 2], 16 * (b // 2))

        def vector(self, dve, b):
            if b == 0:
                dve.wait_ge(self.bias_in, 16)
            if b >= 2:
                dve.wait_ge(self.z_out[b % 2], 16 * (b // 2))
            dve.wait_ge(self.ln.used, b + 1)
            for n in range(2):
                last = nc.vector.tensor_tensor(self.z[:, b % 2, n * HALF:(n + 1) * HALF], self.bank(b, n)[:, :], self.bias[:, n * HALF:(n + 1) * HALF], ALU.add)
            last.then_inc(self.done, 1)

    product_phase(nc, a, t, cst, X, ps, "g2", a["L2_gnn_w_gate"][D:2 * D, :], lambda ctx, ln, done: F(nc, ctx, ln, done, ps, X))


def root_phase(nc, a, t, cst, X, ps):
    class F(Finish):
        def make(self, ctx):
            self.bias = ctx.enter_context(nc.sbuf_tensor("o_bias", [P, D], F32))
            self.bias_in = ctx.sem("o_bias_in")

        def sync(self, sp):
            sp.dma_start(self.bias[:, :], row_broadcast(a["L2_gnn_bias"], D)).then_inc(self.bias_in, 16)

        def vector(self, dve, b):
            if b == 0:
                dve.wait_ge(self.bias_in, 16)
            dve.wait_ge(self.ln.used, b + 1)
            for n in range(2):
                last = nc.vector.tensor_tensor(X[:, b, n * HALF:(n + 1) * HALF], self.bank(b, n)[:, :], self.bias[:, n * HALF:(n + 1) * HALF], ALU.add)
            last.then_inc(self.done, 1)

        def vector_end(self, dve):
            dve.wait_ge(self.done, NT)

    product_phase(nc, a, t, cst, X, ps, "o2", a["L2_gnn_root"], lambda ctx, ln, done: F(nc, ctx, ln, done, ps, X))


def relation_phase(nc, a, t, cst, X, ps, h16):
    with Phase(nc) as ctx:
        def sb(name, shape, dt=F32):
            return ctx.enter_context(nc.sbuf_tensor("r_" + name, shape, dt))

        def sem(name):
            return ctx.sem("r_" + name)

        ones16 = cst["ones16"]
        NC = len(DCH)
        WMAX = max(w for _, w in DCH)
        c16 = [sb(f"c16_{u}", [P, NT, WMAX], F16) for u in range(2)]
        s_hi, s_lo = sb("s_hi", [P, KD, WMAX], F32R), sb("s_lo", [P, KD, WMAX], F32R)
        stage = sb("stage", [P, 2, D])
        w_hi, w_lo = sb("w_hi", [P, KD, D], F32R), sb("w_lo", [P, KD, D], F32R)
        cnt = [sb(f"cnt{u}", [P, 4]) for u in range(2)]
        AB = 3
        c_in = [sem("c_in0"), sem("c_in1")]
        w_in = [sem("w_in0"), sem("w_in1")]
        s_whi, s_wlo, s_wfree = sem("w_hi_out"), sem("w_lo_out"), sem("w_used")
        s_sum, s_shi, s_slo = sem("sums_done"), sem("s_hi_out"), sem("s_lo_out")
        s_cnt, s_inv, s_chain = sem("cnt_done"), sem("inv_ready"), sem("v_chain")
        s_mm, s_add = sem("product_done"), sem("u_added")
        s_cread, s_begun = sem("c_read"), sem("load_begun")
        TILES = sum(w // P for _, w in DCH)
        table = t["typed"][0:R * NP * NP, :].rearrange("(r k p n) w -> r p k (n w)", r=R, p=P, n=NP)
        weight = a["L2_gnn_weight"]
        block = ctx.enter_context(nc.Block())

        @block.gpsimd
        def _(pool):
            def load(r, c, n, u, wait=True):
                c0, cw = DCH[c]
                if wait:
                    pool.wait_ge(s_cread, n - 1)
                    nc.gpsimd.sem_inc(s_begun, 1)
                src = table[bass.ds(r, 1)] if not isinstance(r, int) else table[r:r + 1]
                pool.dma_start(c16[u][:, :, 0:cw], src.rearrange("r p k n -> (r p) k n")[:, :, c0:c0 + cw]).then_inc(c_in[u], 16)

            for j in range(2 * NC):
                load(j // NC, j % NC, j, j % 2, j >= 2)
            with pool.Fori(1, R // 2) as i:
                for j in range(2 * NC):
                    load(2 * i + j // NC, j % NC, 2 * NC * i + j, j % 2)

        @block.sync
        def _(sp):
            def load(r, k, wait=True):
                if wait:
                    sp.wait_ge(s_wlo, r * KD + (k - 1))
                w = weight[bass.ds(r, 1)] if not isinstance(r, int) else weight[r:r + 1]
                sp.dma_start(stage[:, k % 2, :], w.rearrange("r (k p) n -> k (r p) n", p=P)[k]).then_inc(w_in[k % 2], 16)

            for k in range(KD):
                load(0, k, k >= 2)
            with sp.Fori(1, R) as r:
                for k in range(KD):
                    load(r, k)

        @block.scalar
        def _(act):
            def body(r, first):
                for c in range(NC):
                    c0, cw = DCH[c]
                    for k in range(KD):
                        g = c * KD + k
                        act.wait_ge(s_sum, r * (NC * KD) + (g + 1))
                        if not (first and c == 0) and k == 0:
                            act.wait_ge(s_mm, r * TILES + TILES * 0 + before[c])
                        nc.scalar.activation(s_hi[:, k, 0:cw], ps[g % AB][:, 0:cw], ACT.Copy).then_inc(s_shi, 1)
                        if c == 0:
                            act.wait_ge(w_in[k % 2], r * 64 + 16 * (k // 2 + 1))
                            if not first:
                                act.wait_ge(s_wfree, r * KD)
                            nc.scalar.activation(w_hi[:, k, :], stage[:, k % 2, :], ACT.Copy).then_inc(s_whi, 1)

            before = [0, 4, 8]
            body(0, True)
            with act.Fori(1, R) as r:
                body(r, False)

        @block.vector
        def _(dve):
            def body(r, first):
                for c in range(NC):
                    c0, cw = DCH[c]
                    for k in range(KD):
                        g = c * KD + k
                        dve.wait_ge(s_shi, r * (NC * KD) + (g + 1))
                        nc.vector.tensor_tensor(s_lo[:, k, 0:cw], ps[g % AB][:, 0:cw], s_hi[:, k, 0:cw].bitcast(F32), ALU.subtract).then_inc(s_slo, 1)
                        if c == 0:
                            dve.wait_ge(s_whi, r * KD + (k + 1))
                            nc.vector.tensor_tensor(w_lo[:, k, :], stage[:, k % 2, :], w_hi[:, k, :].bitcast(F32), ALU.subtract).then_inc(s_wlo, 1)
                    m = cw // P
                    u = c % 2
                    dve.wait_ge(s_cnt, r * NC + (c + 1))
                    nc.vector.tensor_scalar_max(cnt[u][:, 0:m], ps[3][:, 4 * u:4 * u + m], 1.0).then_inc(s_chain, 1)
                    dve.wait_ge(s_chain, r * (2 * NC) + (2 * c + 1))
                    nc.vector.reciprocal(cnt[u][:, 0:m], cnt[u][:, 0:m]).then_inc(s_chain, 1)
                    dve.wait_ge(s_chain, r * (2 * NC) + (2 * c + 2))
                    nc.vector.sem_inc(s_inv, 1)
                    for i in range(m):
                        b = c0 // P + i
                        dve.wait_ge(s_mm, r * TILES + (b + 1))
                        for n in range(2):
                            last = nc.vector.scalar_tensor_tensor(out=X[:, b, n * HALF:(n + 1) * HALF], in0=ps[4 + 2 * (b % 2) + n][:, :],
                                                                  scalar=cnt[u][:, i:i + 1], in1=X[:, b, n * HALF:(n + 1) * HALF], op0=ALU.mult, op1=ALU.add)
                        last.then_inc(s_add, 1)

            body(0, True)
            with dve.Fori(1, R) as r:
                body(r, False)
            dve.wait_ge(s_add, R * TILES)

        @block.tensor
        def _(pe):
            def sums(r, c, par, first):
                c0, cw = DCH[c]
                u = (par * NC + c) % 2
                pe.wait_ge(c_in[u], half(r, par) + 16 * ((par * NC + c) // 2 + 1))
                for k in range(KD):
                    g = c * KD + k
                    if not (first and g < AB):
                        pe.wait_ge(s_slo, r * (NC * KD) + (g + 1 - AB))
                    for part in range(2):
                        for j in range(NT):
                            last = nc.tensor.matmul(ps[g % AB][:, 0:cw], h16[:, part, j, k * P:(k + 1) * P], c16[u][:, j, 0:cw],
                                                    start=(part == 0 and j == 0), stop=(part == 1 and j == NT - 1))
                    last.then_inc(s_sum, 1)
                if not (first and c < 1):
                    pe.wait_ge(s_inv, r * NC + c)
                for i in range(cw // P):
                    for j in range(NT):
                        last = nc.tensor.matmul(ps[3][:, 4 * (c % 2) + i:4 * (c % 2) + i + 1], c16[u][:, j, i * P:(i + 1) * P], ones16[:, 0:1], start=(j == 0), stop=(j == NT - 1))
                last.then_inc(s_cnt, 1)
                pe.wait_ge(s_cnt, r * NC + (c + 1))
                nc.tensor.sem_inc(s_cread, 1)

            def products(r, c, first):
                c0, cw = DCH[c]
                for i in range(cw // P):
                    b = c0 // P + i
                    if not (first and b < 2):
                        pe.wait_ge(s_add, r * TILES + (b - 1))
                    for k in range(KD):
                        if i == 0:
                            pe.wait_ge(s_slo, r * (NC * KD) + (c * KD + k + 1))
                            if c == 0:
                                pe.wait_ge(s_wlo, r * KD + (k + 1))
                        for x_, w_, f, e in ((s_hi, w_hi, k == 0, False), (s_hi, w_lo, False, False), (s_lo, w_hi, False, k == KD - 1)):
                            for n in range(2):
                                last = nc.tensor.matmul(ps[4 + 2 * (b % 2) + n][:, :], x_[:, k, i * P:(i + 1) * P], w_[:, k, n * HALF:(n + 1) * HALF], start=f, stop=e)
                    last.then_inc(s_mm, 1)
                    if b == NT - 1:
                        pe.wait_ge(s_mm, r * TILES + TILES)
                        nc.tensor.sem_inc(s_wfree, KD)

            def half(r, par):
                return (r - par) * (8 * NC)

            def body(r, par, first):
                for c in range(NC):
                    sums(r, c, par, first)
                    products(r, c, first)

            body(0, 0, True)
            body(1, 1, False)
            with pe.Fori(1, R // 2) as i:
                body(2 * i, 0, False)
                body(2 * i + 1, 1, False)


def gate_phase(nc, a, t, cst, X, ps):
    with Phase(nc) as ctx:
        def sb(name, shape, dt=F32):
            return ctx.enter_context(nc.sbuf_tensor("z_" + name, shape, dt))

        def sem(name):
            return ctx.sem("z_" + name)

        w = Weights(ctx, nc, "zw", a["L2_gnn_w_gate"][0:D, :])
        hi, lo = sb("hi", [P, 2, KD, P], F32R), sb("lo", [P, 2, KD, P], F32R)
        th = sb("th", [P, 2, D])
        ins = {n: sb(n, [P, 2, D]) for n in ("zx", "h2", "x2")}
        arrived = [sem("in0"), sem("in1")]
        s_turn, s_hi, s_lo, s_mm, s_th, s_z, s_x, s_out = (sem(n) for n in (
            "turned", "hi_out", "lo_out", "product_done", "tanh_ready", "z_ready", "x_ready", "x_out"))
        s_chain = sem("v_chain")
        block = ctx.enter_context(nc.Block())

        @block.sync
        def _(sp):
            w.load(sp)
            for b in range(NT):
                if b >= 2:
                    sp.wait_ge(s_x, b - 1)
                for n in ins:
                    sp.dma_start(ins[n][:, b % 2, :], t[n][b * P:(b + 1) * P, :]).then_inc(arrived[b % 2], 16)
            for b in range(NT):
                sp.wait_ge(s_x, b + 1)
                sp.dma_start(t["x3"][b * P:(b + 1) * P, :], X[:, b, :]).then_inc(s_out, 16)
            sp.wait_ge(s_out, 16 * NT)

        @block.scalar
        def _(act):
            for k in range(KD):
                w.part_hi(act, k)
            for b in range(NT):
                for n in range(2):
                    act.wait_ge(s_turn, 2 * b + n + 1)
                    if b >= 2 and n == 0:
                        act.wait_ge(s_mm, b - 1)
                    nc.scalar.activation(hi[:, b % 2, 4 * n:4 * n + 4, :].rearrange("p k n -> p (k n)"), ps[2 * (b % 2) + n][:, :], ACT.Copy).then_inc(s_hi, 1)
                if b >= 2:
                    act.wait_ge(s_x, b - 1)
                nc.scalar.activation(th[:, b % 2, :], X[:, b, :], ACT.Tanh).then_inc(s_th, 1)

        @block.vector
        def _(dve):
            chain = Count(s_chain)

            def link(ins_):
                chain.up(ins_)
                dve.wait_ge(s_chain, chain.n)

            def lows(b):
                for n in range(2):
                    dve.wait_ge(s_hi, 2 * b + n + 1)
                    nc.vector.tensor_tensor(lo[:, b % 2, 4 * n:4 * n + 4, :].rearrange("p k n -> p (k n)"), ps[2 * (b % 2) + n][:, :],
                                            hi[:, b % 2, 4 * n:4 * n + 4, :].rearrange("p k n -> p (k n)").bitcast(F32), ALU.subtract).then_inc(s_lo, 1)

            for k in range(KD):
                w.part_lo(dve, k)
            for b in range(NT + 1):
                if b < NT:
                    lows(b)
                if b >= 1:
                    c = b - 1
                    u = c % 2
                    zx, h2, x2 = (ins[n][:, u, :] for n in ("zx", "h2", "x2"))
                    dve.wait_ge(arrived[u], 48 * (c // 2 + 1))
                    dve.wait_ge(s_mm, c + 1)
                    for n in range(2):
                        cut = slice(n * HALF, (n + 1) * HALF)
                        last = nc.vector.tensor_tensor(zx[:, cut], ps[4 + 2 * u + n][:, :], zx[:, cut], ALU.add)
                    chain.up(last)
                    dve.wait_ge(s_chain, chain.n)
                    nc.vector.sem_inc(s_z, 1)
                    dve.wait_ge(s_th, c + 1)
                    link(nc.vector.tensor_tensor(th[:, u, :], th[:, u, :], h2, ALU.subtract))
                    link(nc.vector.tensor_tensor(th[:, u, :], th[:, u, :], zx, ALU.mult))
                    link(nc.vector.tensor_tensor(x2, x2, h2, ALU.add))
                    nc.vector.tensor_tensor(X[:, c, :], x2, th[:, u, :], ALU.add).then_inc(s_x, 1)

        @block.tensor
        def _(pe):
            def turn(b):
                for n in range(2):
                    if b >= 2:
                        pe.wait_ge(s_lo, 2 * (b - 2) + n + 1)
                    for k in range(4):
                        last = nc.tensor.transpose(ps[2 * (b % 2) + n][:, k * P:(k + 1) * P], X[:, b, (4 * n + k) * P:(4 * n + k + 1) * P], cst["ident"][:, :])
                    last.then_inc(s_turn, 1)

            turn(0)
            pe.wait_ge(w.lo_out, KD)
            for b in range(NT):
                if b + 1 < NT:
                    turn(b + 1)
                if b >= 2:
                    pe.wait_ge(s_z, b - 1)
                for k in range(KD):
                    if k % 4 == 0:
                        pe.wait_ge(s_lo, 2 * b + k // 4 + 1)
                    for x_, w_, f, e in ((hi, w.hi, k == 0, False), (hi, w.lo, False, False), (lo, w.hi, False, k == KD - 1)):
                        for n in range(2):
                            last = nc.tensor.matmul(ps[4 + 2 * (b % 2) + n][:, :], x_[:, b % 2, k, :], w_[:, k, n * HALF:(n + 1) * HALF], start=f, stop=e)
                last.then_inc(s_mm, 1)


def linear_phase(nc, a, t, cst, X, ps, dinv):
    with Phase(nc) as ctx:
        def sb(name, shape, dt=F32):
            return ctx.enter_context(nc.sbuf_tensor("l_" + name, shape, dt))

        def sem(name):
            return ctx.sem("l_" + name)

        ln = LayerNormRelu(ctx, nc, "l3", ps)
        st = norm_stats(nc, ctx, "l3s")
        stage = sb("stage", [P, 2, D])
        w_hi, w_lo = sb("w_hi", [P, KD, D], F32R), sb("w_lo", [P, KD, D], F32R)
        bias = sb("bias", [P, D])
        s_in, s_bias = [sem("w_in0"), sem("w_in1")], sem("bias_in")
        s_turn, s_hi, s_lo, s_done, s_chain = sem("w_turned"), sem("w_hi_out"), sem("w_lo_out"), sem("read"), sem("v_chain")
        block = ctx.enter_context(nc.Block())

        @block.sync
        def _(sp):
            for o in range(KD):
                if o >= 2:
                    sp.wait_ge(s_turn, 2 * (o - 1))
                sp.dma_start(stage[:, o % 2, :], a["L3_gnn_W"][o * P:(o + 1) * P, :]).then_inc(s_in[o % 2], 16)
            sp.dma_start(bias[:, :], row_broadcast(a["L3_gnn_b"], D)).then_inc(s_bias, 16)

        @block.scalar
        def _(act):
            act_std(nc, act, st)
            for g in range(2 * KD):
                o, n = g // 2, g % 2
                act.wait_ge(s_turn, g + 1)
                nc.scalar.activation(w_hi[:, 4 * n:4 * n + 4, o * P:(o + 1) * P], ps[4 + g % 4][:, :].rearrange("p (k n) -> p k n", n=P), ACT.Copy).then_inc(s_hi, 1)
            for b in range(NT):
                act_h(nc, act, ln, X, st, b)
                ln.part_hi(act, b)

        @block.vector
        def _(dve):
            dve_stats(nc, dve, X, st)
            for g in range(2 * KD):
                o, n = g // 2, g % 2
                dve.wait_ge(s_hi, g + 1)
                nc.vector.tensor_tensor(w_lo[:, 4 * n:4 * n + 4, o * P:(o + 1) * P], ps[4 + g % 4][:, :].rearrange("p (k n) -> p k n", n=P),
                                        w_hi[:, 4 * n:4 * n + 4, o * P:(o + 1) * P].bitcast(F32), ALU.subtract).then_inc(s_lo, 1)
            dve.wait_ge(s_bias, 16)
            for b in range(NT + 1):
                if b < NT:
                    ln.part_lo(dve, b)
                if b >= 1:
                    c = b - 1
                    dve.wait_ge(ln.used, c + 1)
                    for n in range(2):
                        cut = slice(n * HALF, (n + 1) * HALF)
                        last = nc.vector.tensor_tensor(X[:, c, cut], ps[4 + 2 * (c % 2) + n][:, :], bias[:, cut], ALU.add)
                    last.then_inc(s_done, 1)
                    dve.wait_ge(s_done, c + 1)
                    nc.vector.tensor_scalar(X[:, c, :], X[:, c, :], dinv[:, c:c + 1], None, ALU.mult).then_inc(s_chain, 1)
            dve.wait_ge(s_chain, NT)

        @block.tensor
        def _(pe):
            for g in range(2 * KD):
                o, n = g // 2, g % 2
                pe.wait_ge(s_in[o % 2], 16 * (o // 2 + 1))
                if g >= 4:
                    pe.wait_ge(s_lo, g - 3)
                for k in range(4):
                    last = nc.tensor.transpose(ps[4 + g % 4][:, k * P:(k + 1) * P], stage[:, o % 2, (4 * n + k) * P:(4 * n + k + 1) * P], cst["ident"][:, :])
                last.then_inc(s_turn, 1)
            ln.turn(pe, cst["ident"][:, :], 0)
            pe.wait_ge(s_lo, 2 * KD)
            for b in range(NT):
                if b + 1 < NT:
                    ln.turn(pe, cst["ident"][:, :], b + 1)
                if b >= 2:
                    pe.wait_ge(s_done, b - 1)
                ln.product(pe, b, w_hi, w_lo, [ps[4 + 2 * (b % 2)], ps[5 + 2 * (b % 2)]])


def spread_phase(nc, a, t, cst, X, ps, dinv, out):
    with Phase(nc) as ctx:
        def sb(name, shape, dt=F32):
            return ctx.enter_context(nc.sbuf_tensor("f_" + name, shape, dt))

        def sem(name):
            return ctx.sem("f_" + name)

        c = sb("c", [P, NT, NP], F32R)
        y_hi, y_lo = sb("y_hi", [P, NT, D], F32R), sb("y_lo", [P, NT, D], F32R)
        x3 = sb("x3", [P, 2, D])
        s_c = [sem(f"c_in{k}") for k in range(NT)]
        s_hi, s_lo = sem("y_hi_out"), sem("y_lo_out")
        s_x, s_mm, s_add, s_out = [sem("x_in0"), sem("x_in1")], sem("sums_done"), sem("x_added"), sem("out")
        block = ctx.enter_context(nc.Block())

        @block.gpsimd
        def _(pool):
            for k in range(NT):
                pool.dma_start(c[:, k, :], t["counts"][k * P:(k + 1) * P, :]).then_inc(s_c[k], 16)

        @block.scalar
        def _(act):
            for k in range(NT):
                nc.scalar.activation(y_hi[:, k, :], X[:, k, :], ACT.Copy).then_inc(s_hi, 1)

        @block.sync
        def _(sp):
            for b in range(NT + 1):
                if b < NT:
                    if b >= 2:
                        sp.wait_ge(s_out, 16 * (b - 1))
                    sp.dma_start(x3[:, b % 2, :], t["x3"][b * P:(b + 1) * P, :]).then_inc(s_x[b % 2], 16)
                if b >= 1:
                    q = b - 1
                    rows = P if q < NT - 1 else TAIL
                    sp.wait_ge(s_add, q + 1)
                    sp.dma_start(out[q * P:q * P + rows, :], x3[0:rows, q % 2, :]).then_inc(s_out, 16)
            sp.wait_ge(s_out, 16 * NT)

        @block.vector
        def _(dve):
            for k in range(NT):
                dve.wait_ge(s_hi, k + 1)
                nc.vector.tensor_tensor(y_lo[:, k, :], X[:, k, :], y_hi[:, k, :].bitcast(F32), ALU.subtract).then_inc(s_lo, 1)
            for b in range(NT):
                dve.wait_ge(s_x[b % 2], 16 * (b // 2 + 1))
                dve.wait_ge(s_mm, b + 1)
                for n in range(2):
                    cut = slice(n * HALF, (n + 1) * HALF)
                    last = nc.vector.scalar_tensor_tensor(out=x3[:, b % 2, cut], in0=ps[2 * (b % 4) + n][:, :], scalar=dinv[:, b:b + 1],
                                                          in1=x3[:, b % 2, cut], op0=ALU.mult, op1=ALU.add)
                last.then_inc(s_add, 1)

        @block.tensor
        def _(pe):
            for b in range(NT):
                if b >= 4:
                    pe.wait_ge(s_add, b - 3)
                for k in range(NT):
                    if b == 0:
                        pe.wait_ge(s_c[k], 16)
                        pe.wait_ge(s_lo, k + 1)
                    for y, f, e in ((y_hi, k == 0, False), (y_lo, False, k == NT - 1)):
                        for n in range(2):
                            last = nc.tensor.matmul(ps[2 * (b % 4) + n][:, :], c[:, k, b * P:(b + 1) * P], y[:, k, n * HALF:(n + 1) * HALF], start=f, stop=e)
                last.then_inc(s_mm, 1)


def constants(nc, cst):
    with Phase(nc) as ctx:
        s_set, s_sel = (ctx.sem(n) for n in ("cst_set", "cst_selected"))
        block = ctx.enter_context(nc.Block())

        @block.gpsimd
        def _(pool):
            nc.gpsimd.memset(cst["ident"][:, :], 0.0).then_inc(s_set, 1)
            nc.gpsimd.memset(cst["tri"][:, :], 1.0).then_inc(s_set, 1)
            pool.wait_ge(s_set, 2)
            nc.gpsimd.affine_select(out=cst["ident"][:, :], in_=cst["ident"][:, :], compare_op=ALU.not_equal, fill=1.0,
                                    base=0, pattern=[[-1, P]], channel_multiplier=1).then_inc(s_sel, 1)
            nc.gpsimd.affine_select(out=cst["tri"][:, :], in_=cst["tri"][:, :], compare_op=ALU.is_gt, fill=0.0,
                                    base=0, pattern=[[1, P]], channel_multiplier=-1).then_inc(s_sel, 1)
            pool.wait_ge(s_sel, 2)

        @block.vector
        def _(dve):
            nc.vector.memset(cst["weigh"][:, 0:1], 1.0)
            nc.vector.memset(cst["weigh"][:, 1:2], 1.0 + LATER)
            nc.vector.memset(cst["weigh"][:, 2:3], LATER)
            nc.vector.memset(cst["ones"][:, :], 1.0)
            nc.vector.memset(cst["ones16"][:, :], 1.0)


def gnn_kernel(nc, a, out, stop=None):
    t = {"xl": nc.dram_tensor("t_xl", [NP, HID], F32, kind="Internal").ap(),
         "xr": nc.dram_tensor("t_xr", [NP, HID], F32, kind="Internal").ap(),
         "pairs": nc.dram_tensor("t_pairs", [NP * NP + CE, PAY], F32, kind="Internal").ap(),
         "typed": nc.dram_tensor("t_typed", [R * NP * NP + CE, 1], F32, kind="Internal").ap(),
         "counts": nc.dram_tensor("t_counts", [NP, NP], F32, kind="Internal").ap()}
    for n in ("x2", "x3", "h2", "zx"):
        t[n] = nc.dram_tensor("t_" + n, [NP, D], F32, kind="Internal").ap()

    with Phase(nc) as ctx:
        def sb(name, shape, dt=F32):
            return ctx.enter_context(nc.sbuf_tensor(name, shape, dt))

        ps = [ctx.enter_context(nc.psum_tensor(f"bank{i}", [P, HALF], F32)) for i in range(8)]
        cst = {"ident": sb("ident", [P, P]), "tri": sb("tri", [P, P], F16), "weigh": sb("weigh", [P, 4], F16),
               "ones": sb("ones", [P, 2]), "ones16": sb("ones16", [P, 2], F16)}
        X = sb("x", [P, NT, D])
        al, ar, dinv = sb("al", [P, NT]), sb("ar", [P, NT]), sb("dinv", [P, NT])
        constants(nc, cst)
        phases = 0
        with ExitStack() as part:
            def keep_sb(name, shape, dt=F32):
                return part.enter_context(nc.sbuf_tensor(name, shape, dt))
            keep = {"xl": keep_sb("keep_xl", [P, NT, H, DH + 2]), "mult8": keep_sb("mult8", [P, EC]), "idx8": keep_sb("idx8", [P, EC], I32)}
            edge_phase(nc, a, t, cst, X, ps, keep)
            pair_phase(nc, a, t, cst, X, ps, keep)
        with ExitStack() as part:
            h1 = part.enter_context(nc.sbuf_tensor("h1", [P, NT, D], F32))
            attention_phase(nc, a, t, cst, X, ps, h1, al, ar)
            neighbour_phase(nc, a, t, cst, X, ps, h1, al, ar, dinv)
        with ExitStack() as part:
            h16 = part.enter_context(nc.sbuf_tensor("h16", [P, 2, NT, D], F16))
            gate_x_phase(nc, a, t, cst, X, ps, h16)
            root_phase(nc, a, t, cst, X, ps)
            relation_phase(nc, a, t, cst, X, ps, h16)
        gate_phase(nc, a, t, cst, X, ps)
        linear_phase(nc, a, t, cst, X, ps, dinv)
        spread_phase(nc, a, t, cst, X, ps, dinv, out)


_INS = ["x", "src", "dst", "edge_type_8", "L0_gnn_rms_w", "L0_gnn_W_down", "L0_gnn_Wl", "L0_gnn_Wr", "L0_gnn_att", "L0_gnn_W_up",
        "L1_gnn_W", "L1_gnn_a", "L2_gnn_weight", "L2_gnn_root", "L2_gnn_bias", "L2_gnn_w_gate", "L2_gnn_b_gate", "L3_gnn_W", "L3_gnn_b"]


def kernel(**inputs):
    import numpy as _np
    import concourse.bacc as _bacc
    from concourse import mybir as _mybir
    from concourse.bass_utils import run_bass_kernel_spmd as _run

    nc = _bacc.Bacc("TRN2", target_bir_lowering=False, num_devices=1)
    arrays, args = {}, {}
    for name in _INS:
        x = _np.ascontiguousarray(inputs[name])
        arrays[f"in_{name}_dram"] = x
        args[name] = nc.dram_tensor(f"in_{name}_dram", x.shape, _mybir.dt.from_np(x.dtype), kind="ExternalInput").ap()
    out = nc.dram_tensor("out_0_dram", (N, D), _mybir.dt.float32, kind="ExternalOutput").ap()
    gnn_kernel(nc, args, out)
    r = _run(nc, [arrays], core_ids=[0])
    return r.results[0]["out_0_dram"]
```

```python
import concourse.bass as bass
from concourse import mybir
from contextlib import ExitStack

F32 = mybir.dt.float32
F32R = mybir.dt.float32r
F16 = mybir.dt.float16
I32 = mybir.dt.int32
ALU = mybir.AluOpType
ACT = mybir.ActivationFunctionType
AX = mybir.AxisListType

P = 128
N = 1250
D = 1024
E = 20000
NT = -(-N // P)
NP = NT * P
TAIL = N - (NT - 1) * P
KD = D // P
HALF = 512
R = 8
HID, H, DH = 256, 4, 64
HK = HID // P
EP = 125
EC = E // EP
G = 4
U = 4
CH = EC // G
CE = G * P
PAY = 1 + H
HL = HID + H
ZW = 3200
LATER = 1024.0
FAR = 1.0e30
DCH = [(0, 512), (512, 512), (1024, 256)]
LN_EPS = 1e-5


class Phase(ExitStack):

    def __init__(self, nc):
        super().__init__()
        self.nc, self.sems = nc, []
        self.callback(self.clear)

    def sem(self, name):
        self.sems.append(self.nc.alloc_semaphore(name))
        return self.sems[-1]

    def clear(self):
        self.nc.clear_and_free_semaphores(self.sems)
        self.nc.all_engine_barrier()


class Count:

    def __init__(self, sem):
        self.sem, self.n = sem, 0

    def up(self, instruction, by=1):
        instruction.then_inc(self.sem, by)
        self.n += by
        return self.n


class LayerNormRelu:

    def __init__(self, ctx, nc, tag, ps, src_tiles=None):
        def sem(name):
            return ctx.sem(f"{tag}_{name}")

        def sb(name, shape, dt):
            return ctx.enter_context(nc.sbuf_tensor(f"{tag}_{name}", shape, dt))

        self.nc, self.ps = nc, ps
        self.h = sb("h", [P, 2, D], F32)
        self.hi = sb("hi", [P, 2, KD, P], F32R)
        self.lo = sb("lo", [P, 2, KD, P], F32R)
        self.h_ready = sem("h_ready")
        self.turned = sem("turned")
        self.hi_ready = sem("hi_ready")
        self.lo_ready = sem("lo_ready")
        self.used = sem("used")
        self.h_read = sem("h_read")

    def turn(self, pe, ident, b):
        pe.wait_ge(self.h_ready, b + 1)
        for half in range(2):
            if b >= 2:
                pe.wait_ge(self.lo_ready, 2 * (b - 2) + half + 1)
            for k in range(4):
                last = self.nc.tensor.transpose(self.ps[2 * (b % 2) + half][:, k * P:(k + 1) * P],
                                                self.h[:, b % 2, (4 * half + k) * P:(4 * half + k + 1) * P], ident)
            last.then_inc(self.turned, 1)

    def part_hi(self, act, b):
        for half in range(2):
            act.wait_ge(self.turned, 2 * b + half + 1)
            if b >= 2 and half == 0:
                act.wait_ge(self.used, b - 1)
            self.nc.scalar.activation(self.hi[:, b % 2, 4 * half:4 * half + 4, :].rearrange("p k n -> p (k n)"),
                                      self.ps[2 * (b % 2) + half][:, :], ACT.Copy).then_inc(self.hi_ready, 1)

    def part_lo(self, dve, b):
        for half in range(2):
            dve.wait_ge(self.hi_ready, 2 * b + half + 1)
            self.nc.vector.tensor_tensor(self.lo[:, b % 2, 4 * half:4 * half + 4, :].rearrange("p k n -> p (k n)"),
                                         self.ps[2 * (b % 2) + half][:, :],
                                         self.hi[:, b % 2, 4 * half:4 * half + 4, :].rearrange("p k n -> p (k n)").bitcast(F32),
                                         ALU.subtract).then_inc(self.lo_ready, 1)

    def product(self, pe, b, w_hi, w_lo, banks, width=D, w_ready=None):
        cuts = [(c, min(HALF, width - c)) for c in range(0, width, HALF)]
        for k in range(KD):
            if k % 4 == 0:
                pe.wait_ge(self.lo_ready, 2 * b + k // 4 + 1)
            if w_ready is not None and b == 0:
                pe.wait_ge(w_ready, k + 1)
            for a, w, first, end in ((self.hi, w_hi, k == 0, False), (self.hi, w_lo, False, False),
                                     (self.lo, w_hi, False, k == KD - 1)):
                for bank, (c, n) in zip(banks, cuts):
                    last = self.nc.tensor.matmul(bank[:, 0:n], a[:, b % 2, k, :], w[:, k, c:c + n],
                                                 start=first, stop=end)
        last.then_inc(self.used, 1)
        return last


class Norm:

    def __init__(self, nc, sb):
        self.nc = nc
        self.parts, self.mv = sb("parts", [P, NT, 2, 6]), sb("mv", [P, NT, 2])
        self.var, self.std = sb("var", [P, NT]), sb("std", [P, NT])
        self.rstd, self.shift = sb("rstd", [P, NT]), sb("shift", [P, NT])

    def begin(self, ctx, tag):
        self.s_var, self.s_std = ctx.sem(tag + "_var"), ctx.sem(tag + "_std")
        self.s_rstd, self.s_ready = ctx.sem(tag + "_rstd"), ctx.sem(tag + "_norm_ready")

    def tile(self, X, b, link):
        self.nc.vector.bn_stats(self.parts[:, b, 0, :], X[:, b, 0:HALF])
        link(self.nc.vector.bn_stats(self.parts[:, b, 1, :], X[:, b, HALF:D]))
        link(self.nc.vector.bn_aggr(self.mv[:, b, :], self.parts[:, b, :, :].rearrange("p a c -> p (a c)")))

    def vector(self, dve):
        self.nc.vector.tensor_scalar_add(self.var[:, :], self.mv[:, :, 1], LN_EPS).then_inc(self.s_var, 1)
        dve.wait_ge(self.s_std, 1)
        self.nc.vector.reciprocal(self.rstd[:, :], self.std[:, :]).then_inc(self.s_rstd, 1)
        dve.wait_ge(self.s_rstd, 1)
        self.nc.vector.scalar_tensor_tensor(out=self.shift[:, :], in0=self.mv[:, :, 0], scalar=-1.0, in1=self.rstd[:, :],
                                            op0=ALU.mult, op1=ALU.mult).then_inc(self.s_ready, 1)

    def scalar(self, act):
        act.wait_ge(self.s_var, 1)
        self.nc.scalar.activation(self.std[:, :], self.var[:, :], ACT.Sqrt).then_inc(self.s_std, 1)
        act.wait_ge(self.s_ready, 1)


def act_h(nc, act, ln, X, s, b):
    if b >= 2:
        act.wait_ge(ln.turned, 2 * (b - 2) + 2)
    nc.scalar.activation(ln.h[:, b % 2, :], X[:, b, :], ACT.Relu, bias=s.shift[:, b:b + 1],
                         scale=s.rstd[:, b:b + 1]).then_inc(ln.h_ready, 1)


class Weights:

    def __init__(self, ctx, nc, tag, dram, width=D):
        def sem(name):
            return ctx.sem(f"{tag}_{name}")
        self.nc, self.dram, self.width = nc, dram, width
        self.stage = ctx.enter_context(nc.sbuf_tensor(f"{tag}_stage", [P, 2, width], F32))
        self.hi = ctx.enter_context(nc.sbuf_tensor(f"{tag}_hi", [P, KD, width], F32R))
        self.lo = ctx.enter_context(nc.sbuf_tensor(f"{tag}_lo", [P, KD, width], F32R))
        self.loaded = [sem("loaded0"), sem("loaded1")]
        self.hi_out = sem("hi_out")
        self.lo_out = sem("lo_out")

    def load(self, sp):
        for k in range(KD):
            if k >= 2:
                sp.wait_ge(self.lo_out, k - 1)
            sp.dma_start(self.stage[:, k % 2, :], self.dram[k * P:(k + 1) * P, :]).then_inc(self.loaded[k % 2], 16)

    def part_hi(self, act, k):
        act.wait_ge(self.loaded[k % 2], 16 * (k // 2 + 1))
        self.nc.scalar.activation(self.hi[:, k, :], self.stage[:, k % 2, :], ACT.Copy).then_inc(self.hi_out, 1)

    def part_lo(self, dve, k):
        dve.wait_ge(self.hi_out, k + 1)
        self.nc.vector.tensor_tensor(self.lo[:, k, :], self.stage[:, k % 2, :], self.hi[:, k, :].bitcast(F32),
                                     ALU.subtract).then_inc(self.lo_out, 1)


def row_broadcast(dram_row, width):
    return dram_row.rearrange("(a n) -> a n", a=1).to_broadcast([P, width])


def edge_phase(nc, a, t, cst, X, ps, keep, st):
    with Phase(nc) as ctx:
        def sb(name, shape, dt=F32):
            return ctx.enter_context(nc.sbuf_tensor("e_" + name, shape, dt))

        def sem(name):
            return ctx.sem("e_" + name)

        ident, tri, ones_w = cst["ident"], cst["tri"], cst["weigh"]
        ln = LayerNormRelu(ctx, nc, "n0", ps)
        st.begin(ctx, "s0")
        wd = Weights(ctx, nc, "wd", a["L0_gnn_W_down"], HID)
        rms = sb("rms", [P, KD])
        wlr = sb("wlr", [P, HK, 2 * HID])
        wlr_hi, wlr_lo = sb("wlr_hi", [P, HK, 2 * HID], F32R), sb("wlr_lo", [P, HK, 2 * HID], F32R)
        att, att2 = sb("att", [P, HID]), sb("att2", [P, HID])
        zero = sb("zero", [P, ZW])
        sumsq, meansq, rroot, rrms = sb("sumsq", [P, NT]), sb("meansq", [P, NT]), sb("rroot", [P, NT]), sb("rrms", [P, NT])
        sq = sb("sq", [P, D])
        xd = sb("xd", [P, 2, HID])
        xd_hi, xd_lo = sb("xd_hi", [P, 2, HK, P], F32R), sb("xd_lo", [P, 2, HK, P], F32R)
        xlr = sb("xlr", [P, 2, 2 * HL])
        sg, sv, sw = sb("sg", [P, HID]), sb("sv", [P, HID]), sb("sw", [P, 2, HID])
        self_pay = sb("self_pay", [P, NT, PAY])
        node_i, node_f, self_idx = sb("node_i", [P, NT], I32), sb("node_f", [P, NT]), sb("self_idx", [P, NT], I32)
        src, dst, typ = sb("src", [P, EC + U * G], I32), sb("dst", [P, EC + U * G], I32), sb("typ", [P, EC], I32)
        slot_i, slot = sb("slot_i", [P, G], I32), sb("slot", [P, G])
        live = sb("live", [P, 1])
        key = [sb(f"key{q}", [P, EC + G]) for q in range(2)]
        kcol = [sb(f"kcol{q}", [P, G]) for q in range(2)]
        rel = [sb(f"rel{q}", [P, EC]) for q in range(2)]
        spill = [sb(f"spill{q}", [P, G]) for q in range(2)]
        krow = [sb(f"krow{q}", [P, CE]) for q in range(2)]
        eq = [sb(f"eq{q}", [P, G, CE], F16) for q in range(2)]
        eqd = [sb(f"eqd{q}", [P, G, P], F16) for q in range(2)]
        mult = [sb(f"mult{q}", [P, G]) for q in range(2)]
        lead = [sb(f"lead{q}", [P, G]) for q in range(2)]
        row_f = [sb(f"row_f{q}", [P, G]) for q in range(2)]
        pair_idx = [sb(f"pair_idx{u}", [P, G], I32) for u in range(2)]
        idx_s = [sb(f"idx_s{u}", [P, G], I32) for u in range(U)]
        idx_d = [sb(f"idx_d{u}", [P, G], I32) for u in range(U)]
        gl = [sb(f"gl{u}", [P, G, HL]) for u in range(U)]
        gr = [sb(f"gr{u}", [P, G, HL]) for u in range(U)]
        gv = [sb(f"gv{u}", [P, G, HID]) for u in range(2)]
        gw = sb("gw", [P, G, HID])
        logit = sb("logit", [P, G, H])
        pay = [sb(f"pay{u}", [P, G, PAY]) for u in range(2)]

        s_x = [sem(f"x_in{i}") for i in range(NT)]
        s_w, s_edges, s_rms = sem("w_in"), sem("edges_in"), sem("rms_in")
        s_xtail = sem("x_tail_zero")
        s_zero = sem("zero_ready")
        s_cleared = [[sem("pairs_cleared0"), sem("pairs_cleared1")], [sem("typed_cleared")]]
        s_rms_done = sem("wd_scaled")
        s_ss, s_ms, s_rr, s_rrms = sem("sumsq"), sem("meansq"), sem("rroot"), sem("rrms")
        s_xd, s_xdT, s_xdhi, s_xdlo, s_xlmm, s_xl = (sem(n) for n in (
            "xd_ready", "xd_turned", "xd_hi", "xd_lo", "lr_done", "xlr_ready"))
        s_wl_hi, s_wl_lo = sem("wlr_hi_out"), sem("wlr_lo_out")
        s_tab, s_xa = [sem("tab0"), sem("tab1")], sem("xl_kept")
        s_chain, s_self, s_iota, s_selfidx = sem("v_chain"), sem("self_pay_ready"), sem("iota"), sem("self_idx_ready")
        s_keys = sem("keys_ready")
        s_lin, s_sum, s_relu = sem("linear_parts"), sem("edge_sums"), sem("edge_relu")
        s_krow, s_krow_out, s_eq, s_mult = sem("krow_turned"), sem("krow_out"), sem("eq_ready"), sem("mult_done")
        s_idx, s_pay = sem("idx_ready"), sem("pay_ready")
        s_gl, s_gr = [sem(f"gl{u}") for u in range(U)], [sem(f"gr{u}") for u in range(U)]
        s_put, s_self_put = sem("pairs_put"), sem("self_loops_put")
        s_free, s_landed, s_begun = sem("gathered_read"), sem("puts_landed"), sem("gather_begun")

        xl_dram, xr_dram, pairs, typed = t["xl"], t["xr"], t["pairs"], t["typed"]
        keep_xl, mult8, idx8 = keep["xl"], keep["mult8"], keep["idx8"]
        n_zero = [(pairs, NP * NP * PAY), (typed, R * NP * NP)]

        pieces = [size // (P * ZW) for _, size in n_zero]

        def clear(eng, q, c):
            tab, size = n_zero[q]
            w = tab.shape[1]
            done = s_cleared[q][c % len(s_cleared[q])]
            if c < pieces[q]:
                flat = tab[0:size // w, :].rearrange("a b -> (a b)").rearrange("(c p n) -> c p n", p=P, n=ZW)
                eng.dma_start(flat[c], zero[:, :]).then_inc(done, 16)
            else:
                eng.dma_start(tab[size // w:size // w + CE, :].rearrange("(p n) w -> p (n w)", p=P),
                              zero[:, 0:CE * w // P]).then_inc(done, 16)

        block = ctx.enter_context(nc.Block())

        @block.sync
        def _(sp):
            for b in range(NT):
                rows = P if b < NT - 1 else TAIL
                if b == NT - 1:
                    sp.wait_ge(s_xtail, 1)
                sp.dma_start(X[0:rows, b, :], a["x"][b * P:b * P + rows, :]).then_inc(s_x[b], 16)
            with nc.allow_non_contiguous_dma(reason="1024 scales, one per partition and tile"):
                sp.dma_start(rms[:, :], a["L0_gnn_rms_w"].rearrange("(k p) -> p k", p=P)).then_inc(s_rms, 16)
            for j, w in enumerate(("L0_gnn_Wl", "L0_gnn_Wr")):
                sp.dma_start(wlr[:, :, j * HID:(j + 1) * HID], a[w].rearrange("(k p) n -> p k n", p=P)).then_inc(s_w, 16)
            sp.dma_start(att[:, :], row_broadcast(a["L0_gnn_att"].rearrange("h d -> (h d)"), HID)).then_inc(s_w, 16)
            wd.load(sp)
            sp.wait_ge(s_zero, 1)
            for c in range(pieces[0] + 1):
                if c >= 2:
                    sp.wait_ge(s_cleared[0][c % 2], 16 * (c // 2))
                clear(sp, 0, c)
                b = c - 8
                if 0 <= b < NT:
                    sp.wait_ge(s_lin, b + 1)
                    sp.dma_start(xl_dram[b * P:(b + 1) * P, :], xlr[:, b % 2, 0:HL]).then_inc(s_tab[b % 2], 16)
                    sp.dma_start(xr_dram[b * P:(b + 1) * P, :], xlr[:, b % 2, HL:2 * HL]).then_inc(s_tab[b % 2], 16)
            for u in range(2):
                sp.wait_ge(s_cleared[0][u], 16 * ((pieces[0] + 2 - u) // 2))
            sp.wait_ge(s_self, NT)
            with nc.allow_non_contiguous_dma(reason="one row of the table per node"):
                for b in range(NT):
                    rows = pairs[b * P * (NP + 1):(b * P + P - 1) * (NP + 1) + 1:NP + 1, :]
                    sp.dma_start(rows, self_pay[:, b, :]).then_inc(s_self_put, 16)
            for c in range(pieces[1] + 1):
                sp.wait_ge(s_pay, c + 1)
                clear(sp, 1, c)

        @block.gpsimd
        def _(pool):
            nc.gpsimd.iota(node_i[:, :], pattern=[[P, NT]], base=0, channel_multiplier=1).then_inc(s_iota, 1)
            nc.gpsimd.iota(slot_i[:, :], pattern=[[P, G]], base=0, channel_multiplier=1).then_inc(s_iota, 1)
            pool.wait_ge(s_tab[0], 16 * NT)
            pool.wait_ge(s_tab[1], 16 * NT)

            def gather(i, u):
                n = U * i + u
                pool.wait_ge(s_idx, n + 1)
                pool.wait_ge(s_free, n + 1)
                nc.gpsimd.sem_inc(s_begun, 1)
                for j in range(G):
                    pool.indirect_dma_start(out=gl[u % U][:, j, :], out_offset=None, in_=xl_dram[:, :],
                                            in_offset=bass.IndirectOffsetOnAxis(ap=idx_s[u % U][:, j:j + 1], axis=0)).then_inc(s_gl[u % U], 16)
                    pool.indirect_dma_start(out=gr[u % U][:, j, :], out_offset=None, in_=xr_dram[:, :],
                                            in_offset=bass.IndirectOffsetOnAxis(ap=idx_d[u % U][:, j:j + 1], axis=0)).then_inc(s_gr[u % U], 16)

            def put(i, u, first=False):
                n = U * i + u
                pool.wait_ge(s_pay, n + 1)
                if not first:
                    pool.wait_ge(s_put, n * 16 * G)
                nc.gpsimd.sem_inc(s_landed, 1)
                for j in range(G):
                    pool.indirect_dma_start(out=pairs[:, :], out_offset=bass.IndirectOffsetOnAxis(ap=pair_idx[u % 2][:, j:j + 1], axis=0),
                                            in_=pay[u % 2][:, j, :], in_offset=None, compute_op=ALU.add).then_inc(s_put, 16)

            for u in range(U - 1):
                gather(0, u)
            pool.wait_ge(s_self_put, 16 * NT)
            nc.gpsimd.sem_inc(s_landed, 1)
            gather(0, U - 1)
            put(0, 0, first=True)
            with pool.Fori(0, CH // U - 1) as i:
                for u in range(U):
                    gather(i, u + U)
                    put(i, u + 1)
            for u in range(1, U):
                put(CH // U - 1, u)
            pool.wait_ge(s_put, CH * G * 16)
            pool.wait_ge(s_cleared[1][0], 16 * (pieces[1] + 1))

        @block.scalar
        def _(act):
            for name, tile in (("src", src), ("dst", dst), ("edge_type_8", typ)):
                act.wait_ge(s_xtail, 2)
                act.dma_start(tile[0:EP, 0:EC], a[name].rearrange("(p c) -> p c", c=EC)).then_inc(s_edges, 16)
            act.wait_ge(s_rms, 16)
            for k in range(KD):
                act.wait_ge(s_rms_done, k + 1)
                nc.scalar.activation(wd.hi[:, k, :], wd.stage[:, k % 2, :], ACT.Copy).then_inc(wd.hi_out, 1)
            act.wait_ge(s_w, 48)
            nc.scalar.activation(wlr_hi[:, :, :], wlr[:, :, :], ACT.Copy).then_inc(s_wl_hi, 1)
            st.scalar(act)
            for b in range(NT + 3):
                if b < NT:
                    act_h(nc, act, ln, X, st, b)
                    act.wait_ge(ln.h_ready, b + 1)
                    nc.scalar.activation(sq[:, :], ln.h[:, b % 2, :], ACT.Square, accum_out=sumsq[:, b:b + 1]).then_inc(s_ss, 1)
                    ln.part_hi(act, b)
                    act.wait_ge(s_ms, b + 1)
                    nc.scalar.activation(rroot[:, b:b + 1], meansq[:, b:b + 1], ACT.Sqrt).then_inc(s_rr, 1)
                if 0 <= b - 2 < NT:
                    c = b - 2
                    act.wait_ge(ln.used, c + 1)
                    act.wait_ge(s_rrms, c + 1)
                    if c >= 2:
                        act.wait_ge(s_xdT, c - 1)
                    nc.scalar.activation(xd[:, c % 2, :], ps[(4, 7)[c % 2]][:, 0:HID], ACT.Copy, scale=rrms[:, c:c + 1]).then_inc(s_xd, 1)
                if 0 <= b - 3 < NT:
                    c = b - 3
                    act.wait_ge(s_xlmm, c + 1)
                    if c >= 2:
                        act.wait_ge(s_tab[c % 2], 32 * (c // 2))
                        act.wait_ge(s_self, c - 1)
                        act.wait_ge(s_xa, c - 1)
                    nc.scalar.activation(xlr[:, c % 2, :].rearrange("p (t n) -> p t n", t=2)[:, :, 0:HID],
                                         ps[6][:, :].rearrange("p (t n) -> p t n", t=2), ACT.Copy).then_inc(s_xl, 1)
                if 0 <= b - 2 < NT:
                    c = b - 2
                    act.wait_ge(s_xdT, c + 1)
                    if c >= 2:
                        act.wait_ge(s_xlmm, c - 1)
                    nc.scalar.activation(xd_hi[:, c % 2, :, :].rearrange("p k n -> p (k n)"), ps[5][:, 0:HID], ACT.Copy).then_inc(s_xdhi, 1)

            def keys_out(n, q):
                act.wait_ge(s_krow, n + 1)
                act.wait_ge(s_eq, n + 1)
                nc.scalar.activation(krow[q][:, :], ps[q][:, :], ACT.Copy).then_inc(s_krow_out, 1)

            nc.scalar.sem_inc(s_krow_out, 2)
            with act.Fori(0, CH // U) as i:
                for u in range(U):
                    n = U * i + u
                    keys_out(2 * n, 0)
                    keys_out(2 * n + 1, 1)
                    act.wait_ge(s_sum, n + 1)
                    nc.scalar.activation(gv[u % 2][:, :, :], gl[u][:, :, 0:HID], ACT.Relu, scale=0.8).then_inc(s_relu, 1)

        @block.vector
        def _(dve):
            chain = Count(s_chain)

            def link(ins):
                chain.up(ins)
                dve.wait_ge(s_chain, chain.n)

            link(nc.vector.memset(X[:, NT - 1, :], 0.0))
            nc.vector.sem_inc(s_xtail, 1)
            for tile in (src, dst, typ):
                last = nc.vector.memset(tile[:, :], 0)
            link(last)
            nc.vector.sem_inc(s_xtail, 1)
            nc.vector.memset(zero[:, :], 0.0).then_inc(s_zero, 1)
            for b in range(NT):
                dve.wait_ge(s_x[b], 16)
                st.tile(X, b, link)
            dve.wait_ge(s_w, 48)
            link(nc.vector.tensor_scalar(att[:, :], att[:, :], -1.0, None, ALU.mult))
            link(nc.vector.tensor_scalar(att2[:, :], att[:, :], 0.2, None, ALU.mult))
            dve.wait_ge(s_rms, 16)
            for k in range(KD):
                dve.wait_ge(wd.loaded[k % 2], 16 * (k // 2 + 1))
                nc.vector.tensor_scalar(wd.stage[:, k % 2, :], wd.stage[:, k % 2, :], rms[:, k:k + 1], None, ALU.mult).then_inc(s_rms_done, 1)
                wd.part_lo(dve, k)
            dve.wait_ge(s_wl_hi, 1)
            nc.vector.tensor_tensor(wlr_lo[:, :, :], wlr[:, :, :], wlr_hi[:, :, :].bitcast(F32), ALU.subtract).then_inc(s_wl_lo, 1)
            st.vector(dve)
            dve.wait_ge(s_iota, 2)
            link(nc.vector.tensor_copy(node_f[:, :], node_i[:, :]))
            link(nc.vector.tensor_scalar(node_f[:, :], node_f[:, :], float(NP + 1), None, ALU.mult))
            nc.vector.tensor_copy(self_idx[:, :], node_f[:, :]).then_inc(s_selfidx, 1)
            link(nc.vector.tensor_copy(slot[:, :], slot_i[:, :]))
            link(nc.vector.tensor_scalar(live[:, :], slot[:, 0:1], float(EP), None, ALU.is_lt))
            link(nc.vector.tensor_scalar(spill[0][:, :], slot[:, :], float(NP * NP), None, ALU.add))
            link(nc.vector.tensor_scalar(spill[1][:, :], slot[:, :], float(R * NP * NP), None, ALU.add))
            dve.wait_ge(s_edges, 48)
            link(nc.vector.scalar_tensor_tensor(out=key[0][:, 0:EC], in0=dst[:, 0:EC], scalar=float(NP), in1=src[:, 0:EC], op0=ALU.mult, op1=ALU.add))
            link(nc.vector.scalar_tensor_tensor(out=key[1][:, 0:EC], in0=typ[:, :], scalar=float(NP), in1=src[:, 0:EC], op0=ALU.mult, op1=ALU.add))
            link(nc.vector.scalar_tensor_tensor(out=key[1][:, 0:EC], in0=key[1][:, 0:EC], scalar=float(NP), in1=dst[:, 0:EC], op0=ALU.mult, op1=ALU.add))
            for q in range(2):
                link(nc.vector.memset(key[q][:, EC:EC + G], 0.0))
                sp_all = spill[q][:, :].unsqueeze(1).to_broadcast([P, CH, G])
                k3, r3 = (v[q][:, 0:EC].rearrange("p (c g) -> p c g", g=G) for v in (key, rel))
                link(nc.vector.tensor_tensor(r3, k3, sp_all, ALU.subtract))
                link(nc.vector.tensor_scalar(rel[q][:, :], rel[q][:, :], live[:, 0:1], None, ALU.mult))
                link(nc.vector.tensor_tensor(k3, r3, sp_all, ALU.add))
                link(nc.vector.tensor_copy(kcol[q][:, :], key[q][:, 0:G]))
            nc.vector.sem_inc(s_keys, 1)

            def self_loops(c):
                dve.wait_ge(s_xl, c + 1)
                both = xlr[:, c % 2, :].rearrange("p (t n) -> p t n", t=2)
                xl_, xr_ = xlr[:, c % 2, 0:HID], xlr[:, c % 2, HL:HL + HID]
                if c >= 1:
                    dve.wait_ge(s_self, c)
                link(nc.vector.tensor_tensor(sw[:, :, :], both[:, :, 0:HID], att2[:, :].unsqueeze(1).to_broadcast([P, 2, HID]), ALU.mult))
                nc.vector.tensor_reduce(both[:, :, HID:HL], sw[:, :, :].rearrange("p t (h d) -> p t h d", d=DH), axis=AX.X, op=ALU.add).then_inc(s_lin, 1)
                nc.vector.tensor_copy(keep_xl[:, c, :, 0:DH], xl_.rearrange("p (h d) -> p h d", d=DH)).then_inc(s_xa, 1)
                link(nc.vector.tensor_tensor(sg[:, :], xl_, xr_, ALU.add))
                link(nc.vector.scalar_tensor_tensor(out=sv[:, :], in0=sg[:, :], scalar=0.2, in1=sg[:, :], op0=ALU.mult, op1=ALU.max))
                dve.wait_ge(s_lin, c + 1)
                link(nc.vector.tensor_tensor(sw[:, 0, :], sv[:, :], att[:, :], ALU.mult))
                nc.vector.tensor_reduce(self_pay[:, c, 1:PAY], sw[:, 0, :].rearrange("p (h d) -> p h d", d=DH), axis=AX.X, op=ALU.add).then_inc(s_self, 1)

            link(nc.vector.memset(keep_xl[:, :, :, DH:DH + 2], 1.0))
            link(nc.vector.memset(self_pay[:, :, 0:1], 1.0))
            for b in range(NT + 3):
                if b < NT:
                    ln.part_lo(dve, b)
                    dve.wait_ge(s_ss, b + 1)
                    nc.vector.tensor_scalar(meansq[:, b:b + 1], sumsq[:, b:b + 1], 1.0 / D, 1e-6, ALU.mult, ALU.add).then_inc(s_ms, 1)
                    dve.wait_ge(s_rr, b + 1)
                    nc.vector.reciprocal(rrms[:, b:b + 1], rroot[:, b:b + 1]).then_inc(s_rrms, 1)
                if 0 <= b - 2 < NT:
                    c = b - 2
                    dve.wait_ge(s_xdhi, c + 1)
                    nc.vector.tensor_tensor(xd_lo[:, c % 2, :, :].rearrange("p k n -> p (k n)"), ps[5][:, 0:HID],
                                            xd_hi[:, c % 2, :, :].rearrange("p k n -> p (k n)").bitcast(F32), ALU.subtract).then_inc(s_xdlo, 1)
                if 0 <= b - 3 < NT:
                    self_loops(b - 3)

            for u in range(U - 1):
                nc.vector.tensor_copy(idx_s[u][:, :], src[:, u * G:(u + 1) * G])
                link(nc.vector.tensor_copy(idx_d[u][:, :], dst[:, u * G:(u + 1) * G]))
                nc.vector.sem_inc(s_idx, 1)
            before = chain.n
            nc.vector.sem_inc(s_eq, 2)
            nc.vector.sem_inc(s_free, U)

            def chunk(i, u, at):
                steps = [0]

                def step(ins):
                    ins.then_inc(s_chain, 1)
                    steps[0] += 1
                    dve.wait_ge(s_chain, at + steps[0])

                n = U * i + u
                cols = bass.ds(n * G, G)
                after = bass.ds(n * G + G, G)
                ahead = bass.ds(n * G + (U - 1) * G, G)
                nc.vector.tensor_copy(idx_s[(u + U - 1) % U][:, :], src[:, ahead])
                step(nc.vector.tensor_copy(idx_d[(u + U - 1) % U][:, :], dst[:, ahead]))
                nc.vector.sem_inc(s_idx, 1)
                dve.wait_ge(s_gl[u], (i + 1) * 16 * G)
                dve.wait_ge(s_gr[u], (i + 1) * 16 * G)
                nc.vector.tensor_tensor(gl[u][:, :, :], gl[u][:, :, :], gr[u][:, :, :], ALU.add).then_inc(s_sum, 1)
                for q in range(2):
                    dve.wait_ge(s_krow_out, 2 * n + q + 3)
                    dve.wait_ge(s_mult, 2 * n + q + 1)
                    for g in range(G):
                        ins = nc.vector.tensor_scalar(eq[q][:, g, :], krow[q][:, :], key[q][:, bass.ds(n * G + g, 1)], None, ALU.is_equal)
                    step(ins)
                    diagonal = eq[q][:, :, :].rearrange("p g (c e) -> p (g c) e", e=P)[:, 0:G * G:G + 1, :]
                    nc.vector.tensor_tensor(eqd[q][:, :, :], diagonal, tri[:, :].unsqueeze(1).to_broadcast([P, G, P]), ALU.mult).then_inc(s_eq, 1)
                nc.vector.tensor_copy(kcol[0][:, :], key[0][:, after])
                step(nc.vector.tensor_copy(kcol[1][:, :], key[1][:, after]))
                nc.vector.sem_inc(s_keys, 1)
                dve.wait_ge(s_landed, n + 1)

                def rows(q):
                    dve.wait_ge(s_mult, 2 * n + q + 3)
                    m = mult[q][:, :] if q == 0 else mult8[:, cols]
                    step(nc.vector.tensor_copy(m, ps[2 + q][:, 0:G]))
                    step(nc.vector.tensor_scalar(lead[q][:, :], m, LATER, None, ALU.is_lt))
                    step(nc.vector.tensor_tensor(row_f[q][:, :], lead[q][:, :], rel[q][:, cols], ALU.mult))
                    step(nc.vector.tensor_tensor(pair_idx[u % 2][:, :] if q == 0 else idx8[:, cols], row_f[q][:, :], spill[q][:, :], ALU.add))

                rows(0)
                dve.wait_ge(s_relu, n + 1)
                step(nc.vector.tensor_tensor(gw[:, :, :], gv[u % 2][:, :, :], att[:, :].unsqueeze(1).to_broadcast([P, G, HID]), ALU.mult))
                step(nc.vector.tensor_reduce(logit[:, :, :].rearrange("p g h -> p (g h)"), gw[:, :, :].rearrange("p g (h d) -> p (g h) d", d=DH), axis=AX.X, op=ALU.add))
                step(nc.vector.tensor_tensor(logit[:, :, :], logit[:, :, :], gl[u][:, :, HID:HL], ALU.add))
                nc.vector.sem_inc(s_free, 1)
                rows(1)
                step(nc.vector.tensor_tensor(pay[u % 2][:, :, 1:PAY], logit[:, :, :], mult[0][:, :].unsqueeze(2).to_broadcast([P, G, H]), ALU.mult))
                step(nc.vector.tensor_copy(pay[u % 2][:, :, 0:1], mult[0][:, :].unsqueeze(2)))
                nc.vector.sem_inc(s_pay, 1)
                return steps[0]

            per = 17
            with dve.Fori(0, CH // U) as i:
                for u in range(U):
                    got = chunk(i, u, i * (U * per) + (before + u * per))
                    assert got == per, got

        @block.tensor
        def _(pe):
            pe.wait_ge(wd.lo_out, KD)
            pe.wait_ge(s_wl_lo, 1)
            for b in range(NT + 3):
                if b < NT:
                    ln.turn(pe, ident[:, :], b)
                if 0 <= b - 1 < NT:
                    c = b - 1
                    if c >= 2:
                        pe.wait_ge(s_xd, c - 1)
                    ln.product(pe, c, wd.hi, wd.lo, [ps[(4, 7)[c % 2]][:, 0:HID]], HID)
                if 0 <= b - 2 < NT:
                    c = b - 2
                    pe.wait_ge(s_xd, c + 1)
                    if c >= 1:
                        pe.wait_ge(s_xdlo, c)
                    for k in range(HK):
                        last = nc.tensor.transpose(ps[5][:, k * P:(k + 1) * P], xd[:, c % 2, k * P:(k + 1) * P], ident[:, :])
                    last.then_inc(s_xdT, 1)
                if 0 <= b - 3 < NT:
                    c = b - 3
                    pe.wait_ge(s_xdlo, c + 1)
                    if c >= 1:
                        pe.wait_ge(s_xl, c)
                    for k in range(HK):
                        for x_, w_, first, end in ((xd_hi, wlr_hi, k == 0, False), (xd_hi, wlr_lo, False, False), (xd_lo, wlr_hi, False, k == HK - 1)):
                            last = nc.tensor.matmul(ps[6][:, :], x_[:, c % 2, k, :], w_[:, k, :], start=first, stop=end)
                    last.then_inc(s_xlmm, 1)
            pe.wait_ge(ln.lo_ready, 2 * NT)
            nc.tensor.sem_inc(s_mult, 2)
            with pe.Fori(0, CH) as i:
                pe.wait_ge(s_keys, i + 1)
                for q in range(2):
                    pe.wait_ge(s_krow_out, 2 * i + 2)
                    for g in range(G):
                        last = nc.tensor.transpose(ps[q][:, g * P:(g + 1) * P],
                                                   kcol[q][:, g:g + 1].to_broadcast([P, P]), ident[:, :])
                    last.then_inc(s_krow, 1)
                for q in range(2):
                    pe.wait_ge(s_eq, 2 * i + q + 3)
                    for j in range(G):
                        for g in range(G):
                            nc.tensor.matmul(ps[2 + q][:, j:j + 1], eq[q][:, g, j * P:(j + 1) * P],
                                             ones_w[:, (1 if g < j else 0):(2 if g < j else 1)], start=(g == 0), stop=False)
                        last = nc.tensor.matmul(ps[2 + q][:, j:j + 1], eqd[q][:, j, :], ones_w[:, 2:3], start=False, stop=True)
                    last.then_inc(s_mult, 1)




def pair_phase(nc, a, t, cst, X, ps, keep, st):
    with Phase(nc) as ctx:
        def sb(name, shape, dt=F32):
            return ctx.enter_context(nc.sbuf_tensor("p_" + name, shape, dt))

        def sem(name):
            return ctx.sem("p_" + name)

        ident = cst["ident"]
        row = [sb(f"row{u}", [P, NP, PAY]) for u in range(2)]
        cnt = [sb(f"cnt{u}", [P, NP]) for u in range(2)]
        off = [sb(f"off{u}", [P, NP]) for u in range(2)]
        least, ninv = sb("least", [P, NP]), [sb(f"ninv{u}", [P, NP]) for u in range(2)]
        LG = 3
        lg, pc = sb("lg", [P, LG, NP]), sb("pc", [P, 2, NP])
        top, neg = sb("top", [P, NT, H]), sb("neg", [P, NT, H])
        pT = sb("pT", [P, 2, NT, P])
        den, iden = sb("den", [P, H]), sb("iden", [P, H])
        agg = sb("agg", [P, HID])
        agg_hi, agg_lo = sb("agg_hi", [P, HK, P], F32R), sb("agg_lo", [P, HK, P], F32R)
        wu, wu_hi, wu_lo = sb("wu", [P, HK, D]), sb("wu_hi", [P, HK, D], F32R), sb("wu_lo", [P, HK, D], F32R)
        s_row = [sem("row_in0"), sem("row_in1")]
        s_w, s_whi, s_wlo = sem("wu_in"), sem("wu_hi_out"), sem("wu_lo_out")
        s_cnt, s_cntout = sem("cnt_ready"), [sem("cnt_out0"), sem("cnt_out1")]
        s_row_free = sem("row_read")
        s_chain, s_top, s_neg, s_exp, s_pc = sem("v_chain"), sem("top_ready"), sem("neg_ready"), sem("exp_ready"), sem("pc_ready")
        s_turn, s_pT, s_head = sem("p_turned"), sem("pT_ready"), sem("head_done")
        s_lnout = sem("ln_out")
        s_least, s_guess, s_inv, s_lg = sem("least_ready"), sem("guess_ready"), sem("ninv_ready"), sem("lg_ready")
        s_norm, s_aggT, s_ahi, s_alo, s_up, s_xadd = (sem(n) for n in (
            "agg_normed", "agg_turned", "agg_hi_out", "agg_lo_out", "up_done", "x_added"))
        rows_dram, counts, typed = t["pairs"], t["counts"], t["typed"]
        keep_xl, mult8, idx8 = keep["xl"], keep["mult8"], keep["idx8"]
        block = ctx.enter_context(nc.Block())
        CUTS = [(0, 4), (4, 4), (8, 2)]

        @block.sync
        def _(sp):
            sp.dma_start(wu[:, :, :], a["L0_gnn_W_up"].rearrange("(k p) n -> p k n", p=P)).then_inc(s_w, 16)
            for b in range(NT):
                if b >= 2:
                    sp.wait_ge(s_row_free, b - 1)
                sp.dma_start(row[b % 2][:, :, :], rows_dram[b * P * NP:(b + 1) * P * NP, :].rearrange("(p n) w -> p n w", p=P)).then_inc(s_row[b % 2], 16)
                if b >= 1:
                    sp.wait_ge(s_cnt, b)
                    sp.dma_start(counts[(b - 1) * P:b * P, :], cnt[(b - 1) % 2][:, :]).then_inc(s_cntout[(b - 1) % 2], 16)
            sp.wait_ge(s_cnt, NT)
            sp.dma_start(counts[(NT - 1) * P:NT * P, :], cnt[(NT - 1) % 2][:, :]).then_inc(s_cntout[(NT - 1) % 2], 16)
            for u in range(2):
                sp.wait_ge(s_cntout[u], 16 * (NT // 2))

        @block.gpsimd
        def _(pool):
            for n in range(NT * H):
                b, h = n // H, n % H
                pool.wait_ge(s_inv, b + 1)
                if n >= LG:
                    pool.wait_ge(s_pc, n - LG + 1)
                ins = nc.gpsimd.tensor_tensor(lg[:, n % LG, :].unsqueeze(2), row[b % 2][:, :, 1 + h:2 + h], ninv[b % 2][:, :].unsqueeze(2), ALU.mult)
                ins.then_inc(s_lg, 1)
                if h == H - 1:
                    pool.wait_ge(s_lg, n + 1)
                    nc.gpsimd.sem_inc(s_row_free, 1)

        @block.vector
        def _(dve):
            chain = Count(s_chain)

            def link(ins):
                chain.up(ins)
                dve.wait_ge(s_chain, chain.n)

            def up_add(b):
                dve.wait_ge(s_up, b + 1)
                for n in range(2):
                    last = nc.vector.tensor_tensor(X[:, b, n * HALF:(n + 1) * HALF], X[:, b, n * HALF:(n + 1) * HALF], ps[6 + n][:, :], ALU.add)
                last.then_inc(s_xadd, 1)
                dve.wait_ge(s_xadd, b + 1)
                st.tile(X, b, link)

            def finish(b):
                dve.wait_ge(s_head, H * (b + 1))
                sums = ps[4][:, 0:H * (DH + 2)].rearrange("p (h d) -> p h d", d=DH + 2)
                link(nc.vector.tensor_scalar_add(den[:, :].unsqueeze(2), sums[:, :, DH:DH + 1], 1e-16))
                link(nc.vector.reciprocal(iden[:, :], den[:, :]))
                nc.vector.tensor_tensor(agg[:, :].rearrange("p (h d) -> p h d", d=DH), sums[:, :, 0:DH],
                                        iden[:, :].unsqueeze(2).to_broadcast([P, H, DH]), ALU.mult).then_inc(s_norm, 1)
                dve.wait_ge(s_ahi, b + 1)
                nc.vector.tensor_tensor(agg_lo[:, :, :].rearrange("p k n -> p (k n)"), ps[5][:, 0:HID],
                                        agg_hi[:, :, :].rearrange("p k n -> p (k n)").bitcast(F32), ALU.subtract).then_inc(s_alo, 1)

            dve.wait_ge(s_whi, 1)
            nc.vector.tensor_tensor(wu_lo[:, :, :], wu[:, :, :], wu_hi[:, :, :].bitcast(F32), ALU.subtract).then_inc(s_wlo, 1)
            def least_one(b):
                u = b % 2
                dve.wait_ge(s_cnt, b + 1)
                nc.vector.tensor_scalar(off[u][:, :], cnt[u][:, :], 0.5, -FAR, ALU.is_lt, ALU.mult)
                link(nc.vector.tensor_scalar_max(least[:, :], cnt[u][:, :], 1.0))
                nc.vector.sem_inc(s_least, 1)

            def invert(b):
                u = b % 2
                dve.wait_ge(s_guess, b + 1)
                link(nc.vector.tensor_tensor(least[:, :], least[:, :], ninv[u][:, :], ALU.mult))
                nc.vector.scalar_tensor_tensor(out=ninv[u][:, :], in0=least[:, :], scalar=-2.0, in1=ninv[u][:, :],
                                               op0=ALU.add, op1=ALU.mult).then_inc(s_inv, 1)

            def mask(n):
                b, h = n // H, n % H
                dve.wait_ge(s_lg, n + 1)
                link(nc.vector.tensor_tensor_reduce(out=lg[:, n % LG, :], in0=lg[:, n % LG, :], in1=off[b % 2][:, :], scale=1.0, scalar=-2.0 * FAR,
                                                    op0=ALU.add, op1=ALU.max, accum_out=top[:, b, h:h + 1]))
                nc.vector.tensor_scalar(neg[:, b, h:h + 1], top[:, b, h:h + 1], -1.0, None, ALU.mult).then_inc(s_neg, 1)

            def weigh(n):
                dve.wait_ge(s_exp, n + 1)
                if n >= 2:
                    dve.wait_ge(s_turn, 3 * (n - 1))
                nc.vector.tensor_tensor(pc[:, n % 2, :], lg[:, n % LG, :], cnt[n // H % 2][:, :], ALU.mult).then_inc(s_pc, 1)

            least_one(0)
            invert(0)
            mask(0)
            for n in range(NT * H):
                if n % H == 0 and n // H + 1 < NT:
                    least_one(n // H + 1)
                if n % H == 1 and n // H + 1 < NT:
                    invert(n // H + 1)
                if n + 1 < NT * H:
                    mask(n + 1)
                weigh(n)
                if n % H == 1 and n > H:
                    finish(n // H - 1)
                if n % H == 3 and n > H:
                    up_add(n // H - 1)
            finish(NT - 1)
            up_add(NT - 1)
            dve.wait_ge(s_xadd, NT)

        @block.scalar
        def _(act):
            act.wait_ge(s_w, 16)
            nc.scalar.activation(wu_hi[:, :, :], wu[:, :, :], ACT.Copy).then_inc(s_whi, 1)

            def evac(n):
                for c, (k0, kn) in enumerate(CUTS):
                    act.wait_ge(s_turn, 3 * n + c + 1)
                    if n >= 2 and c == 0:
                        act.wait_ge(s_head, n - 1)
                    nc.scalar.activation(pT[:, n % 2, k0:k0 + kn, :].rearrange("p k n -> p (k n)"), ps[(3 * n + c) % 4][:, 0:kn * P], ACT.Copy).then_inc(s_pT, 1)

            def agg_hi_out(b):
                act.wait_ge(s_aggT, b + 1)
                if b >= 1:
                    act.wait_ge(s_up, b)
                nc.scalar.activation(agg_hi[:, :, :].rearrange("p k n -> p (k n)"), ps[5][:, 0:HID], ACT.Copy).then_inc(s_ahi, 1)

            def count(b):
                u = b % 2
                act.wait_ge(s_row[u], 16 * (b // 2 + 1))
                if b >= 2:
                    act.wait_ge(s_cntout[u], 16 * (b // 2))
                    act.wait_ge(s_pc, H * (b - 1))
                nc.scalar.activation(cnt[u][:, :].unsqueeze(2), row[u][:, :, 0:1], ACT.Copy).then_inc(s_cnt, 1)

            def guess(b):
                u = b % 2
                act.wait_ge(s_least, b + 1)
                if b >= 2:
                    act.wait_ge(s_lg, H * (b - 1))
                nc.scalar.activation(ninv[u][:, :], least[:, :], ACT.Ln).then_inc(s_lnout, 1)
                act.wait_ge(s_lnout, b + 1)
                nc.scalar.activation(ninv[u][:, :], ninv[u][:, :], ACT.Exp, scale=-1.0).then_inc(s_guess, 1)

            count(0)
            guess(0)
            for b in range(NT):
                if b + 1 < NT:
                    count(b + 1)
                for h in range(H):
                    n = b * H + h
                    act.wait_ge(s_neg, n + 1)
                    nc.scalar.activation(lg[:, n % LG, :], lg[:, n % LG, :], ACT.Exp, bias=neg[:, b, h:h + 1]).then_inc(s_exp, 1)
                    if h == 0 and b + 1 < NT:
                        guess(b + 1)
                    if n >= 1:
                        evac(n - 1)
                    if h == 1 and b >= 1:
                        agg_hi_out(b - 1)
            evac(NT * H - 1)
            agg_hi_out(NT - 1)

        @block.tensor
        def _(pe):
            def turn_up(b):
                pe.wait_ge(s_norm, b + 1)
                if b >= 1:
                    pe.wait_ge(s_alo, b)
                for k in range(HK):
                    last = nc.tensor.transpose(ps[5][:, k * P:(k + 1) * P], agg[:, k * P:(k + 1) * P], ident[:, :])
                last.then_inc(s_aggT, 1)
                pe.wait_ge(s_alo, b + 1)
                if b >= 1:
                    pe.wait_ge(s_xadd, b)
                for k in range(HK):
                    for x_, w_, first, end in ((agg_hi, wu_hi, k == 0, False), (agg_hi, wu_lo, False, False), (agg_lo, wu_hi, False, k == HK - 1)):
                        for n in range(2):
                            last = nc.tensor.matmul(ps[6 + n][:, :], x_[:, k, :], w_[:, k, n * HALF:(n + 1) * HALF], start=first, stop=end)
                last.then_inc(s_up, 1)

            def turn_p(n):
                pe.wait_ge(s_pc, n + 1)
                for c, (k0, kn) in enumerate(CUTS):
                    g = 3 * n + c
                    if g >= 4:
                        pe.wait_ge(s_pT, g - 3)
                    for k in range(kn):
                        last = nc.tensor.transpose(ps[g % 4][:, k * P:(k + 1) * P], pc[:, n % 2, (k0 + k) * P:(k0 + k + 1) * P], ident[:, :])
                    last.then_inc(s_turn, 1)

            def weigh(n):
                b, h = n // H, n % H
                pe.wait_ge(s_pT, 3 * n + 3)
                if h == 0 and b >= 1:
                    pe.wait_ge(s_norm, b)
                for k in range(NT):
                    last = nc.tensor.matmul(ps[4][:, h * (DH + 2):(h + 1) * (DH + 2)], pT[:, n % 2, k, :], keep_xl[:, k, h, :], start=(k == 0), stop=(k == NT - 1))
                last.then_inc(s_head, 1)

            pe.wait_ge(s_wlo, 1)
            for n in range(NT * H):
                turn_p(n)
                if n >= 1:
                    weigh(n - 1)
                    if n % H == 1 and n > H:
                        turn_up(n // H - 1)
            weigh(NT * H - 1)
            turn_up(NT - 1)


def product_phase(nc, a, t, cst, X, ps, st, tag, weight, finish, new_norm=True):
    with Phase(nc) as ctx:
        ln = LayerNormRelu(ctx, nc, tag, ps)
        if new_norm:
            st.begin(ctx, tag + "s")
        w = Weights(ctx, nc, tag + "w", weight)
        done = ctx.sem(tag + "_read")
        f = finish(ctx, ln, done)
        block = ctx.enter_context(nc.Block())

        @block.sync
        def _(sp):
            w.load(sp)
            f.sync(sp)

        @block.gpsimd
        def _(pool):
            f.gpsimd(pool)

        @block.scalar
        def _(act):
            if new_norm:
                st.scalar(act)
            for b in range(NT + 1):
                if b < NT:
                    f.before_h(act, b)
                    act_h(nc, act, ln, X, st, b)
                    if b == 0:
                        for k in range(KD):
                            w.part_hi(act, k)
                            if k == 1:
                                ln.part_hi(act, b)
                    else:
                        ln.part_hi(act, b)
                if b >= 1:
                    f.scalar(act, b - 1)

        @block.vector
        def _(dve):
            if new_norm:
                st.vector(dve)
            for b in range(NT + 1):
                if b == 0:
                    for k in range(KD):
                        w.part_lo(dve, k)
                        if k == 1:
                            ln.part_lo(dve, b)
                elif b < NT:
                    ln.part_lo(dve, b)
                if b >= 1:
                    f.vector(dve, b - 1)
            f.vector_end(dve)

        @block.tensor
        def _(pe):
            ln.turn(pe, cst["ident"][:, :], 0)
            for b in range(NT):
                if b + 1 < NT:
                    ln.turn(pe, cst["ident"][:, :], b + 1)
                if b >= 2:
                    pe.wait_ge(done, b - 1)
                ln.product(pe, b, w.hi, w.lo, [ps[4 + 2 * (b % 2)], ps[5 + 2 * (b % 2)]], w_ready=w.lo_out)


class Finish:

    def __init__(self, nc, ctx, ln, done, ps, X):
        self.nc, self.ln, self.done, self.ps, self.X = nc, ln, done, ps, X
        self.make(ctx)

    def make(self, ctx):
        pass

    def bank(self, b, n):
        return self.ps[4 + 2 * (b % 2) + n]

    def sync(self, sp):
        pass

    def gpsimd(self, pool):
        pass

    def before_h(self, act, b):
        pass

    def scalar(self, act, b):
        pass

    def vector(self, dve, b):
        pass

    def vector_end(self, dve):
        pass


def attention_phase(nc, a, t, cst, X, ps, st, h1, al, ar):
    a_row = a["L1_gnn_a"].rearrange("a n -> (a n)")

    class F(Finish):
        def make(self, ctx):
            def sem(name):
                return ctx.sem("a_" + name)
            self.vec = ctx.enter_context(nc.sbuf_tensor("a_vec", [P, 2 * D], F32))
            self.prod = ctx.enter_context(nc.sbuf_tensor("a_prod", [P, D], F32))
            self.vec_in, self.chain = sem("vec_in"), sem("v_chain")

        def sync(self, sp):
            sp.dma_start(self.vec[:, :], row_broadcast(a_row, 2 * D)).then_inc(self.vec_in, 16)

        def scalar(self, act, b):
            act.wait_ge(self.ln.used, b + 1)
            for n in range(2):
                last = nc.scalar.activation(h1[:, b, n * HALF:(n + 1) * HALF], self.bank(b, n)[:, :], ACT.Copy)
            last.then_inc(self.done, 1)

        def vector(self, dve, b):
            if b == 0:
                dve.wait_ge(self.vec_in, 16)
            dve.wait_ge(self.done, b + 1)
            for j, out in enumerate((al, ar)):
                if 2 * b + j > 0:
                    dve.wait_ge(self.chain, 2 * b + j)
                nc.vector.tensor_tensor_reduce(out=self.prod[:, :], in0=h1[:, b, :], in1=self.vec[:, j * D:(j + 1) * D], scale=1.0, scalar=0.0,
                                               op0=ALU.mult, op1=ALU.add, accum_out=out[:, b:b + 1]).then_inc(self.chain, 1)

        def vector_end(self, dve):
            dve.wait_ge(self.chain, 2 * NT)

    product_phase(nc, a, t, cst, X, ps, st, "a1", a["L1_gnn_W"], lambda ctx, ln, done: F(nc, ctx, ln, done, ps, X))


def neighbour_phase(nc, a, t, cst, X, ps, st, h1, al, ar, dinv, keep):
    with Phase(nc) as ctx:
        def sb(name, shape, dt=F32):
            return ctx.enter_context(nc.sbuf_tensor("q_" + name, shape, dt))

        def sem(name):
            return ctx.sem("q_" + name)

        ident, ones = cst["ident"], cst["ones"]
        p = sb("p", [P, NT, NP])
        al_row = sb("al_row", [P, NP])
        u1, u2, ex = sb("u1", [P, 2, NP]), sb("u2", [P, 2, NP]), sb("ex", [P, 2, NP])
        root = sb("root", [P, NT])
        rs = sb("rs", [P, NT])
        irs = sb("irs", [P, NT])
        neg, pos, en = sb("neg", [P, 2, D]), sb("pos", [P, 2, D]), sb("en", [P, 2, D])
        s_p = [sem(f"p_in{u}") for u in range(2)]
        s_deg, s_root, s_dinv = sem("deg_done"), sem("deg_root"), sem("dinv_ready")
        s_row, s_rowout = sem("al_turned"), sem("al_row_out")
        s_chain, s_u, s_ex, s_pr = sem("v_chain"), sem("u_ready"), sem("ex_ready"), sem("p_ready")
        s_agg, s_neg, s_en, s_x, s_out = sem("agg_done"), sem("neg_ready"), sem("exp_ready"), sem("x_ready"), sem("x_out")
        s_bank, s_typed = sem("banks_read"), sem("typed_put")
        block = ctx.enter_context(nc.Block())

        @block.sync
        def _(sp):
            for k in range(NT):
                sp.dma_start(p[:, k, :], t["counts"][k * P:(k + 1) * P, :]).then_inc(s_p[k // 5], 16)
            for b in range(NT):
                sp.wait_ge(s_x, b + 1)
                sp.dma_start(t["x2"][b * P:(b + 1) * P, :], X[:, b, :]).then_inc(s_out, 16)
            sp.wait_ge(s_out, 16 * NT)

        @block.gpsimd
        def _(pool):
            for c in range(CH):
                if c >= 1:
                    pool.wait_ge(s_typed, 16 * G * c)
                for j in range(G):
                    e = c * G + j
                    pool.indirect_dma_start(out=t["typed"][:, :], out_offset=bass.IndirectOffsetOnAxis(ap=keep["idx8"][:, e:e + 1], axis=0),
                                            in_=keep["mult8"][:, e:e + 1], in_offset=None, compute_op=ALU.add).then_inc(s_typed, 16)
            pool.wait_ge(s_typed, 16 * G * CH)

        @block.scalar
        def _(act):
            for c in range(3):
                n = min(4, NT - 4 * c)
                act.wait_ge(s_row, c + 1)
                nc.scalar.activation(al_row[:, 4 * c * P:(4 * c + n) * P], ps[c][:, 0:n * P], ACT.Copy).then_inc(s_rowout, 1)
            act.wait_ge(s_deg, 1)
            nc.scalar.activation(root[:, :], ps[3][:, 0:NT], ACT.Sqrt).then_inc(s_root, 1)
            for k in range(NT):
                act.wait_ge(s_u, k + 1)
                if k >= 2:
                    act.wait_ge(s_pr, k - 1)
                nc.scalar.activation(ex[:, k % 2, :], u2[:, k % 2, :], ACT.Exp, scale=-1.0).then_inc(s_ex, 1)
            for b in range(NT):
                act.wait_ge(s_neg, b + 1)
                if b >= 2:
                    act.wait_ge(s_x, b - 1)
                nc.scalar.activation(en[:, b % 2, :], neg[:, b % 2, :], ACT.Exp).then_inc(s_en, 1)

        @block.vector
        def _(dve):
            chain = Count(s_chain)

            def link(ins):
                chain.up(ins)
                dve.wait_ge(s_chain, chain.n)

            dve.wait_ge(s_root, 1)
            nc.vector.reciprocal(dinv[:, :], root[:, :]).then_inc(s_dinv, 1)
            dve.wait_ge(s_rowout, 3)
            for k in range(NT):
                link(nc.vector.tensor_tensor(p[:, k, k * P:(k + 1) * P], p[:, k, k * P:(k + 1) * P], ident[:, :], ALU.subtract))
                link(nc.vector.tensor_scalar(u1[:, k % 2, :], al_row[:, :], ar[:, k:k + 1], None, ALU.add))
                if k >= 2:
                    dve.wait_ge(s_ex, k - 1)
                nc.vector.scalar_tensor_tensor(out=u2[:, k % 2, :], in0=u1[:, k % 2, :], scalar=0.1, in1=u1[:, k % 2, :], op0=ALU.mult, op1=ALU.max).then_inc(s_u, 1)
                if k >= 1:
                    dve.wait_ge(s_ex, k)
                    nc.vector.tensor_tensor(p[:, k - 1, :], p[:, k - 1, :], ex[:, (k - 1) % 2, :], ALU.mult).then_inc(s_pr, 1)
            dve.wait_ge(s_ex, NT)
            nc.vector.tensor_tensor(p[:, NT - 1, :], p[:, NT - 1, :], ex[:, (NT - 1) % 2, :], ALU.mult).then_inc(s_pr, 1)

            def start(b):
                dve.wait_ge(s_agg, b + 1)
                link(nc.vector.tensor_scalar_add(rs[:, b:b + 1], ps[6 + b % 2][:, 0:1], 1e-5))
                link(nc.vector.reciprocal(irs[:, b:b + 1], rs[:, b:b + 1]))
                if b >= 2:
                    dve.wait_ge(s_en, b - 1)
                for n in range(2):
                    last = nc.vector.tensor_scalar(neg[:, b % 2, n * HALF:(n + 1) * HALF], ps[2 * (b % 2) + n][:, :], irs[:, b:b + 1], 0.0, ALU.mult, ALU.min)
                last.then_inc(s_neg, 1)
                for n in range(2):
                    last = nc.vector.tensor_scalar(pos[:, b % 2, n * HALF:(n + 1) * HALF], ps[2 * (b % 2) + n][:, :], irs[:, b:b + 1], 0.0, ALU.mult, ALU.max)
                last.then_inc(s_bank, 1)

            def end(b):
                dve.wait_ge(s_bank, b + 1)
                link(nc.vector.tensor_tensor(X[:, b, :], X[:, b, :], pos[:, b % 2, :], ALU.add))
                dve.wait_ge(s_en, b + 1)
                nc.vector.scalar_tensor_tensor(out=X[:, b, :], in0=en[:, b % 2, :], scalar=-1.0, in1=X[:, b, :], op0=ALU.add, op1=ALU.add).then_inc(s_x, 1)
                dve.wait_ge(s_x, b + 1)
                st.tile(X, b, link)

            for b in range(NT):
                start(b)
                if b >= 1:
                    end(b - 1)
            end(NT - 1)

        @block.tensor
        def _(pe):
            for c in range(3):
                for k in range(min(4, NT - 4 * c)):
                    last = nc.tensor.transpose(ps[c][:, k * P:(k + 1) * P], al[:, 4 * c + k:4 * c + k + 1].to_broadcast([P, P]), ident[:, :])
                last.then_inc(s_row, 1)
            for u in range(2):
                pe.wait_ge(s_p[u], 16 * 5)
            for b in range(NT):
                for k in range(NT):
                    last = nc.tensor.matmul(ps[3][:, b:b + 1], p[:, k, b * P:(b + 1) * P], ones[:, 0:1], start=(k == 0), stop=(k == NT - 1))
            last.then_inc(s_deg, 1)
            pe.wait_ge(s_root, 1)
            for b in range(NT):
                if b >= 2:
                    pe.wait_ge(s_bank, b - 1)
                for k in range(NT):
                    if b == 0:
                        pe.wait_ge(s_pr, k + 1)
                    first, end = k == 0, k == NT - 1
                    for n in range(2):
                        nc.tensor.matmul(ps[2 * (b % 2) + n][:, :], p[:, k, b * P:(b + 1) * P], h1[:, k, n * HALF:(n + 1) * HALF], start=first, stop=end)
                    last = nc.tensor.matmul(ps[6 + b % 2][:, 0:1], p[:, k, b * P:(b + 1) * P], ones[:, 0:1], start=first, stop=end)
                last.then_inc(s_agg, 1)


def gate_x_phase(nc, a, t, cst, X, ps, st, h16):
    class F(Finish):
        def make(self, ctx):
            def sem(name):
                return ctx.sem("g_" + name)
            self.bias = ctx.enter_context(nc.sbuf_tensor("g_bias", [P, D], F32))
            self.z = ctx.enter_context(nc.sbuf_tensor("g_z", [P, 2, D], F32))
            self.bias_in, self.h_out, self.z_out = sem("bias_in"), [sem("h_out0"), sem("h_out1")], [sem("z_out0"), sem("z_out1")]
            self.h_hi, self.h_lo = sem("h16_hi"), sem("h16_lo")

        def sync(self, sp):
            sp.dma_start(self.bias[:, :], row_broadcast(a["L2_gnn_b_gate"], D)).then_inc(self.bias_in, 16)
            for b in range(NT + 1):
                if b < NT:
                    sp.wait_ge(self.ln.h_ready, b + 1)
                    sp.dma_start(t["h2"][b * P:(b + 1) * P, :], self.ln.h[:, b % 2, :]).then_inc(self.h_out[b % 2], 16)
                if b >= 1:
                    sp.wait_ge(self.done, b)
                    sp.dma_start(t["zx"][(b - 1) * P:b * P, :], self.z[:, (b - 1) % 2, :]).then_inc(self.z_out[(b - 1) % 2], 16)
            for u in range(2):
                sp.wait_ge(self.z_out[u], 16 * (NT // 2))
                sp.wait_ge(self.h_out[u], 16 * (NT // 2))

        def gpsimd(self, pool):
            for b in range(NT):
                pool.wait_ge(self.ln.h_ready, b + 1)
                nc.gpsimd.tensor_copy(h16[:, 0, b, :], self.ln.h[:, b % 2, :]).then_inc(self.h_hi, 1)
                pool.wait_ge(self.h_hi, b + 1)
                nc.gpsimd.tensor_tensor(h16[:, 1, b, :], self.ln.h[:, b % 2, :], h16[:, 0, b, :], ALU.subtract).then_inc(self.h_lo, 1)

        def before_h(self, act, b):
            if b >= 2:
                act.wait_ge(self.h_lo, b - 1)
                act.wait_ge(self.h_out[b % 2], 16 * (b // 2))

        def vector(self, dve, b):
            if b == 0:
                dve.wait_ge(self.bias_in, 16)
            if b >= 2:
                dve.wait_ge(self.z_out[b % 2], 16 * (b // 2))
            dve.wait_ge(self.ln.used, b + 1)
            for n in range(2):
                last = nc.vector.tensor_tensor(self.z[:, b % 2, n * HALF:(n + 1) * HALF], self.bank(b, n)[:, :], self.bias[:, n * HALF:(n + 1) * HALF], ALU.add)
            last.then_inc(self.done, 1)

    product_phase(nc, a, t, cst, X, ps, st, "g2", a["L2_gnn_w_gate"][D:2 * D, :], lambda ctx, ln, done: F(nc, ctx, ln, done, ps, X))


def root_phase(nc, a, t, cst, X, ps, st):
    class F(Finish):
        def make(self, ctx):
            self.bias = ctx.enter_context(nc.sbuf_tensor("o_bias", [P, D], F32))
            self.bias_in = ctx.sem("o_bias_in")

        def sync(self, sp):
            sp.dma_start(self.bias[:, :], row_broadcast(a["L2_gnn_bias"], D)).then_inc(self.bias_in, 16)

        def vector(self, dve, b):
            if b == 0:
                dve.wait_ge(self.bias_in, 16)
            dve.wait_ge(self.ln.used, b + 1)
            for n in range(2):
                last = nc.vector.tensor_tensor(X[:, b, n * HALF:(n + 1) * HALF], self.bank(b, n)[:, :], self.bias[:, n * HALF:(n + 1) * HALF], ALU.add)
            last.then_inc(self.done, 1)

        def vector_end(self, dve):
            dve.wait_ge(self.done, NT)

    product_phase(nc, a, t, cst, X, ps, st, "o2", a["L2_gnn_root"], lambda ctx, ln, done: F(nc, ctx, ln, done, ps, X), new_norm=False)


def relation_phase(nc, a, t, cst, X, ps, h16):
    with Phase(nc) as ctx:
        def sb(name, shape, dt=F32):
            return ctx.enter_context(nc.sbuf_tensor("r_" + name, shape, dt))

        def sem(name):
            return ctx.sem("r_" + name)

        ones16 = cst["ones16"]
        NC = len(DCH)
        WMAX = max(w for _, w in DCH)
        c16 = [sb(f"c16_{u}", [P, NT, WMAX], F16) for u in range(2)]
        s_hi, s_lo = sb("s_hi", [P, KD, WMAX], F32R), sb("s_lo", [P, KD, WMAX], F32R)
        stage = sb("stage", [P, 2, D])
        w_hi, w_lo = sb("w_hi", [P, KD, D], F32R), sb("w_lo", [P, KD, D], F32R)
        cnt = [sb(f"cnt{u}", [P, 4]) for u in range(2)]
        AB = 3
        c_in = [sem("c_in0"), sem("c_in1")]
        w_in = [sem("w_in0"), sem("w_in1")]
        s_whi, s_wlo, s_wfree = sem("w_hi_out"), sem("w_lo_out"), sem("w_used")
        s_sum, s_shi, s_slo = sem("sums_done"), sem("s_hi_out"), sem("s_lo_out")
        s_cnt, s_inv, s_chain = sem("cnt_done"), sem("inv_ready"), sem("v_chain")
        s_mm, s_add = sem("product_done"), sem("u_added")
        s_cread, s_begun = sem("c_read"), sem("load_begun")
        TILES = sum(w // P for _, w in DCH)
        table = t["typed"][0:R * NP * NP, :].rearrange("(r k p n) w -> r p k (n w)", r=R, p=P, n=NP)
        weight = a["L2_gnn_weight"]
        block = ctx.enter_context(nc.Block())

        @block.gpsimd
        def _(pool):
            def load(r, c, n, u, wait=True):
                c0, cw = DCH[c]
                if wait:
                    pool.wait_ge(s_cread, n - 1)
                    nc.gpsimd.sem_inc(s_begun, 1)
                src = table[bass.ds(r, 1)] if not isinstance(r, int) else table[r:r + 1]
                pool.dma_start(c16[u][:, :, 0:cw], src.rearrange("r p k n -> (r p) k n")[:, :, c0:c0 + cw]).then_inc(c_in[u], 16)

            for j in range(2 * NC):
                load(j // NC, j % NC, j, j % 2, j >= 2)
            with pool.Fori(1, R // 2) as i:
                for j in range(2 * NC):
                    load(2 * i + j // NC, j % NC, 2 * NC * i + j, j % 2)

        @block.sync
        def _(sp):
            def load(r, k, wait=True):
                if wait:
                    sp.wait_ge(s_wlo, r * KD + (k - 1))
                w = weight[bass.ds(r, 1)] if not isinstance(r, int) else weight[r:r + 1]
                sp.dma_start(stage[:, k % 2, :], w.rearrange("r (k p) n -> k (r p) n", p=P)[k]).then_inc(w_in[k % 2], 16)

            for k in range(KD):
                load(0, k, k >= 2)
            with sp.Fori(1, R) as r:
                for k in range(KD):
                    load(r, k)

        @block.scalar
        def _(act):
            def body(r, first):
                for c in range(NC):
                    c0, cw = DCH[c]
                    for k in range(KD):
                        g = c * KD + k
                        act.wait_ge(s_sum, r * (NC * KD) + (g + 1))
                        if not (first and c == 0) and k == 0:
                            act.wait_ge(s_mm, r * TILES + TILES * 0 + before[c])
                        nc.scalar.activation(s_hi[:, k, 0:cw], ps[g % AB][:, 0:cw], ACT.Copy).then_inc(s_shi, 1)
                        if c == 0:
                            act.wait_ge(w_in[k % 2], r * 64 + 16 * (k // 2 + 1))
                            if not first:
                                act.wait_ge(s_wfree, r * KD)
                            nc.scalar.activation(w_hi[:, k, :], stage[:, k % 2, :], ACT.Copy).then_inc(s_whi, 1)

            before = [0, 4, 8]
            body(0, True)
            with act.Fori(1, R) as r:
                body(r, False)

        @block.vector
        def _(dve):
            def body(r, first):
                for c in range(NC):
                    c0, cw = DCH[c]
                    for k in range(KD):
                        g = c * KD + k
                        dve.wait_ge(s_shi, r * (NC * KD) + (g + 1))
                        nc.vector.tensor_tensor(s_lo[:, k, 0:cw], ps[g % AB][:, 0:cw], s_hi[:, k, 0:cw].bitcast(F32), ALU.subtract).then_inc(s_slo, 1)
                        if c == 0:
                            dve.wait_ge(s_whi, r * KD + (k + 1))
                            nc.vector.tensor_tensor(w_lo[:, k, :], stage[:, k % 2, :], w_hi[:, k, :].bitcast(F32), ALU.subtract).then_inc(s_wlo, 1)
                    m = cw // P
                    u = c % 2
                    dve.wait_ge(s_cnt, r * NC + (c + 1))
                    nc.vector.tensor_scalar_max(cnt[u][:, 0:m], ps[3][:, 4 * u:4 * u + m], 1.0).then_inc(s_chain, 1)
                    dve.wait_ge(s_chain, r * (2 * NC) + (2 * c + 1))
                    nc.vector.reciprocal(cnt[u][:, 0:m], cnt[u][:, 0:m]).then_inc(s_chain, 1)
                    dve.wait_ge(s_chain, r * (2 * NC) + (2 * c + 2))
                    nc.vector.sem_inc(s_inv, 1)
                    for i in range(m):
                        b = c0 // P + i
                        dve.wait_ge(s_mm, r * TILES + (b + 1))
                        for n in range(2):
                            last = nc.vector.scalar_tensor_tensor(out=X[:, b, n * HALF:(n + 1) * HALF], in0=ps[4 + 2 * (b % 2) + n][:, :],
                                                                  scalar=cnt[u][:, i:i + 1], in1=X[:, b, n * HALF:(n + 1) * HALF], op0=ALU.mult, op1=ALU.add)
                        last.then_inc(s_add, 1)

            body(0, True)
            with dve.Fori(1, R) as r:
                body(r, False)
            dve.wait_ge(s_add, R * TILES)

        @block.tensor
        def _(pe):
            def sums(r, c, par, first):
                c0, cw = DCH[c]
                u = (par * NC + c) % 2
                pe.wait_ge(c_in[u], half(r, par) + 16 * ((par * NC + c) // 2 + 1))
                for k in range(KD):
                    g = c * KD + k
                    if not (first and g < AB):
                        pe.wait_ge(s_slo, r * (NC * KD) + (g + 1 - AB))
                    for part in range(2):
                        for j in range(NT):
                            last = nc.tensor.matmul(ps[g % AB][:, 0:cw], h16[:, part, j, k * P:(k + 1) * P], c16[u][:, j, 0:cw],
                                                    start=(part == 0 and j == 0), stop=(part == 1 and j == NT - 1))
                    last.then_inc(s_sum, 1)
                if not (first and c < 1):
                    pe.wait_ge(s_inv, r * NC + c)
                for i in range(cw // P):
                    for j in range(NT):
                        last = nc.tensor.matmul(ps[3][:, 4 * (c % 2) + i:4 * (c % 2) + i + 1], c16[u][:, j, i * P:(i + 1) * P], ones16[:, 0:1], start=(j == 0), stop=(j == NT - 1))
                last.then_inc(s_cnt, 1)
                pe.wait_ge(s_cnt, r * NC + (c + 1))
                nc.tensor.sem_inc(s_cread, 1)

            def products(r, c, first):
                c0, cw = DCH[c]
                for i in range(cw // P):
                    b = c0 // P + i
                    if not (first and b < 2):
                        pe.wait_ge(s_add, r * TILES + (b - 1))
                    for k in range(KD):
                        if i == 0:
                            pe.wait_ge(s_slo, r * (NC * KD) + (c * KD + k + 1))
                            if c == 0:
                                pe.wait_ge(s_wlo, r * KD + (k + 1))
                        for x_, w_, f, e in ((s_hi, w_hi, k == 0, False), (s_hi, w_lo, False, False), (s_lo, w_hi, False, k == KD - 1)):
                            for n in range(2):
                                last = nc.tensor.matmul(ps[4 + 2 * (b % 2) + n][:, :], x_[:, k, i * P:(i + 1) * P], w_[:, k, n * HALF:(n + 1) * HALF], start=f, stop=e)
                    last.then_inc(s_mm, 1)
                    if b == NT - 1:
                        pe.wait_ge(s_mm, r * TILES + TILES)
                        nc.tensor.sem_inc(s_wfree, KD)

            def half(r, par):
                return (r - par) * (8 * NC)

            def body(r, par, first):
                for c in range(NC):
                    sums(r, c, par, first)
                    products(r, c, first)

            body(0, 0, True)
            body(1, 1, False)
            with pe.Fori(1, R // 2) as i:
                body(2 * i, 0, False)
                body(2 * i + 1, 1, False)


def gate_phase(nc, a, t, cst, X, ps, st):
    with Phase(nc) as ctx:
        def sb(name, shape, dt=F32):
            return ctx.enter_context(nc.sbuf_tensor("z_" + name, shape, dt))

        def sem(name):
            return ctx.sem("z_" + name)

        w = Weights(ctx, nc, "zw", a["L2_gnn_w_gate"][0:D, :])
        hi, lo = sb("hi", [P, 2, KD, P], F32R), sb("lo", [P, 2, KD, P], F32R)
        th = sb("th", [P, 2, D])
        ins = {n: sb(n, [P, 2, D]) for n in ("zx", "h2", "x2")}
        arrived = [sem("in0"), sem("in1")]
        s_turn, s_hi, s_lo, s_mm, s_th, s_z, s_x, s_out = (sem(n) for n in (
            "turned", "hi_out", "lo_out", "product_done", "tanh_ready", "z_ready", "x_ready", "x_out"))
        s_chain = sem("v_chain")
        block = ctx.enter_context(nc.Block())

        @block.sync
        def _(sp):
            w.load(sp)
            for b in range(NT):
                if b >= 2:
                    sp.wait_ge(s_x, b - 1)
                for n in ins:
                    sp.dma_start(ins[n][:, b % 2, :], t[n][b * P:(b + 1) * P, :]).then_inc(arrived[b % 2], 16)
            for b in range(NT):
                sp.wait_ge(s_x, b + 1)
                sp.dma_start(t["x3"][b * P:(b + 1) * P, :], X[:, b, :]).then_inc(s_out, 16)
            sp.wait_ge(s_out, 16 * NT)

        @block.scalar
        def _(act):
            for b in range(NT):
                if b == 1:
                    for k in range(2, KD):
                        w.part_hi(act, k)
                for n in range(2):
                    if b == 0:
                        w.part_hi(act, n)
                    act.wait_ge(s_turn, 2 * b + n + 1)
                    if b >= 2 and n == 0:
                        act.wait_ge(s_mm, b - 1)
                    nc.scalar.activation(hi[:, b % 2, 4 * n:4 * n + 4, :].rearrange("p k n -> p (k n)"), ps[2 * (b % 2) + n][:, :], ACT.Copy).then_inc(s_hi, 1)
                if b >= 2:
                    act.wait_ge(s_x, b - 1)
                nc.scalar.activation(th[:, b % 2, :], X[:, b, :], ACT.Tanh).then_inc(s_th, 1)

        @block.vector
        def _(dve):
            chain = Count(s_chain)

            def link(ins_):
                chain.up(ins_)
                dve.wait_ge(s_chain, chain.n)

            def lows(b):
                for n in range(2):
                    dve.wait_ge(s_hi, 2 * b + n + 1)
                    nc.vector.tensor_tensor(lo[:, b % 2, 4 * n:4 * n + 4, :].rearrange("p k n -> p (k n)"), ps[2 * (b % 2) + n][:, :],
                                            hi[:, b % 2, 4 * n:4 * n + 4, :].rearrange("p k n -> p (k n)").bitcast(F32), ALU.subtract).then_inc(s_lo, 1)

            for b in range(NT + 1):
                if b == 0:
                    w.part_lo(dve, 0)
                    w.part_lo(dve, 1)
                if b < NT:
                    lows(b)
                if b == 0:
                    for k in range(2, KD):
                        w.part_lo(dve, k)
                if b >= 1:
                    c = b - 1
                    u = c % 2
                    zx, h2, x2 = (ins[n][:, u, :] for n in ("zx", "h2", "x2"))
                    dve.wait_ge(arrived[u], 48 * (c // 2 + 1))
                    dve.wait_ge(s_mm, c + 1)
                    for n in range(2):
                        cut = slice(n * HALF, (n + 1) * HALF)
                        last = nc.vector.tensor_tensor(zx[:, cut], ps[4 + 2 * u + n][:, :], zx[:, cut], ALU.add)
                    chain.up(last)
                    dve.wait_ge(s_chain, chain.n)
                    nc.vector.sem_inc(s_z, 1)
                    dve.wait_ge(s_th, c + 1)
                    link(nc.vector.tensor_tensor(th[:, u, :], th[:, u, :], h2, ALU.subtract))
                    link(nc.vector.tensor_tensor(th[:, u, :], th[:, u, :], zx, ALU.mult))
                    link(nc.vector.tensor_tensor(x2, x2, h2, ALU.add))
                    nc.vector.tensor_tensor(X[:, c, :], x2, th[:, u, :], ALU.add).then_inc(s_x, 1)
                    dve.wait_ge(s_x, b)
                    st.tile(X, c, link)

        @block.tensor
        def _(pe):
            def turn(b):
                for n in range(2):
                    if b >= 2:
                        pe.wait_ge(s_lo, 2 * (b - 2) + n + 1)
                    for k in range(4):
                        last = nc.tensor.transpose(ps[2 * (b % 2) + n][:, k * P:(k + 1) * P], X[:, b, (4 * n + k) * P:(4 * n + k + 1) * P], cst["ident"][:, :])
                    last.then_inc(s_turn, 1)

            turn(0)
            for b in range(NT):
                if b + 1 < NT:
                    turn(b + 1)
                if b >= 2:
                    pe.wait_ge(s_z, b - 1)
                for k in range(KD):
                    if b == 0:
                        pe.wait_ge(w.lo_out, k + 1)
                    if k % 4 == 0:
                        pe.wait_ge(s_lo, 2 * b + k // 4 + 1)
                    for x_, w_, f, e in ((hi, w.hi, k == 0, False), (hi, w.lo, False, False), (lo, w.hi, False, k == KD - 1)):
                        for n in range(2):
                            last = nc.tensor.matmul(ps[4 + 2 * (b % 2) + n][:, :], x_[:, b % 2, k, :], w_[:, k, n * HALF:(n + 1) * HALF], start=f, stop=e)
                last.then_inc(s_mm, 1)


def linear_phase(nc, a, t, cst, X, ps, st, dinv):
    with Phase(nc) as ctx:
        def sb(name, shape, dt=F32):
            return ctx.enter_context(nc.sbuf_tensor("l_" + name, shape, dt))

        def sem(name):
            return ctx.sem("l_" + name)

        ln = LayerNormRelu(ctx, nc, "l3", ps)
        st.begin(ctx, "l3s")
        stage = sb("stage", [P, 2, D])
        w_hi, w_lo = sb("w_hi", [P, KD, D], F32R), sb("w_lo", [P, KD, D], F32R)
        bias = sb("bias", [P, D])
        s_in, s_bias = [sem("w_in0"), sem("w_in1")], sem("bias_in")
        s_turn, s_hi, s_lo, s_done, s_chain = sem("w_turned"), sem("w_hi_out"), sem("w_lo_out"), sem("read"), sem("v_chain")
        block = ctx.enter_context(nc.Block())

        @block.sync
        def _(sp):
            for o in range(KD):
                if o >= 2:
                    sp.wait_ge(s_turn, 2 * (o - 1))
                sp.dma_start(stage[:, o % 2, :], a["L3_gnn_W"][o * P:(o + 1) * P, :]).then_inc(s_in[o % 2], 16)
            sp.dma_start(bias[:, :], row_broadcast(a["L3_gnn_b"], D)).then_inc(s_bias, 16)

        @block.scalar
        def _(act):
            st.scalar(act)
            for g in range(2 * KD):
                o, n = g // 2, g % 2
                act.wait_ge(s_turn, g + 1)
                nc.scalar.activation(w_hi[:, 4 * n:4 * n + 4, o * P:(o + 1) * P], ps[4 + g % 4][:, :].rearrange("p (k n) -> p k n", n=P), ACT.Copy).then_inc(s_hi, 1)
            for b in range(NT):
                act_h(nc, act, ln, X, st, b)
                ln.part_hi(act, b)

        @block.vector
        def _(dve):
            st.vector(dve)
            for g in range(2 * KD):
                o, n = g // 2, g % 2
                dve.wait_ge(s_hi, g + 1)
                nc.vector.tensor_tensor(w_lo[:, 4 * n:4 * n + 4, o * P:(o + 1) * P], ps[4 + g % 4][:, :].rearrange("p (k n) -> p k n", n=P),
                                        w_hi[:, 4 * n:4 * n + 4, o * P:(o + 1) * P].bitcast(F32), ALU.subtract).then_inc(s_lo, 1)
            dve.wait_ge(s_bias, 16)
            for b in range(NT + 1):
                if b < NT:
                    ln.part_lo(dve, b)
                if b >= 1:
                    c = b - 1
                    dve.wait_ge(ln.used, c + 1)
                    for n in range(2):
                        cut = slice(n * HALF, (n + 1) * HALF)
                        last = nc.vector.tensor_tensor(X[:, c, cut], ps[4 + 2 * (c % 2) + n][:, :], bias[:, cut], ALU.add)
                    last.then_inc(s_done, 1)
                    dve.wait_ge(s_done, c + 1)
                    nc.vector.tensor_scalar(X[:, c, :], X[:, c, :], dinv[:, c:c + 1], None, ALU.mult).then_inc(s_chain, 1)
            dve.wait_ge(s_chain, NT)

        @block.tensor
        def _(pe):
            for g in range(2 * KD):
                o, n = g // 2, g % 2
                pe.wait_ge(s_in[o % 2], 16 * (o // 2 + 1))
                if g >= 4:
                    pe.wait_ge(s_lo, g - 3)
                for k in range(4):
                    last = nc.tensor.transpose(ps[4 + g % 4][:, k * P:(k + 1) * P], stage[:, o % 2, (4 * n + k) * P:(4 * n + k + 1) * P], cst["ident"][:, :])
                last.then_inc(s_turn, 1)
            ln.turn(pe, cst["ident"][:, :], 0)
            pe.wait_ge(s_lo, 2 * KD)
            for b in range(NT):
                if b + 1 < NT:
                    ln.turn(pe, cst["ident"][:, :], b + 1)
                if b >= 2:
                    pe.wait_ge(s_done, b - 1)
                ln.product(pe, b, w_hi, w_lo, [ps[4 + 2 * (b % 2)], ps[5 + 2 * (b % 2)]])


def spread_phase(nc, a, t, cst, X, ps, dinv, out):
    with Phase(nc) as ctx:
        def sb(name, shape, dt=F32):
            return ctx.enter_context(nc.sbuf_tensor("f_" + name, shape, dt))

        def sem(name):
            return ctx.sem("f_" + name)

        c = sb("c", [P, NT, NP], F32R)
        y_hi, y_lo = sb("y_hi", [P, NT, D], F32R), sb("y_lo", [P, NT, D], F32R)
        x3 = sb("x3", [P, 2, D])
        s_c = [sem(f"c_in{k}") for k in range(NT)]
        s_hi, s_lo = sem("y_hi_out"), sem("y_lo_out")
        s_x, s_mm, s_add, s_out = [sem("x_in0"), sem("x_in1")], sem("sums_done"), sem("x_added"), sem("out")
        block = ctx.enter_context(nc.Block())

        @block.gpsimd
        def _(pool):
            for k in range(NT):
                pool.dma_start(c[:, k, :], t["counts"][k * P:(k + 1) * P, :]).then_inc(s_c[k], 16)

        @block.scalar
        def _(act):
            for k in range(NT):
                nc.scalar.activation(y_hi[:, k, :], X[:, k, :], ACT.Copy).then_inc(s_hi, 1)

        @block.sync
        def _(sp):
            for b in range(NT + 1):
                if b < NT:
                    if b >= 2:
                        sp.wait_ge(s_out, 16 * (b - 1))
                    sp.dma_start(x3[:, b % 2, :], t["x3"][b * P:(b + 1) * P, :]).then_inc(s_x[b % 2], 16)
                if b >= 1:
                    q = b - 1
                    rows = P if q < NT - 1 else TAIL
                    sp.wait_ge(s_add, q + 1)
                    sp.dma_start(out[q * P:q * P + rows, :], x3[0:rows, q % 2, :]).then_inc(s_out, 16)
            sp.wait_ge(s_out, 16 * NT)

        @block.vector
        def _(dve):
            for k in range(NT):
                dve.wait_ge(s_hi, k + 1)
                nc.vector.tensor_tensor(y_lo[:, k, :], X[:, k, :], y_hi[:, k, :].bitcast(F32), ALU.subtract).then_inc(s_lo, 1)
            for b in range(NT):
                dve.wait_ge(s_x[b % 2], 16 * (b // 2 + 1))
                dve.wait_ge(s_mm, b + 1)
                for n in range(2):
                    cut = slice(n * HALF, (n + 1) * HALF)
                    last = nc.vector.scalar_tensor_tensor(out=x3[:, b % 2, cut], in0=ps[2 * (b % 4) + n][:, :], scalar=dinv[:, b:b + 1],
                                                          in1=x3[:, b % 2, cut], op0=ALU.mult, op1=ALU.add)
                last.then_inc(s_add, 1)

        @block.tensor
        def _(pe):
            for b in range(NT):
                if b >= 4:
                    pe.wait_ge(s_add, b - 3)
                for k in range(NT):
                    if b == 0:
                        pe.wait_ge(s_c[k], 16)
                        pe.wait_ge(s_lo, k + 1)
                    for y, f, e in ((y_hi, k == 0, False), (y_lo, False, k == NT - 1)):
                        for n in range(2):
                            last = nc.tensor.matmul(ps[2 * (b % 4) + n][:, :], c[:, k, b * P:(b + 1) * P], y[:, k, n * HALF:(n + 1) * HALF], start=f, stop=e)
                last.then_inc(s_mm, 1)


def constants(nc, cst):
    with Phase(nc) as ctx:
        s_set, s_sel = (ctx.sem(n) for n in ("cst_set", "cst_selected"))
        block = ctx.enter_context(nc.Block())

        @block.gpsimd
        def _(pool):
            nc.gpsimd.memset(cst["ident"][:, :], 0.0).then_inc(s_set, 1)
            nc.gpsimd.memset(cst["tri"][:, :], 1.0).then_inc(s_set, 1)
            pool.wait_ge(s_set, 2)
            nc.gpsimd.affine_select(out=cst["ident"][:, :], in_=cst["ident"][:, :], compare_op=ALU.not_equal, fill=1.0,
                                    base=0, pattern=[[-1, P]], channel_multiplier=1).then_inc(s_sel, 1)
            nc.gpsimd.affine_select(out=cst["tri"][:, :], in_=cst["tri"][:, :], compare_op=ALU.is_gt, fill=0.0,
                                    base=0, pattern=[[1, P]], channel_multiplier=-1).then_inc(s_sel, 1)
            pool.wait_ge(s_sel, 2)

        @block.vector
        def _(dve):
            nc.vector.memset(cst["weigh"][:, 0:1], 1.0)
            nc.vector.memset(cst["weigh"][:, 1:2], 1.0 + LATER)
            nc.vector.memset(cst["weigh"][:, 2:3], LATER)
            nc.vector.memset(cst["ones"][:, :], 1.0)
            nc.vector.memset(cst["ones16"][:, :], 1.0)


def gnn_kernel(nc, a, out, stop=None):
    t = {"xl": nc.dram_tensor("t_xl", [NP, HL], F32, kind="Internal").ap(),
         "xr": nc.dram_tensor("t_xr", [NP, HL], F32, kind="Internal").ap(),
         "pairs": nc.dram_tensor("t_pairs", [NP * NP + CE, PAY], F32, kind="Internal").ap(),
         "typed": nc.dram_tensor("t_typed", [R * NP * NP + CE, 1], F32, kind="Internal").ap(),
         "counts": nc.dram_tensor("t_counts", [NP, NP], F32, kind="Internal").ap()}
    for n in ("x2", "x3", "h2", "zx"):
        t[n] = nc.dram_tensor("t_" + n, [NP, D], F32, kind="Internal").ap()

    with Phase(nc) as ctx:
        def sb(name, shape, dt=F32):
            return ctx.enter_context(nc.sbuf_tensor(name, shape, dt))

        ps = [ctx.enter_context(nc.psum_tensor(f"bank{i}", [P, HALF], F32)) for i in range(8)]
        cst = {"ident": sb("ident", [P, P]), "tri": sb("tri", [P, P], F16), "weigh": sb("weigh", [P, 4], F16),
               "ones": sb("ones", [P, 2]), "ones16": sb("ones16", [P, 2], F16)}
        X = sb("x", [P, NT, D])
        al, ar, dinv = sb("al", [P, NT]), sb("ar", [P, NT]), sb("dinv", [P, NT])
        constants(nc, cst)
        st = Norm(nc, sb)
        keep = {"mult8": sb("mult8", [P, EC]), "idx8": sb("idx8", [P, EC], I32)}
        with ExitStack() as part:
            def keep_sb(name, shape, dt=F32):
                return part.enter_context(nc.sbuf_tensor(name, shape, dt))
            keep["xl"] = keep_sb("keep_xl", [P, NT, H, DH + 2])
            edge_phase(nc, a, t, cst, X, ps, keep, st)
            pair_phase(nc, a, t, cst, X, ps, keep, st)
        with ExitStack() as part:
            h1 = part.enter_context(nc.sbuf_tensor("h1", [P, NT, D], F32))
            attention_phase(nc, a, t, cst, X, ps, st, h1, al, ar)
            neighbour_phase(nc, a, t, cst, X, ps, st, h1, al, ar, dinv, keep)
        with ExitStack() as part:
            h16 = part.enter_context(nc.sbuf_tensor("h16", [P, 2, NT, D], F16))
            gate_x_phase(nc, a, t, cst, X, ps, st, h16)
            root_phase(nc, a, t, cst, X, ps, st)
            relation_phase(nc, a, t, cst, X, ps, h16)
        gate_phase(nc, a, t, cst, X, ps, st)
        linear_phase(nc, a, t, cst, X, ps, st, dinv)
        spread_phase(nc, a, t, cst, X, ps, dinv, out)


_INS = ["x", "src", "dst", "edge_type_8", "L0_gnn_rms_w", "L0_gnn_W_down", "L0_gnn_Wl", "L0_gnn_Wr", "L0_gnn_att", "L0_gnn_W_up",
        "L1_gnn_W", "L1_gnn_a", "L2_gnn_weight", "L2_gnn_root", "L2_gnn_bias", "L2_gnn_w_gate", "L2_gnn_b_gate", "L3_gnn_W", "L3_gnn_b"]


def kernel(**inputs):
    import numpy as _np
    import concourse.bacc as _bacc
    from concourse import mybir as _mybir
    from concourse.bass_utils import run_bass_kernel_spmd as _run

    nc = _bacc.Bacc("TRN2", target_bir_lowering=False, num_devices=1)
    arrays, args = {}, {}
    for name in _INS:
        x = _np.ascontiguousarray(inputs[name])
        arrays[f"in_{name}_dram"] = x
        args[name] = nc.dram_tensor(f"in_{name}_dram", x.shape, _mybir.dt.from_np(x.dtype), kind="ExternalInput").ap()
    out = nc.dram_tensor("out_0_dram", (N, D), _mybir.dt.float32, kind="ExternalOutput").ap()
    gnn_kernel(nc, args, out)
    r = _run(nc, [arrays], core_ids=[0])
    return r.results[0]["out_0_dram"]
```

```python
import concourse.bass as bass
from concourse import mybir
from contextlib import ExitStack

F32 = mybir.dt.float32
F32R = mybir.dt.float32r
F16 = mybir.dt.float16
I32 = mybir.dt.int32
ALU = mybir.AluOpType
ACT = mybir.ActivationFunctionType
AX = mybir.AxisListType

P = 128
N = 1250
D = 1024
E = 20000
NT = -(-N // P)
NP = NT * P
TAIL = N - (NT - 1) * P
KD = D // P
HALF = 512
R = 8
HID, H, DH = 256, 4, 64
HK = HID // P
EP = 125
EC = E // EP
G = 4
U = 4
CH = EC // G
CE = G * P
PAY = 1 + H
HL = HID + H
PUTS_A1 = 20
XB = 4
ZW = 3200
LATER = 1024.0
FAR = 1.0e30
DCH = [(0, 512), (512, 512), (1024, N - 1024)]
LN_EPS = 1e-5


class Phase(ExitStack):

    def __init__(self, nc):
        super().__init__()
        self.nc, self.sems = nc, []
        self.callback(self.clear)

    def sem(self, name):
        self.sems.append(self.nc.alloc_semaphore(name))
        return self.sems[-1]

    def clear(self):
        self.nc.clear_and_free_semaphores(self.sems)
        self.nc.all_engine_barrier()


class Count:

    def __init__(self, sem):
        self.sem, self.n = sem, 0

    def up(self, instruction, by=1):
        instruction.then_inc(self.sem, by)
        self.n += by
        return self.n


class LayerNormRelu:

    def __init__(self, ctx, nc, tag, ps, src_tiles=None):
        def sem(name):
            return ctx.sem(f"{tag}_{name}")

        def sb(name, shape, dt):
            return ctx.enter_context(nc.sbuf_tensor(f"{tag}_{name}", shape, dt))

        self.nc, self.ps = nc, ps
        self.h = sb("h", [P, 2, D], F32)
        self.hi = sb("hi", [P, 2, KD, P], F32R)
        self.lo = sb("lo", [P, 2, KD, P], F32R)
        self.h_ready = sem("h_ready")
        self.turned = sem("turned")
        self.hi_ready = sem("hi_ready")
        self.lo_ready = sem("lo_ready")
        self.used = sem("used")
        self.h_read = sem("h_read")

    def turn(self, pe, ident, b):
        pe.wait_ge(self.h_ready, b + 1)
        for half in range(2):
            if b >= 2:
                pe.wait_ge(self.lo_ready, 2 * (b - 2) + half + 1)
            for k in range(4):
                last = self.nc.tensor.transpose(self.ps[2 * (b % 2) + half][:, k * P:(k + 1) * P],
                                                self.h[:, b % 2, (4 * half + k) * P:(4 * half + k + 1) * P], ident)
            last.then_inc(self.turned, 1)

    def part_hi(self, act, b):
        for half in range(2):
            act.wait_ge(self.turned, 2 * b + half + 1)
            if b >= 2 and half == 0:
                act.wait_ge(self.used, b - 1)
            self.nc.scalar.activation(self.hi[:, b % 2, 4 * half:4 * half + 4, :].rearrange("p k n -> p (k n)"),
                                      self.ps[2 * (b % 2) + half][:, :], ACT.Copy).then_inc(self.hi_ready, 1)

    def part_lo(self, dve, b):
        for half in range(2):
            dve.wait_ge(self.hi_ready, 2 * b + half + 1)
            self.nc.vector.tensor_tensor(self.lo[:, b % 2, 4 * half:4 * half + 4, :].rearrange("p k n -> p (k n)"),
                                         self.ps[2 * (b % 2) + half][:, :],
                                         self.hi[:, b % 2, 4 * half:4 * half + 4, :].rearrange("p k n -> p (k n)").bitcast(F32),
                                         ALU.subtract).then_inc(self.lo_ready, 1)

    def product(self, pe, b, w_hi, w_lo, banks, width=D, w_ready=None):
        cuts = [(c, min(HALF, width - c)) for c in range(0, width, HALF)]
        for k in range(KD):
            if k % 4 == 0:
                pe.wait_ge(self.lo_ready, 2 * b + k // 4 + 1)
            if w_ready is not None and b == 0:
                pe.wait_ge(w_ready, k + 1)
            for a, w, first, end in ((self.hi, w_hi, k == 0, False), (self.hi, w_lo, False, False),
                                     (self.lo, w_hi, False, k == KD - 1)):
                for bank, (c, n) in zip(banks, cuts):
                    last = self.nc.tensor.matmul(bank[:, 0:n], a[:, b % 2, k, :], w[:, k, c:c + n],
                                                 start=first, stop=end)
        last.then_inc(self.used, 1)
        return last


class Norm:

    def __init__(self, nc, sb):
        self.nc = nc
        self.parts, self.mv = sb("parts", [P, NT, 2, 6]), sb("mv", [P, NT, 2])
        self.var, self.std = sb("var", [P, NT]), sb("std", [P, NT])
        self.rstd, self.shift = sb("rstd", [P, NT]), sb("shift", [P, NT])

    def begin(self, ctx, tag):
        self.s_var, self.s_std = ctx.sem(tag + "_var"), ctx.sem(tag + "_std")
        self.s_rstd, self.s_ready = ctx.sem(tag + "_rstd"), ctx.sem(tag + "_norm_ready")

    def tile(self, X, b, link):
        self.nc.vector.bn_stats(self.parts[:, b, 0, :], X[:, b, 0:HALF])
        link(self.nc.vector.bn_stats(self.parts[:, b, 1, :], X[:, b, HALF:D]))
        link(self.nc.vector.bn_aggr(self.mv[:, b, :], self.parts[:, b, :, :].rearrange("p a c -> p (a c)")))

    def vector(self, dve):
        self.nc.vector.tensor_scalar_add(self.var[:, :], self.mv[:, :, 1], LN_EPS).then_inc(self.s_var, 1)
        dve.wait_ge(self.s_std, 1)
        self.nc.vector.reciprocal(self.rstd[:, :], self.std[:, :]).then_inc(self.s_rstd, 1)
        dve.wait_ge(self.s_rstd, 1)
        self.nc.vector.scalar_tensor_tensor(out=self.shift[:, :], in0=self.mv[:, :, 0], scalar=-1.0, in1=self.rstd[:, :],
                                            op0=ALU.mult, op1=ALU.mult).then_inc(self.s_ready, 1)

    def scalar(self, act):
        act.wait_ge(self.s_var, 1)
        self.nc.scalar.activation(self.std[:, :], self.var[:, :], ACT.Sqrt).then_inc(self.s_std, 1)
        act.wait_ge(self.s_ready, 1)


def act_h(nc, act, ln, X, s, b):
    if b >= 2:
        act.wait_ge(ln.turned, 2 * (b - 2) + 2)
    nc.scalar.activation(ln.h[:, b % 2, :], X[:, b, :], ACT.Relu, bias=s.shift[:, b:b + 1],
                         scale=s.rstd[:, b:b + 1]).then_inc(ln.h_ready, 1)


class Weights:

    def __init__(self, ctx, nc, tag, dram, width=D, slots=4):
        def sem(name):
            return ctx.sem(f"{tag}_{name}")
        self.nc, self.dram, self.slots = nc, dram, slots
        self.stage = ctx.enter_context(nc.sbuf_tensor(f"{tag}_stage", [P, slots, width], F32))
        self.hi = ctx.enter_context(nc.sbuf_tensor(f"{tag}_hi", [P, KD, width], F32R))
        self.lo = ctx.enter_context(nc.sbuf_tensor(f"{tag}_lo", [P, KD, width], F32R))
        self.loaded = [sem(f"loaded{i}") for i in range(slots)]
        self.hi_out = sem("hi_out")
        self.lo_out = sem("lo_out")

    def load(self, sp, ks=range(KD)):
        for k in ks:
            if k >= self.slots:
                sp.wait_ge(self.lo_out, k - self.slots + 1)
            sp.dma_start(self.stage[:, k % self.slots, :], self.dram[k * P:(k + 1) * P, :]).then_inc(self.loaded[k % self.slots], 16)

    def part_hi(self, act, k):
        act.wait_ge(self.loaded[k % self.slots], 16 * (k // self.slots + 1))
        self.nc.scalar.activation(self.hi[:, k, :], self.stage[:, k % self.slots, :], ACT.Copy).then_inc(self.hi_out, 1)

    def part_lo(self, dve, k):
        dve.wait_ge(self.hi_out, k + 1)
        self.nc.vector.tensor_tensor(self.lo[:, k, :], self.stage[:, k % self.slots, :], self.hi[:, k, :].bitcast(F32),
                                     ALU.subtract).then_inc(self.lo_out, 1)


def row_broadcast(dram_row, width):
    return dram_row.rearrange("(a n) -> a n", a=1).to_broadcast([P, width])


def edge_phase(nc, a, t, cst, X, ps, keep, st):
    with Phase(nc) as ctx:
        def sb(name, shape, dt=F32):
            return ctx.enter_context(nc.sbuf_tensor("e_" + name, shape, dt))

        def sem(name):
            return ctx.sem("e_" + name)

        ident, tri, ones_w = cst["ident"], cst["tri"], cst["weigh"]
        ln = LayerNormRelu(ctx, nc, "n0", ps)
        st.begin(ctx, "s0")
        wd = Weights(ctx, nc, "wd", a["L0_gnn_W_down"], HID, slots=4)
        rms = sb("rms", [P, KD])
        wlr = sb("wlr", [P, HK, 2 * HID])
        wlr_hi, wlr_lo = sb("wlr_hi", [P, HK, 2 * HID], F32R), sb("wlr_lo", [P, HK, 2 * HID], F32R)
        att, att2 = sb("att", [P, HID]), sb("att2", [P, HID])
        zero = sb("zero", [P, ZW])
        sumsq, meansq, rroot, rrms = sb("sumsq", [P, NT]), sb("meansq", [P, NT]), sb("rroot", [P, NT]), sb("rrms", [P, NT])
        sq = sb("sq", [P, D])
        xd = sb("xd", [P, 2, HID])
        xd_hi, xd_lo = sb("xd_hi", [P, 2, HK, P], F32R), sb("xd_lo", [P, 2, HK, P], F32R)
        xlr = sb("xlr", [P, XB, 2 * HL])
        sg, sv, sw = sb("sg", [P, HID]), sb("sv", [P, HID]), sb("sw", [P, 2, HID])
        self_pay = sb("self_pay", [P, NT, PAY])
        node_i, node_f, self_idx = sb("node_i", [P, NT], I32), sb("node_f", [P, NT]), sb("self_idx", [P, NT], I32)
        src, dst, typ = sb("src", [P, EC + U * G], I32), sb("dst", [P, EC + U * G], I32), sb("typ", [P, EC], I32)
        slot_i, slot = sb("slot_i", [P, G], I32), sb("slot", [P, G])
        live = sb("live", [P, 1])
        key = [sb(f"key{q}", [P, EC + G]) for q in range(2)]
        kcol = [sb(f"kcol{q}", [P, G]) for q in range(2)]
        rel = [sb(f"rel{q}", [P, EC]) for q in range(2)]
        spill = [sb(f"spill{q}", [P, G]) for q in range(2)]
        krow = [sb(f"krow{q}", [P, CE]) for q in range(2)]
        eq = [sb(f"eq{q}", [P, G, CE], F16) for q in range(2)]
        eqd = [sb(f"eqd{q}", [P, G, P], F16) for q in range(2)]
        mult = [sb(f"mult{q}", [P, G]) for q in range(2)]
        lead = [sb(f"lead{q}", [P, G]) for q in range(2)]
        row_f = [sb(f"row_f{q}", [P, G]) for q in range(2)]
        pair_idx = [sb(f"pair_idx{u}", [P, G], I32) for u in range(2)]
        idx_s = [sb(f"idx_s{u}", [P, G], I32) for u in range(U)]
        idx_d = [sb(f"idx_d{u}", [P, G], I32) for u in range(U)]
        gl = [sb(f"gl{u}", [P, G, HL]) for u in range(U)]
        gr = [sb(f"gr{u}", [P, G, HL]) for u in range(U)]
        gv = [sb(f"gv{u}", [P, G, HID]) for u in range(2)]
        logit = sb("logit", [P, G, H])
        pay = [sb(f"pay{u}", [P, G, PAY]) for u in range(2)]

        s_x = [sem(f"x_in{i}") for i in range(NT)]
        s_w, s_edges, s_rms = sem("w_in"), sem("edges_in"), sem("rms_in")
        s_xtail = sem("x_tail_zero")
        s_zero = sem("zero_ready")
        s_cleared = [[sem("pairs_cleared0"), sem("pairs_cleared1")], [sem("typed_cleared")]]
        s_rms_done = sem("wd_scaled")
        s_ss, s_ms, s_rr, s_rrms = sem("sumsq"), sem("meansq"), sem("rroot"), sem("rrms")
        s_xd, s_xdT, s_xdhi, s_xdlo, s_xlmm, s_xl = (sem(n) for n in (
            "xd_ready", "xd_turned", "xd_hi", "xd_lo", "lr_done", "xlr_ready"))
        s_wl_hi, s_wl_lo = sem("wlr_hi_out"), sem("wlr_lo_out")
        s_tab, s_xa = [sem(f"tab{i}") for i in range(XB)], sem("xl_kept")
        s_chain, s_self, s_iota, s_selfidx = sem("v_chain"), sem("self_pay_ready"), sem("iota"), sem("self_idx_ready")
        s_keys = sem("keys_ready")
        s_lin, s_sum, s_relu = sem("linear_parts"), sem("edge_sums"), sem("edge_relu")
        s_krow, s_krow_out, s_eq, s_mult = sem("krow_turned"), sem("krow_out"), sem("eq_ready"), sem("mult_done")
        s_idx, s_pay = sem("idx_ready"), sem("pay_ready")
        s_gl, s_gr = [sem(f"gl{u}") for u in range(U)], [sem(f"gr{u}") for u in range(U)]
        s_put, s_self_put = sem("pairs_put"), sem("self_loops_put")
        s_free, s_landed, s_begun = sem("gathered_read"), sem("puts_landed"), sem("gather_begun")

        xl_dram, xr_dram, pairs, typed = t["xl"], t["xr"], t["pairs"], t["typed"]
        keep_xl, mult8, idx8 = keep["xl"], keep["mult8"], keep["idx8"]
        n_zero = [(pairs, NP * NP * PAY), (typed, R * NP * NP)]

        pieces = [size // (P * ZW) for _, size in n_zero]

        def clear(eng, q, c):
            tab, size = n_zero[q]
            w = tab.shape[1]
            done = s_cleared[q][c % len(s_cleared[q])]
            if c < pieces[q]:
                flat = tab[0:size // w, :].rearrange("a b -> (a b)").rearrange("(c p n) -> c p n", p=P, n=ZW)
                eng.dma_start(flat[c], zero[:, :]).then_inc(done, 16)
            else:
                eng.dma_start(tab[size // w:size // w + CE, :].rearrange("(p n) w -> p (n w)", p=P),
                              zero[:, 0:CE * w // P]).then_inc(done, 16)

        block = ctx.enter_context(nc.Block())

        @block.sync
        def _(sp):
            with nc.allow_non_contiguous_dma(reason="1024 scales, one per partition and tile"):
                sp.dma_start(rms[:, :], a["L0_gnn_rms_w"].rearrange("(k p) -> p k", p=P)).then_inc(s_rms, 16)
            wd.load(sp, range(wd.slots))
            for b in range(NT):
                rows = P if b < NT - 1 else TAIL
                if b == 2:
                    wd.load(sp, range(wd.slots, KD))
                if b == NT - 1:
                    sp.wait_ge(s_xtail, 1)
                sp.dma_start(X[0:rows, b, :], a["x"][b * P:b * P + rows, :]).then_inc(s_x[b], 16)
            for j, w in enumerate(("L0_gnn_Wl", "L0_gnn_Wr")):
                sp.dma_start(wlr[:, :, j * HID:(j + 1) * HID], a[w].rearrange("(k p) n -> p k n", p=P)).then_inc(s_w, 16)
            sp.dma_start(att[:, :], row_broadcast(a["L0_gnn_att"].rearrange("h d -> (h d)"), HID)).then_inc(s_w, 16)
            sp.wait_ge(s_zero, 1)
            for c in range(2):
                clear(sp, 0, c)
            for c in range(2, pieces[0] + 1):
                sp.wait_ge(s_cleared[0][c % 2], 16 * (c // 2))
                clear(sp, 0, c)
                b = c - 8
                if 0 <= b < NT:
                    sp.wait_ge(s_lin, b + 1)
                    sp.dma_start(xl_dram[b * P:(b + 1) * P, :], xlr[:, b % XB, 0:HL]).then_inc(s_tab[b % XB], 16)
                    sp.dma_start(xr_dram[b * P:(b + 1) * P, :], xlr[:, b % XB, HL:2 * HL]).then_inc(s_tab[b % XB], 16)
            for u in range(2):
                sp.wait_ge(s_cleared[0][u], 16 * ((pieces[0] + 2 - u) // 2))
            sp.wait_ge(s_self, NT)
            with nc.allow_non_contiguous_dma(reason="one row of the table per node"):
                for b in range(NT):
                    rows = pairs[b * P * (NP + 1):(b * P + P - 1) * (NP + 1) + 1:NP + 1, :]
                    sp.dma_start(rows, self_pay[:, b, :]).then_inc(s_self_put, 16)
            for c in range(pieces[1] + 1):
                sp.wait_ge(s_pay, c + 1)
                clear(sp, 1, c)

        @block.gpsimd
        def _(pool):
            nc.gpsimd.memset(zero[:, :], 0.0).then_inc(s_zero, 1)
            nc.gpsimd.iota(node_i[:, :], pattern=[[P, NT]], base=0, channel_multiplier=1).then_inc(s_iota, 1)
            nc.gpsimd.iota(slot_i[:, :], pattern=[[P, G]], base=0, channel_multiplier=1).then_inc(s_iota, 1)
            for u in range(XB):
                pool.wait_ge(s_tab[u], 32 * len(range(u, NT, XB)))

            def gather(i, u):
                n = U * i + u
                pool.wait_ge(s_idx, n + 1)
                pool.wait_ge(s_free, n + 1)
                nc.gpsimd.sem_inc(s_begun, 1)
                for j in range(G):
                    pool.indirect_dma_start(out=gl[u % U][:, j, :], out_offset=None, in_=xl_dram[:, :],
                                            in_offset=bass.IndirectOffsetOnAxis(ap=idx_s[u % U][:, j:j + 1], axis=0)).then_inc(s_gl[u % U], 16)
                    pool.indirect_dma_start(out=gr[u % U][:, j, :], out_offset=None, in_=xr_dram[:, :],
                                            in_offset=bass.IndirectOffsetOnAxis(ap=idx_d[u % U][:, j:j + 1], axis=0)).then_inc(s_gr[u % U], 16)

            def put(i, u, first=False):
                n = U * i + u
                pool.wait_ge(s_pay, n + 1)
                if not first:
                    pool.wait_ge(s_put, n * 16 * G)
                nc.gpsimd.sem_inc(s_landed, 1)
                for j in range(G):
                    pool.indirect_dma_start(out=pairs[:, :], out_offset=bass.IndirectOffsetOnAxis(ap=pair_idx[u % 2][:, j:j + 1], axis=0),
                                            in_=pay[u % 2][:, j, :], in_offset=None, compute_op=ALU.add).then_inc(s_put, 16)

            for u in range(U - 1):
                gather(0, u)
            pool.wait_ge(s_self_put, 16 * NT)
            nc.gpsimd.sem_inc(s_landed, 1)
            gather(0, U - 1)
            put(0, 0, first=True)
            with pool.Fori(0, CH // U - 1) as i:
                for u in range(U):
                    gather(i, u + U)
                    put(i, u + 1)
            for u in range(1, U):
                put(CH // U - 1, u)
            pool.wait_ge(s_put, CH * G * 16)
            pool.wait_ge(s_cleared[1][0], 16 * (pieces[1] + 1))

        @block.scalar
        def _(act):
            for k in range(KD):
                act.wait_ge(s_rms_done, k + 1)
                nc.scalar.activation(wd.hi[:, k, :], wd.stage[:, k % wd.slots, :], ACT.Copy).then_inc(wd.hi_out, 1)
            for name, tile in (("src", src), ("dst", dst), ("edge_type_8", typ)):
                act.wait_ge(s_xtail, 2)
                act.dma_start(tile[0:EP, 0:EC], a[name].rearrange("(p c) -> p c", c=EC)).then_inc(s_edges, 16)
            st.scalar(act)
            for b in range(-1, NT + 3):
                if b == 1:
                    act.wait_ge(s_w, 48)
                    nc.scalar.activation(wlr_hi[:, :, :], wlr[:, :, :], ACT.Copy).then_inc(s_wl_hi, 1)
                if b + 1 < NT:
                    act_h(nc, act, ln, X, st, b + 1)
                    act.wait_ge(ln.h_ready, b + 2)
                    nc.scalar.activation(sq[:, :], ln.h[:, (b + 1) % 2, :], ACT.Square, accum_out=sumsq[:, b + 1:b + 2]).then_inc(s_ss, 1)
                if 0 <= b < NT:
                    ln.part_hi(act, b)
                    act.wait_ge(s_ms, b + 1)
                    nc.scalar.activation(rroot[:, b:b + 1], meansq[:, b:b + 1], ACT.Sqrt).then_inc(s_rr, 1)
                if 0 <= b - 2 < NT:
                    c = b - 2
                    act.wait_ge(ln.used, c + 1)
                    act.wait_ge(s_rrms, c + 1)
                    if c >= 2:
                        act.wait_ge(s_xdT, c - 1)
                    nc.scalar.activation(xd[:, c % 2, :], ps[(4, 7)[c % 2]][:, 0:HID], ACT.Copy, scale=rrms[:, c:c + 1]).then_inc(s_xd, 1)
                    act.wait_ge(s_xdT, c + 1)
                    if c >= 2:
                        act.wait_ge(s_xlmm, c - 1)
                    nc.scalar.activation(xd_hi[:, c % 2, :, :].rearrange("p k n -> p (k n)"), ps[5][:, 0:HID], ACT.Copy).then_inc(s_xdhi, 1)
                if 0 <= b - 3 < NT:
                    c = b - 3
                    act.wait_ge(s_xlmm, c + 1)
                    if c >= XB:
                        act.wait_ge(s_tab[c % XB], 32 * (c // XB))
                        act.wait_ge(s_self, c - XB + 1)
                        act.wait_ge(s_xa, c - XB + 1)
                    nc.scalar.activation(xlr[:, c % XB, :].rearrange("p (t n) -> p t n", t=2)[:, :, 0:HID],
                                         ps[6][:, :].rearrange("p (t n) -> p t n", t=2), ACT.Copy).then_inc(s_xl, 1)

            def keys_out(n, q):
                act.wait_ge(s_krow, n + 1)
                act.wait_ge(s_eq, n + 1)
                nc.scalar.activation(krow[q][:, :], ps[q][:, :], ACT.Copy).then_inc(s_krow_out, 1)

            nc.scalar.sem_inc(s_krow_out, 2)
            with act.Fori(0, CH // U) as i:
                for u in range(U):
                    n = U * i + u
                    keys_out(2 * n, 0)
                    keys_out(2 * n + 1, 1)
                    act.wait_ge(s_sum, n + 1)
                    nc.scalar.activation(gv[u % 2][:, :, :], gl[u][:, :, 0:HID], ACT.Relu, scale=0.8).then_inc(s_relu, 1)

        @block.vector
        def _(dve):
            chain = Count(s_chain)

            def link(ins):
                chain.up(ins)
                dve.wait_ge(s_chain, chain.n)

            link(nc.vector.memset(X[:, NT - 1, :], 0.0))
            nc.vector.sem_inc(s_xtail, 1)
            dve.wait_ge(s_rms, 16)
            for k in range(KD):
                dve.wait_ge(wd.loaded[k % wd.slots], 16 * (k // wd.slots + 1))
                nc.vector.tensor_scalar(wd.stage[:, k % wd.slots, :], wd.stage[:, k % wd.slots, :], rms[:, k:k + 1], None, ALU.mult).then_inc(s_rms_done, 1)
                if k >= 1:
                    wd.part_lo(dve, k - 1)
            wd.part_lo(dve, KD - 1)
            for tile in (src, dst, typ):
                last = nc.vector.memset(tile[:, :], 0)
            link(last)
            nc.vector.sem_inc(s_xtail, 1)
            for b in range(NT):
                dve.wait_ge(s_x[b], 16)
                st.tile(X, b, link)
            st.vector(dve)
            dve.wait_ge(s_w, 48)
            link(nc.vector.tensor_scalar(att[:, :], att[:, :], -1.0, None, ALU.mult))
            link(nc.vector.tensor_scalar(att2[:, :], att[:, :], 0.2, None, ALU.mult))
            def self_loops(c):
                dve.wait_ge(s_xl, c + 1)
                both = xlr[:, c % XB, :].rearrange("p (t n) -> p t n", t=2)
                xl_, xr_ = xlr[:, c % XB, 0:HID], xlr[:, c % XB, HL:HL + HID]
                if c >= 1:
                    dve.wait_ge(s_self, c)
                link(nc.vector.tensor_tensor(sw[:, :, :], both[:, :, 0:HID], att2[:, :].unsqueeze(1).to_broadcast([P, 2, HID]), ALU.mult))
                nc.vector.tensor_reduce(both[:, :, HID:HL], sw[:, :, :].rearrange("p t (h d) -> p t h d", d=DH), axis=AX.X, op=ALU.add).then_inc(s_lin, 1)
                nc.vector.tensor_copy(keep_xl[:, c, :, 0:DH], xl_.rearrange("p (h d) -> p h d", d=DH)).then_inc(s_xa, 1)
                link(nc.vector.tensor_tensor(sg[:, :], xl_, xr_, ALU.add))
                link(nc.vector.scalar_tensor_tensor(out=sv[:, :], in0=sg[:, :], scalar=0.2, in1=sg[:, :], op0=ALU.mult, op1=ALU.max))
                dve.wait_ge(s_lin, c + 1)
                link(nc.vector.tensor_tensor(sw[:, 0, :], sv[:, :], att[:, :], ALU.mult))
                nc.vector.tensor_reduce(self_pay[:, c, 1:PAY], sw[:, 0, :].rearrange("p (h d) -> p h d", d=DH), axis=AX.X, op=ALU.add).then_inc(s_self, 1)

            link(nc.vector.memset(keep_xl[:, :, :, DH:DH + 2], 1.0))
            link(nc.vector.memset(self_pay[:, :, 0:1], 1.0))
            for b in range(NT + 4):
                if b < NT:
                    dve.wait_ge(s_ss, b + 1)
                    nc.vector.tensor_scalar(meansq[:, b:b + 1], sumsq[:, b:b + 1], 1.0 / D, 1e-6, ALU.mult, ALU.add).then_inc(s_ms, 1)
                    ln.part_lo(dve, b)
                    dve.wait_ge(s_rr, b + 1)
                    nc.vector.reciprocal(rrms[:, b:b + 1], rroot[:, b:b + 1]).then_inc(s_rrms, 1)
                if b == 1:
                    dve.wait_ge(s_wl_hi, 1)
                    nc.vector.tensor_tensor(wlr_lo[:, :, :], wlr[:, :, :], wlr_hi[:, :, :].bitcast(F32), ALU.subtract).then_inc(s_wl_lo, 1)
                    dve.wait_ge(s_iota, 2)
                    link(nc.vector.tensor_copy(node_f[:, :], node_i[:, :]))
                    link(nc.vector.tensor_scalar(node_f[:, :], node_f[:, :], float(NP + 1), None, ALU.mult))
                    nc.vector.tensor_copy(self_idx[:, :], node_f[:, :]).then_inc(s_selfidx, 1)
                    link(nc.vector.tensor_copy(slot[:, :], slot_i[:, :]))
                    link(nc.vector.tensor_scalar(live[:, :], slot[:, 0:1], float(EP), None, ALU.is_lt))
                    link(nc.vector.tensor_scalar(spill[0][:, :], slot[:, :], float(NP * NP), None, ALU.add))
                    link(nc.vector.tensor_scalar(spill[1][:, :], slot[:, :], float(R * NP * NP), None, ALU.add))
                    dve.wait_ge(s_edges, 48)
                    link(nc.vector.scalar_tensor_tensor(out=key[0][:, 0:EC], in0=dst[:, 0:EC], scalar=float(NP), in1=src[:, 0:EC], op0=ALU.mult, op1=ALU.add))
                    link(nc.vector.scalar_tensor_tensor(out=key[1][:, 0:EC], in0=typ[:, :], scalar=float(NP), in1=src[:, 0:EC], op0=ALU.mult, op1=ALU.add))
                    link(nc.vector.scalar_tensor_tensor(out=key[1][:, 0:EC], in0=key[1][:, 0:EC], scalar=float(NP), in1=dst[:, 0:EC], op0=ALU.mult, op1=ALU.add))
                    for q in range(2):
                        link(nc.vector.memset(key[q][:, EC:EC + G], 0.0))
                        sp_all = spill[q][:, :].unsqueeze(1).to_broadcast([P, CH, G])
                        k3, r3 = (v[q][:, 0:EC].rearrange("p (c g) -> p c g", g=G) for v in (key, rel))
                        link(nc.vector.tensor_tensor(r3, k3, sp_all, ALU.subtract))
                        link(nc.vector.tensor_scalar(rel[q][:, :], rel[q][:, :], live[:, 0:1], None, ALU.mult))
                        link(nc.vector.tensor_tensor(k3, r3, sp_all, ALU.add))
                        link(nc.vector.tensor_copy(kcol[q][:, :], key[q][:, 0:G]))
                    nc.vector.sem_inc(s_keys, 1)
                if 0 <= b - 4 < NT:
                    self_loops(b - 4)
                if 0 <= b - 2 < NT:
                    c = b - 2
                    dve.wait_ge(s_xdhi, c + 1)
                    nc.vector.tensor_tensor(xd_lo[:, c % 2, :, :].rearrange("p k n -> p (k n)"), ps[5][:, 0:HID],
                                            xd_hi[:, c % 2, :, :].rearrange("p k n -> p (k n)").bitcast(F32), ALU.subtract).then_inc(s_xdlo, 1)

            for u in range(U - 1):
                nc.vector.tensor_copy(idx_s[u][:, :], src[:, u * G:(u + 1) * G])
                link(nc.vector.tensor_copy(idx_d[u][:, :], dst[:, u * G:(u + 1) * G]))
                nc.vector.sem_inc(s_idx, 1)
            before = chain.n
            nc.vector.sem_inc(s_eq, 2)
            nc.vector.sem_inc(s_free, U)

            def chunk(i, u, at):
                steps = [0]

                def step(ins):
                    ins.then_inc(s_chain, 1)
                    steps[0] += 1
                    dve.wait_ge(s_chain, at + steps[0])

                n = U * i + u
                cols = bass.ds(n * G, G)
                after = bass.ds(n * G + G, G)
                ahead = bass.ds(n * G + (U - 1) * G, G)
                nc.vector.tensor_copy(idx_s[(u + U - 1) % U][:, :], src[:, ahead])
                step(nc.vector.tensor_copy(idx_d[(u + U - 1) % U][:, :], dst[:, ahead]))
                nc.vector.sem_inc(s_idx, 1)
                dve.wait_ge(s_gl[u], (i + 1) * 16 * G)
                dve.wait_ge(s_gr[u], (i + 1) * 16 * G)
                nc.vector.tensor_tensor(gl[u][:, :, :], gl[u][:, :, :], gr[u][:, :, :], ALU.add).then_inc(s_sum, 1)
                for q in range(2):
                    dve.wait_ge(s_krow_out, 2 * n + q + 3)
                    dve.wait_ge(s_mult, 2 * n + q + 1)
                    for g in range(G):
                        ins = nc.vector.tensor_scalar(eq[q][:, g, :], krow[q][:, :], key[q][:, bass.ds(n * G + g, 1)], None, ALU.is_equal)
                    step(ins)
                    diagonal = eq[q][:, :, :].rearrange("p g (c e) -> p (g c) e", e=P)[:, 0:G * G:G + 1, :]
                    nc.vector.tensor_tensor(eqd[q][:, :, :], diagonal, tri[:, :].unsqueeze(1).to_broadcast([P, G, P]), ALU.mult).then_inc(s_eq, 1)
                nc.vector.tensor_copy(kcol[0][:, :], key[0][:, after])
                step(nc.vector.tensor_copy(kcol[1][:, :], key[1][:, after]))
                nc.vector.sem_inc(s_keys, 1)
                dve.wait_ge(s_landed, n + 1)

                def rows(q):
                    dve.wait_ge(s_mult, 2 * n + q + 3)
                    m = mult[q][:, :] if q == 0 else mult8[:, cols]
                    step(nc.vector.tensor_copy(m, ps[2 + q][:, 0:G]))
                    step(nc.vector.tensor_scalar(lead[q][:, :], m, LATER, None, ALU.is_lt))
                    step(nc.vector.tensor_tensor(row_f[q][:, :], lead[q][:, :], rel[q][:, cols], ALU.mult))
                    step(nc.vector.tensor_tensor(pair_idx[u % 2][:, :] if q == 0 else idx8[:, cols], row_f[q][:, :], spill[q][:, :], ALU.add))

                rows(0)
                dve.wait_ge(s_relu, n + 1)
                gw = gr[u][:, :, 0:HID]
                step(nc.vector.tensor_tensor(gw, gv[u % 2][:, :, :], att[:, :].unsqueeze(1).to_broadcast([P, G, HID]), ALU.mult))
                step(nc.vector.tensor_reduce(logit[:, :, :], gw.rearrange("p g (h d) -> p g h d", d=DH), axis=AX.X, op=ALU.add))
                step(nc.vector.tensor_tensor(logit[:, :, :], logit[:, :, :], gl[u][:, :, HID:HL], ALU.add))
                nc.vector.sem_inc(s_free, 1)
                rows(1)
                step(nc.vector.tensor_tensor(pay[u % 2][:, :, 1:PAY], logit[:, :, :], mult[0][:, :].unsqueeze(2).to_broadcast([P, G, H]), ALU.mult))
                step(nc.vector.tensor_copy(pay[u % 2][:, :, 0:1], mult[0][:, :].unsqueeze(2)))
                nc.vector.sem_inc(s_pay, 1)
                return steps[0]

            per = 17
            with dve.Fori(0, CH // U) as i:
                for u in range(U):
                    got = chunk(i, u, i * (U * per) + (before + u * per))
                    assert got == per, got

        @block.tensor
        def _(pe):
            pe.wait_ge(wd.lo_out, KD)
            for b in range(NT + 3):
                if b < NT:
                    ln.turn(pe, ident[:, :], b)
                if 0 <= b - 1 < NT:
                    c = b - 1
                    if c >= 2:
                        pe.wait_ge(s_xd, c - 1)
                    ln.product(pe, c, wd.hi, wd.lo, [ps[(4, 7)[c % 2]][:, 0:HID]], HID)
                if 0 <= b - 2 < NT:
                    c = b - 2
                    pe.wait_ge(s_xd, c + 1)
                    if c >= 1:
                        pe.wait_ge(s_xdlo, c)
                    for k in range(HK):
                        last = nc.tensor.transpose(ps[5][:, k * P:(k + 1) * P], xd[:, c % 2, k * P:(k + 1) * P], ident[:, :])
                    last.then_inc(s_xdT, 1)
                if 0 <= b - 3 < NT:
                    c = b - 3
                    if c == 0:
                        pe.wait_ge(s_wl_lo, 1)
                    pe.wait_ge(s_xdlo, c + 1)
                    if c >= 1:
                        pe.wait_ge(s_xl, c)
                    for k in range(HK):
                        for x_, w_, first, end in ((xd_hi, wlr_hi, k == 0, False), (xd_hi, wlr_lo, False, False), (xd_lo, wlr_hi, False, k == HK - 1)):
                            last = nc.tensor.matmul(ps[6][:, :], x_[:, c % 2, k, :], w_[:, k, :], start=first, stop=end)
                    last.then_inc(s_xlmm, 1)
            pe.wait_ge(ln.lo_ready, 2 * NT)
            nc.tensor.sem_inc(s_mult, 2)
            with pe.Fori(0, CH) as i:
                pe.wait_ge(s_keys, i + 1)
                for q in range(2):
                    pe.wait_ge(s_krow_out, 2 * i + 2)
                    for g in range(G):
                        last = nc.tensor.transpose(ps[q][:, g * P:(g + 1) * P],
                                                   kcol[q][:, g:g + 1].to_broadcast([P, P]), ident[:, :])
                    last.then_inc(s_krow, 1)
                for q in range(2):
                    pe.wait_ge(s_eq, 2 * i + q + 3)
                    for j in range(G):
                        for g in range(G):
                            nc.tensor.matmul(ps[2 + q][:, j:j + 1], eq[q][:, g, j * P:(j + 1) * P],
                                             ones_w[:, (1 if g < j else 0):(2 if g < j else 1)], start=(g == 0), stop=False)
                        last = nc.tensor.matmul(ps[2 + q][:, j:j + 1], eqd[q][:, j, :], ones_w[:, 2:3], start=False, stop=True)
                    last.then_inc(s_mult, 1)




def pair_phase(nc, a, t, cst, X, ps, keep, st):
    with Phase(nc) as ctx:
        def sb(name, shape, dt=F32):
            return ctx.enter_context(nc.sbuf_tensor("p_" + name, shape, dt))

        def sem(name):
            return ctx.sem("p_" + name)

        ident = cst["ident"]
        row = [sb(f"row{u}", [P, NP, PAY]) for u in range(2)]
        cnt = [sb(f"cnt{u}", [P, NP]) for u in range(2)]
        off = [sb(f"off{u}", [P, NP]) for u in range(2)]
        least, ninv = sb("least", [P, NP]), [sb(f"ninv{u}", [P, NP]) for u in range(2)]
        lnc = sb("lnc", [P, NP])
        LG = 4
        lg = sb("lg", [P, LG, NP])
        TB = 3
        top, neg = sb("top", [P, NT, H]), sb("neg", [P, NT, H])
        pT = sb("pT", [P, 2, NT, P])
        den, iden = sb("den", [P, H]), sb("iden", [P, H])
        agg = sb("agg", [P, HID])
        agg_hi, agg_lo = sb("agg_hi", [P, HK, P], F32R), sb("agg_lo", [P, HK, P], F32R)
        wu, wu_hi, wu_lo = sb("wu", [P, HK, D]), sb("wu_hi", [P, HK, D], F32R), sb("wu_lo", [P, HK, D], F32R)
        s_row = [sem("row_in0"), sem("row_in1")]
        s_w, s_whi, s_wlo = sem("wu_in"), sem("wu_hi_out"), sem("wu_lo_out")
        s_cnt, s_cntout = sem("cnt_ready"), [sem("cnt_out0"), sem("cnt_out1")]
        s_row_free = sem("row_read")
        s_chain, s_neg, s_exp = sem("v_chain"), sem("neg_ready"), sem("exp_ready")
        s_turn, s_pT, s_head = sem("p_turned"), sem("pT_ready"), sem("head_done")
        s_lnout = sem("ln_out")
        s_off, s_least, s_guess, s_inv, s_lg = sem("off_ready"), sem("least_ready"), sem("guess_ready"), sem("ninv_ready"), sem("lg_ready")
        s_norm, s_aggT, s_ahi, s_alo, s_up, s_xadd = (sem(n) for n in (
            "agg_normed", "agg_turned", "agg_hi_out", "agg_lo_out", "up_done", "x_added"))
        rows_dram, counts, typed = t["pairs"], t["counts"], t["typed"]
        keep_xl, mult8, idx8 = keep["xl"], keep["mult8"], keep["idx8"]
        block = ctx.enter_context(nc.Block())
        CUTS = [(0, 4), (4, 4), (8, 2)]

        @block.sync
        def _(sp):
            for b in range(NT):
                if b == 1:
                    sp.dma_start(wu[:, :, :], a["L0_gnn_W_up"].rearrange("(k p) n -> p k n", p=P)).then_inc(s_w, 16)
                if b >= 2:
                    sp.wait_ge(s_row_free, b - 1)
                sp.dma_start(row[b % 2][:, :, :], rows_dram[b * P * NP:(b + 1) * P * NP, :].rearrange("(p n) w -> p n w", p=P)).then_inc(s_row[b % 2], 16)
                if b >= 1:
                    sp.wait_ge(s_cnt, b)
                    sp.dma_start(counts[(b - 1) * P:b * P, :], cnt[(b - 1) % 2][:, :]).then_inc(s_cntout[(b - 1) % 2], 16)
            sp.wait_ge(s_cnt, NT)
            sp.dma_start(counts[(NT - 1) * P:NT * P, :], cnt[(NT - 1) % 2][:, :]).then_inc(s_cntout[(NT - 1) % 2], 16)
            for u in range(2):
                sp.wait_ge(s_cntout[u], 16 * (NT // 2))

        @block.gpsimd
        def _(pool):
            for n in range(NT * H):
                b, h = n // H, n % H
                pool.wait_ge(s_inv, b + 1)
                if n >= LG:
                    pool.wait_ge(s_turn, 3 * (n - LG + 1))
                ins = nc.gpsimd.tensor_tensor(lg[:, n % LG, :].unsqueeze(2), row[b % 2][:, :, 1 + h:2 + h], ninv[b % 2][:, :].unsqueeze(2), ALU.mult)
                ins.then_inc(s_lg, 1)
                if h == H - 1:
                    pool.wait_ge(s_cnt, b + 1)
                    pool.wait_ge(s_lg, n + 1)
                    nc.gpsimd.sem_inc(s_row_free, 1)

        @block.vector
        def _(dve):
            chain = Count(s_chain)

            def link(ins):
                chain.up(ins)
                dve.wait_ge(s_chain, chain.n)

            def up_add(b):
                dve.wait_ge(s_up, b + 1)
                for n in range(2):
                    last = nc.vector.tensor_tensor(X[:, b, n * HALF:(n + 1) * HALF], X[:, b, n * HALF:(n + 1) * HALF], ps[6 + n][:, :], ALU.add)
                last.then_inc(s_xadd, 1)
                dve.wait_ge(s_xadd, b + 1)
                st.tile(X, b, link)

            def finish(b):
                dve.wait_ge(s_head, H * (b + 1))
                sums = ps[(4, 3)[b % 2]][:, 0:H * (DH + 2)].rearrange("p (h d) -> p h d", d=DH + 2)
                link(nc.vector.tensor_scalar_add(den[:, :].unsqueeze(2), sums[:, :, DH:DH + 1], 1e-16))
                link(nc.vector.reciprocal(iden[:, :], den[:, :]))
                nc.vector.tensor_tensor(agg[:, :].rearrange("p (h d) -> p h d", d=DH), sums[:, :, 0:DH],
                                        iden[:, :].unsqueeze(2).to_broadcast([P, H, DH]), ALU.mult).then_inc(s_norm, 1)

            def agg_low(b):
                dve.wait_ge(s_ahi, b + 1)
                nc.vector.tensor_tensor(agg_lo[:, :, :].rearrange("p k n -> p (k n)"), ps[5][:, 0:HID],
                                        agg_hi[:, :, :].rearrange("p k n -> p (k n)").bitcast(F32), ALU.subtract).then_inc(s_alo, 1)

            def least_one(b):
                u = b % 2
                dve.wait_ge(s_row[u], 16 * (b // 2 + 1))
                nc.vector.tensor_scalar_max(least[:, :].unsqueeze(2), row[u][:, :, 0:1], 1.0).then_inc(s_least, 1)
                link(nc.vector.tensor_scalar(off[u][:, :].unsqueeze(2), row[u][:, :, 0:1], 0.5, -FAR, ALU.is_lt, ALU.mult))

            def invert(b):
                u = b % 2
                dve.wait_ge(s_guess, b + 1)
                link(nc.vector.tensor_tensor(least[:, :], least[:, :], ninv[u][:, :], ALU.mult))
                nc.vector.scalar_tensor_tensor(out=ninv[u][:, :], in0=least[:, :], scalar=-2.0, in1=ninv[u][:, :],
                                               op0=ALU.add, op1=ALU.mult).then_inc(s_inv, 1)
                nc.vector.tensor_tensor(off[u][:, :], off[u][:, :], lnc[:, :], ALU.add).then_inc(s_off, 1)

            def mask(n):
                b, h = n // H, n % H
                dve.wait_ge(s_off, b + 1)
                dve.wait_ge(s_lg, n + 1)
                link(nc.vector.tensor_tensor_reduce(out=lg[:, n % LG, :], in0=lg[:, n % LG, :], in1=off[b % 2][:, :], scale=1.0, scalar=-2.0 * FAR,
                                                    op0=ALU.add, op1=ALU.max, accum_out=top[:, b, h:h + 1]))
                nc.vector.tensor_scalar(neg[:, b, h:h + 1], top[:, b, h:h + 1], -1.0, None, ALU.mult).then_inc(s_neg, 1)

            least_one(0)
            invert(0)
            for n in range(NT * H):
                b, h = n // H, n % H
                mask(n)
                if n == 3:
                    dve.wait_ge(s_whi, 1)
                    nc.vector.tensor_tensor(wu_lo[:, :, :], wu[:, :, :], wu_hi[:, :, :].bitcast(F32), ALU.subtract).then_inc(s_wlo, 1)
                if h == 0 and b >= 2:
                    agg_low(b - 2)
                if h == 1 and b + 1 < NT:
                    least_one(b + 1)
                if h == 2 and b + 1 < NT:
                    invert(b + 1)
                if h == 2 and b >= 1:
                    finish(b - 1)
                if h == 3 and b >= 2:
                    up_add(b - 2)
            agg_low(NT - 2)
            up_add(NT - 2)
            finish(NT - 1)
            agg_low(NT - 1)
            up_add(NT - 1)
            dve.wait_ge(s_xadd, NT)

        @block.scalar
        def _(act):
            def evac(n):
                for c, (k0, kn) in enumerate(CUTS):
                    act.wait_ge(s_turn, 3 * n + c + 1)
                    if n >= 2 and c == 0:
                        act.wait_ge(s_head, n - 1)
                    nc.scalar.activation(pT[:, n % 2, k0:k0 + kn, :].rearrange("p k n -> p (k n)"), ps[c][:, 0:kn * P], ACT.Copy).then_inc(s_pT, 1)

            def agg_hi_out(b):
                act.wait_ge(s_aggT, b + 1)
                if b >= 1:
                    act.wait_ge(s_up, b)
                nc.scalar.activation(agg_hi[:, :, :].rearrange("p k n -> p (k n)"), ps[5][:, 0:HID], ACT.Copy).then_inc(s_ahi, 1)

            def count(b):
                u = b % 2
                act.wait_ge(s_row[u], 16 * (b // 2 + 1))
                if b >= 2:
                    act.wait_ge(s_cntout[u], 16 * (b // 2))
                nc.scalar.activation(cnt[u][:, :].unsqueeze(2), row[u][:, :, 0:1], ACT.Copy).then_inc(s_cnt, 1)

            def guess(b):
                u = b % 2
                act.wait_ge(s_least, b + 1)
                if b >= 1:
                    act.wait_ge(s_off, b)
                nc.scalar.activation(lnc[:, :], least[:, :], ACT.Ln).then_inc(s_lnout, 1)
                act.wait_ge(s_lnout, b + 1)
                if b >= 2:
                    act.wait_ge(s_lg, H * (b - 1))
                nc.scalar.activation(ninv[u][:, :], lnc[:, :], ACT.Exp, scale=-1.0).then_inc(s_guess, 1)

            guess(0)
            count(0)
            for b in range(NT):
                for h in range(H):
                    n = b * H + h
                    act.wait_ge(s_neg, n + 1)
                    nc.scalar.activation(lg[:, n % LG, :], lg[:, n % LG, :], ACT.Exp, bias=neg[:, b, h:h + 1]).then_inc(s_exp, 1)
                    if h == 1 and b + 1 < NT:
                        guess(b + 1)
                    if h == 2 and b + 1 < NT:
                        count(b + 1)
                    if n >= 1:
                        evac(n - 1)
                    if n == 1:
                        act.wait_ge(s_w, 16)
                        nc.scalar.activation(wu_hi[:, :, :], wu[:, :, :], ACT.Copy).then_inc(s_whi, 1)
                    if h == 3 and b >= 1:
                        agg_hi_out(b - 1)
            evac(NT * H - 1)
            agg_hi_out(NT - 1)

        @block.tensor
        def _(pe):
            def turn_agg(b):
                pe.wait_ge(s_norm, b + 1)
                if b >= 1:
                    pe.wait_ge(s_alo, b)
                for k in range(HK):
                    last = nc.tensor.transpose(ps[5][:, k * P:(k + 1) * P], agg[:, k * P:(k + 1) * P], ident[:, :])
                last.then_inc(s_aggT, 1)

            def up(b):
                if b == 0:
                    pe.wait_ge(s_wlo, 1)
                pe.wait_ge(s_alo, b + 1)
                if b >= 1:
                    pe.wait_ge(s_xadd, b)
                for k in range(HK):
                    for x_, w_, first, end in ((agg_hi, wu_hi, k == 0, False), (agg_hi, wu_lo, False, False), (agg_lo, wu_hi, False, k == HK - 1)):
                        for n in range(2):
                            last = nc.tensor.matmul(ps[6 + n][:, :], x_[:, k, :], w_[:, k, n * HALF:(n + 1) * HALF], start=first, stop=end)
                last.then_inc(s_up, 1)

            def turn_p(n):
                pe.wait_ge(s_exp, n + 1)
                for c, (k0, kn) in enumerate(CUTS):
                    g = 3 * n + c
                    if g >= TB:
                        pe.wait_ge(s_pT, g - TB + 1)
                    for k in range(kn):
                        last = nc.tensor.transpose(ps[g % TB][:, k * P:(k + 1) * P], lg[:, n % LG, (k0 + k) * P:(k0 + k + 1) * P], ident[:, :])
                    last.then_inc(s_turn, 1)

            def weigh(n):
                b, h = n // H, n % H
                pe.wait_ge(s_pT, 3 * n + 3)
                if h == 0 and b >= 2:
                    pe.wait_ge(s_norm, b - 1)
                for k in range(NT):
                    last = nc.tensor.matmul(ps[(4, 3)[b % 2]][:, h * (DH + 2):(h + 1) * (DH + 2)], pT[:, n % 2, k, :], keep_xl[:, k, h, :], start=(k == 0), stop=(k == NT - 1))
                last.then_inc(s_head, 1)

            for n in range(NT * H):
                turn_p(n)
                if n >= 1:
                    weigh(n - 1)
                if n % H == 2 and n > H:
                    turn_agg(n // H - 1)
                if n % H == 0 and n // H >= 2:
                    up(n // H - 2)
            weigh(NT * H - 1)
            up(NT - 2)
            turn_agg(NT - 1)
            up(NT - 1)


def product_phase(nc, a, t, cst, X, ps, st, tag, weight, finish, new_norm=True):
    with Phase(nc) as ctx:
        ln = LayerNormRelu(ctx, nc, tag, ps)
        if new_norm:
            st.begin(ctx, tag + "s")
        w = Weights(ctx, nc, tag + "w", weight)
        done = ctx.sem(tag + "_read")
        f = finish(ctx, ln, done)
        block = ctx.enter_context(nc.Block())

        @block.sync
        def _(sp):
            w.load(sp)
            f.sync(sp)

        @block.gpsimd
        def _(pool):
            f.gpsimd(pool)

        @block.scalar
        def _(act):
            if new_norm:
                st.scalar(act)
            f.before_h(act, 0)
            act_h(nc, act, ln, X, st, 0)
            for b in range(NT + 1):
                if b + 1 < NT:
                    f.before_h(act, b + 1)
                    act_h(nc, act, ln, X, st, b + 1)
                if b < NT:
                    if b == 0:
                        for k in range(KD):
                            w.part_hi(act, k)
                            if k == 1:
                                ln.part_hi(act, b)
                    else:
                        ln.part_hi(act, b)
                if b >= 1:
                    f.scalar(act, b - 1)

        @block.vector
        def _(dve):
            if new_norm:
                st.vector(dve)
            for b in range(NT + 1):
                if b == 0:
                    for k in range(KD):
                        w.part_lo(dve, k)
                        if k == 1:
                            ln.part_lo(dve, b)
                elif b < NT:
                    ln.part_lo(dve, b)
                if b >= 1:
                    f.vector(dve, b - 1)
            f.vector_end(dve)

        @block.tensor
        def _(pe):
            ln.turn(pe, cst["ident"][:, :], 0)
            for b in range(NT):
                if b + 1 < NT:
                    ln.turn(pe, cst["ident"][:, :], b + 1)
                if b >= 2:
                    pe.wait_ge(done, b - 1)
                ln.product(pe, b, w.hi, w.lo, [ps[4 + 2 * (b % 2)], ps[5 + 2 * (b % 2)]], w_ready=w.lo_out)


class Finish:

    def __init__(self, nc, ctx, ln, done, ps, X):
        self.nc, self.ln, self.done, self.ps, self.X = nc, ln, done, ps, X
        self.make(ctx)

    def make(self, ctx):
        pass

    def bank(self, b, n):
        return self.ps[4 + 2 * (b % 2) + n]

    def sync(self, sp):
        pass

    def gpsimd(self, pool):
        pass

    def before_h(self, act, b):
        pass

    def scalar(self, act, b):
        pass

    def vector(self, dve, b):
        pass

    def vector_end(self, dve):
        pass


def attention_phase(nc, a, t, cst, X, ps, st, h1, al, ar, keep):
    a_row = a["L1_gnn_a"].rearrange("a n -> (a n)")

    class F(Finish):
        def make(self, ctx):
            def sem(name):
                return ctx.sem("a_" + name)
            self.vec = ctx.enter_context(nc.sbuf_tensor("a_vec", [P, 2 * D], F32))
            self.prod = ctx.enter_context(nc.sbuf_tensor("a_prod", [P, D], F32))
            self.vec_in, self.chain, self.typed = sem("vec_in"), sem("v_chain"), sem("typed_put")

        def gpsimd(self, pool):
            typed_puts(nc, pool, t, keep, self.typed, range(PUTS_A1))

        def sync(self, sp):
            sp.dma_start(self.vec[:, :], row_broadcast(a_row, 2 * D)).then_inc(self.vec_in, 16)

        def scalar(self, act, b):
            act.wait_ge(self.ln.used, b + 1)
            for n in range(2):
                last = nc.scalar.activation(h1[:, b, n * HALF:(n + 1) * HALF], self.bank(b, n)[:, :], ACT.Copy)
            last.then_inc(self.done, 1)

        def vector(self, dve, b):
            if b == 0:
                dve.wait_ge(self.vec_in, 16)
            dve.wait_ge(self.done, b + 1)
            for j, out in enumerate((al, ar)):
                if 2 * b + j > 0:
                    dve.wait_ge(self.chain, 2 * b + j)
                nc.vector.tensor_tensor_reduce(out=self.prod[:, :], in0=h1[:, b, :], in1=self.vec[:, j * D:(j + 1) * D], scale=1.0, scalar=0.0,
                                               op0=ALU.mult, op1=ALU.add, accum_out=out[:, b:b + 1]).then_inc(self.chain, 1)

        def vector_end(self, dve):
            dve.wait_ge(self.chain, 2 * NT)

    product_phase(nc, a, t, cst, X, ps, st, "a1", a["L1_gnn_W"], lambda ctx, ln, done: F(nc, ctx, ln, done, ps, X))


def typed_puts(nc, pool, t, keep, done, chunks):
    for i, c in enumerate(chunks):
        if i >= 1:
            pool.wait_ge(done, 16 * G * i)
        for e in range(c * G, (c + 1) * G):
            pool.indirect_dma_start(out=t["typed"][:, :], out_offset=bass.IndirectOffsetOnAxis(ap=keep["idx8"][:, e:e + 1], axis=0),
                                    in_=keep["mult8"][:, e:e + 1], in_offset=None, compute_op=ALU.add).then_inc(done, 16)
    pool.wait_ge(done, 16 * G * len(chunks))


def neighbour_phase(nc, a, t, cst, X, ps, st, h1, al, ar, dinv, keep):
    with Phase(nc) as ctx:
        def sb(name, shape, dt=F32):
            return ctx.enter_context(nc.sbuf_tensor("q_" + name, shape, dt))

        def sem(name):
            return ctx.sem("q_" + name)

        ident, ones = cst["ident"], cst["ones"]
        h1_lo = sb("h1_lo", [P, NT, D], F32R)
        CB = 3
        p = sb("p", [P, CB, NT, P])
        p_hi, p_lo = sb("p_hi", [P, 2, NT, P], F32R), sb("p_lo", [P, 2, NT, P], F32R)
        h1_hi = sb("h1_hi", [P, NT, D], F32R)
        whole = sb("whole", [P, NT, P], F16)
        al_row = sb("al_row", [P, NP])
        u1, u2, ex = sb("u1", [P, NT, P]), sb("u2", [P, 2, NT, P]), sb("ex", [P, 2, NT, P])
        root = sb("root", [P, NT])
        rs = sb("rs", [P, NT])
        irs = sb("irs", [P, NT])
        neg, pos = sb("neg", [P, 2, D]), sb("pos", [P, D])
        s_p = [sem(f"p_in{u}") for u in range(CB)]
        s_off, s_whole, s_deg, s_root = sem("self_off"), sem("counts_copied"), sem("deg_done"), sem("deg_root")
        s_row, s_rowout = sem("al_turned"), sem("al_row_out")
        s_chain, s_u, s_ex, s_pr = sem("v_chain"), sem("u_ready"), sem("ex_ready"), sem("p_ready")
        s_phi, s_plo, s_hhi, s_hlo = sem("p_hi_out"), sem("p_lo_out"), sem("h1_hi_out"), sem("h1_lo_out")
        s_agg, s_neg, s_en, s_x, s_out = sem("agg_done"), sem("neg_ready"), sem("exp_ready"), sem("x_ready"), sem("x_out")
        s_bank, s_typed = sem("banks_read"), sem("typed_put")
        block = ctx.enter_context(nc.Block())

        @block.sync
        def _(sp):
            def counts_in(b):
                cols = t["counts"].rearrange("(k p) n -> p k n", p=P)[:, :, b * P:(b + 1) * P]
                sp.dma_start(p[:, b % CB, :, :], cols).then_inc(s_p[b % CB], 16)

            for b in range(CB):
                counts_in(b)
            for b in range(NT):
                if b + CB < NT:
                    sp.wait_ge(s_agg, b + 1)
                    counts_in(b + CB)
                if b >= 2:
                    sp.wait_ge(s_x, b - 1)
                    sp.dma_start(t["x2"][(b - 2) * P:(b - 1) * P, :], X[:, b - 2, :]).then_inc(s_out, 16)
            for b in range(NT - 2, NT):
                sp.wait_ge(s_x, b + 1)
                sp.dma_start(t["x2"][b * P:(b + 1) * P, :], X[:, b, :]).then_inc(s_out, 16)
            sp.wait_ge(s_out, 16 * NT)

        @block.gpsimd
        def _(pool):
            typed_puts(nc, pool, t, keep, s_typed, range(PUTS_A1, CH))

        @block.scalar
        def _(act):
            for c in range(3):
                n = min(4, NT - 4 * c)
                act.wait_ge(s_row, c + 1)
                nc.scalar.activation(al_row[:, 4 * c * P:(4 * c + n) * P], ps[c][:, 0:n * P], ACT.Copy).then_inc(s_rowout, 1)

            def exp_u(b):
                act.wait_ge(s_p[b % CB], 16 * (b // CB + 1))
                if b >= 1:
                    act.wait_ge(s_deg, b)
                nc.scalar.activation(whole[:, :, :], p[:, b % CB, :, :], ACT.Copy).then_inc(s_whole, 1)
                act.wait_ge(s_u, b + 1)
                if b >= 2:
                    act.wait_ge(s_pr, b - 1)
                nc.scalar.activation(ex[:, b % 2, :, :], u2[:, b % 2, :, :], ACT.Exp, scale=-1.0).then_inc(s_ex, 1)

            def p_part(b):
                act.wait_ge(s_pr, b + 1)
                if b >= 2:
                    act.wait_ge(s_agg, b - 1)
                nc.scalar.activation(p_hi[:, b % 2, :, :], p[:, b % CB, :, :], ACT.Copy).then_inc(s_phi, 1)

            nc.scalar.activation(h1_hi[:, 0, :], h1[:, 0, :], ACT.Copy).then_inc(s_hhi, 1)
            exp_u(0)
            nc.scalar.activation(h1_hi[:, 1, :], h1[:, 1, :], ACT.Copy).then_inc(s_hhi, 1)
            p_part(0)
            for k in range(2, 5):
                nc.scalar.activation(h1_hi[:, k, :], h1[:, k, :], ACT.Copy).then_inc(s_hhi, 1)
            exp_u(1)
            for k in range(5, NT):
                nc.scalar.activation(h1_hi[:, k, :], h1[:, k, :], ACT.Copy).then_inc(s_hhi, 1)
            for b in range(NT + 1):
                if b + 1 < NT:
                    p_part(b + 1)
                if b + 2 < NT:
                    exp_u(b + 2)
                if b >= 1:
                    act.wait_ge(s_neg, b)
                    nc.scalar.activation(neg[:, (b - 1) % 2, :], neg[:, (b - 1) % 2, :], ACT.Exp).then_inc(s_en, 1)
            act.wait_ge(s_deg, NT)
            nc.scalar.activation(root[:, :], ps[5][:, 0:NT], ACT.Sqrt).then_inc(s_root, 1)

        @block.vector
        def _(dve):
            chain = Count(s_chain)

            def link(ins):
                chain.up(ins)
                dve.wait_ge(s_chain, chain.n)

            def leaky(b):
                link(nc.vector.tensor_tensor(u1[:, :, :], al_row[:, b * P:(b + 1) * P].unsqueeze(1).to_broadcast([P, NT, P]),
                                             ar[:, :].unsqueeze(2).to_broadcast([P, NT, P]), ALU.add))
                if b >= 2:
                    dve.wait_ge(s_ex, b - 1)
                nc.vector.scalar_tensor_tensor(out=u2[:, b % 2, :, :], in0=u1[:, :, :], scalar=0.1, in1=u1[:, :, :], op0=ALU.mult, op1=ALU.max).then_inc(s_u, 1)
                dve.wait_ge(s_u, b + 1)
                dve.wait_ge(s_whole, b + 1)
                nc.vector.tensor_tensor(p[:, b % CB, b, :], p[:, b % CB, b, :], ident[:, :], ALU.subtract).then_inc(s_off, 1)

            def weigh(b):
                dve.wait_ge(s_ex, b + 1)
                dve.wait_ge(s_off, b + 1)
                nc.vector.tensor_tensor(p[:, b % CB, :, :], p[:, b % CB, :, :], ex[:, b % 2, :, :], ALU.mult).then_inc(s_pr, 1)

            def p_part(b):
                dve.wait_ge(s_phi, b + 1)
                nc.vector.tensor_tensor(p_lo[:, b % 2, :, :], p[:, b % CB, :, :], p_hi[:, b % 2, :, :].bitcast(F32), ALU.subtract).then_inc(s_plo, 1)

            def h1_part(k):
                dve.wait_ge(s_hhi, k + 1)
                nc.vector.tensor_tensor(h1_lo[:, k, :], h1[:, k, :], h1_hi[:, k, :].bitcast(F32), ALU.subtract).then_inc(s_hlo, 1)

            def start(b):
                dve.wait_ge(s_agg, b + 1)
                link(nc.vector.tensor_scalar_add(rs[:, b:b + 1], ps[6 + b % 2][:, 0:1], 1e-5))
                link(nc.vector.reciprocal(irs[:, b:b + 1], rs[:, b:b + 1]))
                if b >= 2:
                    dve.wait_ge(s_x, b - 1)
                for n in range(2):
                    last = nc.vector.tensor_scalar(neg[:, b % 2, n * HALF:(n + 1) * HALF], ps[2 * (b % 2) + n][:, :], irs[:, b:b + 1], 0.0, ALU.mult, ALU.min)
                last.then_inc(s_neg, 1)
                for n in range(2):
                    last = nc.vector.tensor_scalar(pos[:, n * HALF:(n + 1) * HALF], ps[2 * (b % 2) + n][:, :], irs[:, b:b + 1], 0.0, ALU.mult, ALU.max)
                last.then_inc(s_bank, 1)

            def end(b):
                dve.wait_ge(s_bank, b + 1)
                link(nc.vector.tensor_tensor(X[:, b, :], X[:, b, :], pos[:, :], ALU.add))
                dve.wait_ge(s_en, b + 1)
                nc.vector.scalar_tensor_tensor(out=X[:, b, :], in0=neg[:, b % 2, :], scalar=-1.0, in1=X[:, b, :], op0=ALU.add, op1=ALU.add).then_inc(s_x, 1)
                dve.wait_ge(s_x, b + 1)
                st.tile(X, b, link)

            dve.wait_ge(s_rowout, 3)
            leaky(0)
            h1_part(0)
            weigh(0)
            h1_part(1)
            p_part(0)
            for k in range(2, 5):
                h1_part(k)
            leaky(1)
            for k in range(5, NT):
                h1_part(k)
            for b in range(NT + 1):
                if b + 1 < NT:
                    weigh(b + 1)
                if b + 2 < NT:
                    leaky(b + 2)
                if b + 1 < NT:
                    p_part(b + 1)
                if b >= 1:
                    start(b - 1)
                    end(b - 1)
            dve.wait_ge(s_root, 1)
            link(nc.vector.reciprocal(dinv[:, :], root[:, :]))

        @block.tensor
        def _(pe):
            for c in range(3):
                for k in range(min(4, NT - 4 * c)):
                    last = nc.tensor.transpose(ps[c][:, k * P:(k + 1) * P], al[:, 4 * c + k:4 * c + k + 1].to_broadcast([P, P]), ident[:, :])
                last.then_inc(s_row, 1)

            def degree(b):
                pe.wait_ge(s_whole, b + 1)
                for k in range(NT):
                    last = nc.tensor.matmul(ps[5][:, b:b + 1], whole[:, k, :], cst["ones16"][:, 0:1], start=(k == 0), stop=(k == NT - 1))
                last.then_inc(s_deg, 1)

            degree(0)
            for b in range(NT):
                if 1 <= b < NT - 1:
                    degree(b + 1)
                if b >= 2:
                    pe.wait_ge(s_bank, b - 1)
                pe.wait_ge(s_plo, b + 1)
                for k in range(NT):
                    if b == 0 and k == 5:
                        degree(1)
                    if b == 0:
                        pe.wait_ge(s_hlo, k + 1)
                    first, end = k == 0, k == NT - 1
                    hi, lo = p_hi[:, b % 2, k, :], p_lo[:, b % 2, k, :]
                    nc.tensor.matmul(ps[6 + b % 2][:, 0:1], p[:, b % CB, k, :], ones[:, 0:1], start=first, stop=end)
                    for w_, h_, start_, stop_ in ((hi, h1_hi, first, False), (hi, h1_lo, False, False), (lo, h1_hi, False, end)):
                        for n in range(2):
                            last = nc.tensor.matmul(ps[2 * (b % 2) + n][:, :], w_, h_[:, k, n * HALF:(n + 1) * HALF], start=start_, stop=stop_)
                last.then_inc(s_agg, 1)


def gate_x_phase(nc, a, t, cst, X, ps, st, h16):
    class F(Finish):
        def make(self, ctx):
            def sem(name):
                return ctx.sem("g_" + name)
            self.bias = ctx.enter_context(nc.sbuf_tensor("g_bias", [P, D], F32))
            self.z = ctx.enter_context(nc.sbuf_tensor("g_z", [P, 2, D], F32))
            self.bias_in, self.h_out, self.z_out = sem("bias_in"), [sem("h_out0"), sem("h_out1")], [sem("z_out0"), sem("z_out1")]
            self.h_hi, self.h_lo = sem("h16_hi"), sem("h16_lo")

        def sync(self, sp):
            sp.dma_start(self.bias[:, :], row_broadcast(a["L2_gnn_b_gate"], D)).then_inc(self.bias_in, 16)
            for b in range(NT + 1):
                if b < NT:
                    sp.wait_ge(self.ln.h_ready, b + 1)
                    sp.dma_start(t["h2"][b * P:(b + 1) * P, :], self.ln.h[:, b % 2, :]).then_inc(self.h_out[b % 2], 16)
                if b >= 1:
                    sp.wait_ge(self.done, b)
                    sp.dma_start(t["zx"][(b - 1) * P:b * P, :], self.z[:, (b - 1) % 2, :]).then_inc(self.z_out[(b - 1) % 2], 16)
            for u in range(2):
                sp.wait_ge(self.z_out[u], 16 * (NT // 2))
                sp.wait_ge(self.h_out[u], 16 * (NT // 2))

        def gpsimd(self, pool):
            for b in range(NT):
                pool.wait_ge(self.ln.h_ready, b + 1)
                nc.gpsimd.tensor_copy(h16[:, 0, b, :], self.ln.h[:, b % 2, :]).then_inc(self.h_hi, 1)
                pool.wait_ge(self.h_hi, b + 1)
                nc.gpsimd.tensor_tensor(h16[:, 1, b, :], self.ln.h[:, b % 2, :], h16[:, 0, b, :], ALU.subtract).then_inc(self.h_lo, 1)

        def before_h(self, act, b):
            if b >= 2:
                act.wait_ge(self.h_lo, b - 1)
                act.wait_ge(self.h_out[b % 2], 16 * (b // 2))

        def vector(self, dve, b):
            if b == 0:
                dve.wait_ge(self.bias_in, 16)
            if b >= 2:
                dve.wait_ge(self.z_out[b % 2], 16 * (b // 2))
            dve.wait_ge(self.ln.used, b + 1)
            for n in range(2):
                last = nc.vector.tensor_tensor(self.z[:, b % 2, n * HALF:(n + 1) * HALF], self.bank(b, n)[:, :], self.bias[:, n * HALF:(n + 1) * HALF], ALU.add)
            last.then_inc(self.done, 1)

    product_phase(nc, a, t, cst, X, ps, st, "g2", a["L2_gnn_w_gate"][D:2 * D, :], lambda ctx, ln, done: F(nc, ctx, ln, done, ps, X))


def root_phase(nc, a, t, cst, X, ps, st):
    class F(Finish):
        def make(self, ctx):
            self.bias = ctx.enter_context(nc.sbuf_tensor("o_bias", [P, D], F32))
            self.bias_in = ctx.sem("o_bias_in")

        def sync(self, sp):
            sp.dma_start(self.bias[:, :], row_broadcast(a["L2_gnn_bias"], D)).then_inc(self.bias_in, 16)

        def vector(self, dve, b):
            if b == 0:
                dve.wait_ge(self.bias_in, 16)
            dve.wait_ge(self.ln.used, b + 1)
            for n in range(2):
                last = nc.vector.tensor_tensor(X[:, b, n * HALF:(n + 1) * HALF], self.bank(b, n)[:, :], self.bias[:, n * HALF:(n + 1) * HALF], ALU.add)
            last.then_inc(self.done, 1)

        def vector_end(self, dve):
            dve.wait_ge(self.done, NT)

    product_phase(nc, a, t, cst, X, ps, st, "o2", a["L2_gnn_root"], lambda ctx, ln, done: F(nc, ctx, ln, done, ps, X), new_norm=False)


def relation_phase(nc, a, t, cst, X, ps, h16):
    with Phase(nc) as ctx:
        def sb(name, shape, dt=F32):
            return ctx.enter_context(nc.sbuf_tensor("r_" + name, shape, dt))

        def sem(name):
            return ctx.sem("r_" + name)

        ones16 = cst["ones16"]
        NC = len(DCH)
        WMAX = max(w for _, w in DCH)
        c16 = [sb(f"c16_{u}", [P, NT, WMAX], F16) for u in range(2)]
        s_hi, s_lo = sb("s_hi", [P, KD, WMAX], F32R), sb("s_lo", [P, KD, WMAX], F32R)
        stage = sb("stage", [P, 2, D])
        w_hi, w_lo = sb("w_hi", [P, KD, D], F32R), sb("w_lo", [P, KD, D], F32R)
        cnt = [sb(f"cnt{u}", [P, 4]) for u in range(2)]
        AB = 3
        c_in = [sem("c_in0"), sem("c_in1")]
        w_in = [sem("w_in0"), sem("w_in1")]
        s_whi, s_wlo, s_wfree = sem("w_hi_out"), sem("w_lo_out"), sem("w_used")
        s_sum, s_shi, s_slo = sem("sums_done"), sem("s_hi_out"), sem("s_lo_out")
        s_cnt, s_inv, s_chain = sem("cnt_done"), sem("inv_ready"), sem("v_chain")
        s_mm, s_add = sem("product_done"), sem("u_added")
        s_cread, s_begun = sem("c_read"), sem("load_begun")
        TILES = NT
        table = t["typed"][0:R * NP * NP, :].rearrange("(r k p n) w -> r p k (n w)", r=R, p=P, n=NP)
        weight = a["L2_gnn_weight"]
        block = ctx.enter_context(nc.Block())

        @block.gpsimd
        def _(pool):
            def load(r, c, n, u, wait=True):
                c0, cw = DCH[c]
                if wait:
                    pool.wait_ge(s_cread, n - 1)
                    nc.gpsimd.sem_inc(s_begun, 1)
                src = table[bass.ds(r, 1)] if not isinstance(r, int) else table[r:r + 1]
                pool.dma_start(c16[u][:, :, 0:cw], src.rearrange("r p k n -> (r p) k n")[:, :, c0:c0 + cw]).then_inc(c_in[u], 16)

            for j in range(2 * NC):
                load(j // NC, j % NC, j, j % 2, j >= 2)
            with pool.Fori(1, R // 2) as i:
                for j in range(2 * NC):
                    load(2 * i + j // NC, j % NC, 2 * NC * i + j, j % 2)

        @block.sync
        def _(sp):
            def load(r, k, wait=True):
                if wait:
                    sp.wait_ge(s_wlo, r * KD + (k - 1))
                w = weight[bass.ds(r, 1)] if not isinstance(r, int) else weight[r:r + 1]
                sp.dma_start(stage[:, k % 2, :], w.rearrange("r (k p) n -> k (r p) n", p=P)[k]).then_inc(w_in[k % 2], 16)

            for k in range(KD):
                load(0, k, k >= 2)
            with sp.Fori(1, R) as r:
                for k in range(KD):
                    load(r, k)

        @block.scalar
        def _(act):
            def body(r, first):
                for c in range(NC):
                    c0, cw = DCH[c]
                    for k in range(KD):
                        g = c * KD + k
                        act.wait_ge(s_sum, r * (NC * KD) + (g + 1))
                        if not (first and c == 0) and k == 0:
                            act.wait_ge(s_mm, r * TILES + TILES * 0 + before[c])
                        nc.scalar.activation(s_hi[:, k, 0:cw], ps[g % AB][:, 0:cw], ACT.Copy).then_inc(s_shi, 1)
                        if c == 0:
                            act.wait_ge(w_in[k % 2], r * 64 + 16 * (k // 2 + 1))
                            if not first:
                                act.wait_ge(s_wfree, r * KD)
                            nc.scalar.activation(w_hi[:, k, :], stage[:, k % 2, :], ACT.Copy).then_inc(s_whi, 1)

            before = [0, 4, 8]
            body(0, True)
            with act.Fori(1, R) as r:
                body(r, False)

        @block.vector
        def _(dve):
            def body(r, first):
                for c in range(NC):
                    c0, cw = DCH[c]
                    for k in range(KD):
                        g = c * KD + k
                        dve.wait_ge(s_shi, r * (NC * KD) + (g + 1))
                        nc.vector.tensor_tensor(s_lo[:, k, 0:cw], ps[g % AB][:, 0:cw], s_hi[:, k, 0:cw].bitcast(F32), ALU.subtract).then_inc(s_slo, 1)
                        if c == 0:
                            dve.wait_ge(s_whi, r * KD + (k + 1))
                            nc.vector.tensor_tensor(w_lo[:, k, :], stage[:, k % 2, :], w_hi[:, k, :].bitcast(F32), ALU.subtract).then_inc(s_wlo, 1)
                    m = -(-cw // P)
                    u = c % 2
                    dve.wait_ge(s_cnt, r * NC + (c + 1))
                    nc.vector.tensor_scalar_max(cnt[u][:, 0:m], ps[3][:, 4 * u:4 * u + m], 1.0).then_inc(s_chain, 1)
                    dve.wait_ge(s_chain, r * (2 * NC) + (2 * c + 1))
                    nc.vector.reciprocal(cnt[u][:, 0:m], cnt[u][:, 0:m]).then_inc(s_chain, 1)
                    dve.wait_ge(s_chain, r * (2 * NC) + (2 * c + 2))
                    nc.vector.sem_inc(s_inv, 1)
                    for i in range(m):
                        b = c0 // P + i
                        dve.wait_ge(s_mm, r * TILES + (b + 1))
                        rows = min(P, cw - i * P)
                        for n in range(2):
                            last = nc.vector.scalar_tensor_tensor(out=X[0:rows, b, n * HALF:(n + 1) * HALF], in0=ps[4 + 2 * (b % 2) + n][0:rows, :],
                                                                  scalar=cnt[u][0:rows, i:i + 1], in1=X[0:rows, b, n * HALF:(n + 1) * HALF], op0=ALU.mult, op1=ALU.add)
                        last.then_inc(s_add, 1)

            body(0, True)
            with dve.Fori(1, R) as r:
                body(r, False)
            dve.wait_ge(s_add, R * TILES)

        @block.tensor
        def _(pe):
            def sums(r, c, par, first):
                c0, cw = DCH[c]
                u = (par * NC + c) % 2
                pe.wait_ge(c_in[u], half(r, par) + 16 * ((par * NC + c) // 2 + 1))
                for k in range(KD):
                    g = c * KD + k
                    if not (first and g < AB):
                        pe.wait_ge(s_slo, r * (NC * KD) + (g + 1 - AB))
                    for part in range(2):
                        for j in range(NT):
                            last = nc.tensor.matmul(ps[g % AB][:, 0:cw], h16[:, part, j, k * P:(k + 1) * P], c16[u][:, j, 0:cw],
                                                    start=(part == 0 and j == 0), stop=(part == 1 and j == NT - 1))
                    last.then_inc(s_sum, 1)
                if not (first and c < 1):
                    pe.wait_ge(s_inv, r * NC + c)
                for i in range(-(-cw // P)):
                    rows = min(P, cw - i * P)
                    for j in range(NT):
                        last = nc.tensor.matmul(ps[3][0:rows, 4 * (c % 2) + i:4 * (c % 2) + i + 1], c16[u][:, j, i * P:i * P + rows], ones16[:, 0:1], start=(j == 0), stop=(j == NT - 1))
                last.then_inc(s_cnt, 1)
                pe.wait_ge(s_cnt, r * NC + (c + 1))
                nc.tensor.sem_inc(s_cread, 1)

            def products(r, c, first):
                c0, cw = DCH[c]
                for i in range(-(-cw // P)):
                    b = c0 // P + i
                    rows = min(P, cw - i * P)
                    if not (first and b < 2):
                        pe.wait_ge(s_add, r * TILES + (b - 1))
                    for k in range(KD):
                        if i == 0:
                            pe.wait_ge(s_slo, r * (NC * KD) + (c * KD + k + 1))
                            if c == 0:
                                pe.wait_ge(s_wlo, r * KD + (k + 1))
                        for x_, w_, f, e in ((s_hi, w_hi, k == 0, False), (s_hi, w_lo, False, False), (s_lo, w_hi, False, k == KD - 1)):
                            for n in range(2):
                                last = nc.tensor.matmul(ps[4 + 2 * (b % 2) + n][0:rows, :], x_[:, k, i * P:i * P + rows], w_[:, k, n * HALF:(n + 1) * HALF], start=f, stop=e)
                    last.then_inc(s_mm, 1)
                    if b == NT - 1:
                        pe.wait_ge(s_mm, r * TILES + TILES)
                        nc.tensor.sem_inc(s_wfree, KD)

            def half(r, par):
                return (r - par) * (8 * NC)

            def body(r, par, first):
                for c in range(NC):
                    sums(r, c, par, first)
                    products(r, c, first)

            body(0, 0, True)
            body(1, 1, False)
            with pe.Fori(1, R // 2) as i:
                body(2 * i, 0, False)
                body(2 * i + 1, 1, False)


def gate_phase(nc, a, t, cst, X, ps, st):
    with Phase(nc) as ctx:
        def sb(name, shape, dt=F32):
            return ctx.enter_context(nc.sbuf_tensor("z_" + name, shape, dt))

        def sem(name):
            return ctx.sem("z_" + name)

        w = Weights(ctx, nc, "zw", a["L2_gnn_w_gate"][0:D, :])
        hi, lo = sb("hi", [P, 2, KD, P], F32R), sb("lo", [P, 2, KD, P], F32R)
        th = sb("th", [P, 2, D])
        ins = {n: sb(n, [P, 2, D]) for n in ("zx", "h2", "x2")}
        arrived = [sem("in0"), sem("in1")]
        s_turn, s_hi, s_lo, s_mm, s_th, s_z, s_x, s_out = (sem(n) for n in (
            "turned", "hi_out", "lo_out", "product_done", "tanh_ready", "z_ready", "x_ready", "x_out"))
        s_chain = sem("v_chain")
        block = ctx.enter_context(nc.Block())

        @block.sync
        def _(sp):
            w.load(sp)
            for b in range(NT):
                if b >= 2:
                    sp.wait_ge(s_x, b - 1)
                for n in ins:
                    sp.dma_start(ins[n][:, b % 2, :], t[n][b * P:(b + 1) * P, :]).then_inc(arrived[b % 2], 16)
            for b in range(NT):
                sp.wait_ge(s_x, b + 1)
                sp.dma_start(t["x3"][b * P:(b + 1) * P, :], X[:, b, :]).then_inc(s_out, 16)
            sp.wait_ge(s_out, 16 * NT)

        @block.scalar
        def _(act):
            for b in range(NT):
                if b == 1:
                    for k in range(2, KD):
                        w.part_hi(act, k)
                for n in range(2):
                    if b == 0:
                        w.part_hi(act, n)
                    act.wait_ge(s_turn, 2 * b + n + 1)
                    if b >= 2 and n == 0:
                        act.wait_ge(s_mm, b - 1)
                    nc.scalar.activation(hi[:, b % 2, 4 * n:4 * n + 4, :].rearrange("p k n -> p (k n)"), ps[2 * (b % 2) + n][:, :], ACT.Copy).then_inc(s_hi, 1)
                if b >= 2:
                    act.wait_ge(s_x, b - 1)
                nc.scalar.activation(th[:, b % 2, :], X[:, b, :], ACT.Tanh).then_inc(s_th, 1)

        @block.vector
        def _(dve):
            chain = Count(s_chain)

            def link(ins_):
                chain.up(ins_)
                dve.wait_ge(s_chain, chain.n)

            def lows(b):
                for n in range(2):
                    dve.wait_ge(s_hi, 2 * b + n + 1)
                    nc.vector.tensor_tensor(lo[:, b % 2, 4 * n:4 * n + 4, :].rearrange("p k n -> p (k n)"), ps[2 * (b % 2) + n][:, :],
                                            hi[:, b % 2, 4 * n:4 * n + 4, :].rearrange("p k n -> p (k n)").bitcast(F32), ALU.subtract).then_inc(s_lo, 1)

            for b in range(NT + 1):
                if b == 0:
                    w.part_lo(dve, 0)
                    w.part_lo(dve, 1)
                if b < NT:
                    lows(b)
                if b == 0:
                    for k in range(2, KD):
                        w.part_lo(dve, k)
                if b >= 1:
                    c = b - 1
                    u = c % 2
                    zx, h2, x2 = (ins[n][:, u, :] for n in ("zx", "h2", "x2"))
                    dve.wait_ge(arrived[u], 48 * (c // 2 + 1))
                    dve.wait_ge(s_mm, c + 1)
                    for n in range(2):
                        cut = slice(n * HALF, (n + 1) * HALF)
                        last = nc.vector.tensor_tensor(zx[:, cut], ps[4 + 2 * u + n][:, :], zx[:, cut], ALU.add)
                    chain.up(last)
                    dve.wait_ge(s_chain, chain.n)
                    nc.vector.sem_inc(s_z, 1)
                    dve.wait_ge(s_th, c + 1)
                    link(nc.vector.tensor_tensor(th[:, u, :], th[:, u, :], h2, ALU.subtract))
                    link(nc.vector.tensor_tensor(th[:, u, :], th[:, u, :], zx, ALU.mult))
                    link(nc.vector.tensor_tensor(x2, x2, h2, ALU.add))
                    nc.vector.tensor_tensor(X[:, c, :], x2, th[:, u, :], ALU.add).then_inc(s_x, 1)
                    dve.wait_ge(s_x, b)
                    st.tile(X, c, link)

        @block.tensor
        def _(pe):
            def turn(b):
                for n in range(2):
                    if b >= 2:
                        pe.wait_ge(s_lo, 2 * (b - 2) + n + 1)
                    for k in range(4):
                        last = nc.tensor.transpose(ps[2 * (b % 2) + n][:, k * P:(k + 1) * P], X[:, b, (4 * n + k) * P:(4 * n + k + 1) * P], cst["ident"][:, :])
                    last.then_inc(s_turn, 1)

            turn(0)
            for b in range(NT):
                if b + 1 < NT:
                    turn(b + 1)
                if b >= 2:
                    pe.wait_ge(s_z, b - 1)
                for k in range(KD):
                    if b == 0:
                        pe.wait_ge(w.lo_out, k + 1)
                    if k % 4 == 0:
                        pe.wait_ge(s_lo, 2 * b + k // 4 + 1)
                    for x_, w_, f, e in ((hi, w.hi, k == 0, False), (hi, w.lo, False, False), (lo, w.hi, False, k == KD - 1)):
                        for n in range(2):
                            last = nc.tensor.matmul(ps[4 + 2 * (b % 2) + n][:, :], x_[:, b % 2, k, :], w_[:, k, n * HALF:(n + 1) * HALF], start=f, stop=e)
                last.then_inc(s_mm, 1)


def linear_phase(nc, a, t, cst, X, ps, st, dinv):
    with Phase(nc) as ctx:
        def sb(name, shape, dt=F32):
            return ctx.enter_context(nc.sbuf_tensor("l_" + name, shape, dt))

        def sem(name):
            return ctx.sem("l_" + name)

        ln = LayerNormRelu(ctx, nc, "l3", ps)
        st.begin(ctx, "l3s")
        stage = sb("stage", [P, KD, D])
        w_hi, w_lo = sb("w_hi", [P, KD, D], F32R), sb("w_lo", [P, KD, D], F32R)
        bias = sb("bias", [P, D])
        s_in, s_bias = [sem(f"w_in{o}") for o in range(KD)], sem("bias_in")
        s_turn, s_hi, s_lo, s_done, s_chain = sem("w_turned"), sem("w_hi_out"), sem("w_lo_out"), sem("read"), sem("v_chain")
        block = ctx.enter_context(nc.Block())

        @block.sync
        def _(sp):
            for o in range(KD):
                sp.dma_start(stage[:, o, :], a["L3_gnn_W"][o * P:(o + 1) * P, :]).then_inc(s_in[o], 16)
            sp.dma_start(bias[:, :], row_broadcast(a["L3_gnn_b"], D)).then_inc(s_bias, 16)

        @block.scalar
        def _(act):
            st.scalar(act)
            act_h(nc, act, ln, X, st, 0)
            act_h(nc, act, ln, X, st, 1)
            for g in range(2 * KD):
                o, n = g // 2, g % 2
                if g == 2:
                    ln.part_hi(act, 0)
                act.wait_ge(s_turn, g + 1)
                nc.scalar.activation(w_hi[:, 4 * n:4 * n + 4, o * P:(o + 1) * P], ps[4 + g % 4][:, :].rearrange("p (k n) -> p k n", n=P), ACT.Copy).then_inc(s_hi, 1)
            for b in range(NT):
                if b >= 1:
                    if b + 1 < NT:
                        act_h(nc, act, ln, X, st, b + 1)
                    ln.part_hi(act, b)

        @block.vector
        def _(dve):
            st.vector(dve)
            for g in range(2 * KD):
                o, n = g // 2, g % 2
                if g == 2:
                    ln.part_lo(dve, 0)
                dve.wait_ge(s_hi, g + 1)
                nc.vector.tensor_tensor(w_lo[:, 4 * n:4 * n + 4, o * P:(o + 1) * P], ps[4 + g % 4][:, :].rearrange("p (k n) -> p k n", n=P),
                                        w_hi[:, 4 * n:4 * n + 4, o * P:(o + 1) * P].bitcast(F32), ALU.subtract).then_inc(s_lo, 1)
            dve.wait_ge(s_bias, 16)
            for b in range(NT + 1):
                if 1 <= b < NT:
                    ln.part_lo(dve, b)
                if b >= 1:
                    c = b - 1
                    dve.wait_ge(ln.used, c + 1)
                    for n in range(2):
                        cut = slice(n * HALF, (n + 1) * HALF)
                        last = nc.vector.tensor_tensor(X[:, c, cut], ps[4 + 2 * (c % 2) + n][:, :], bias[:, cut], ALU.add)
                    last.then_inc(s_done, 1)
                    dve.wait_ge(s_done, c + 1)
                    nc.vector.tensor_scalar(X[:, c, :], X[:, c, :], dinv[:, c:c + 1], None, ALU.mult).then_inc(s_chain, 1)
            dve.wait_ge(s_chain, NT)

        @block.tensor
        def _(pe):
            ln.turn(pe, cst["ident"][:, :], 0)
            ln.turn(pe, cst["ident"][:, :], 1)
            for g in range(2 * KD):
                o, n = g // 2, g % 2
                pe.wait_ge(s_in[o], 16)
                if g >= 4:
                    pe.wait_ge(s_lo, g - 3)
                for k in range(4):
                    last = nc.tensor.transpose(ps[4 + g % 4][:, k * P:(k + 1) * P], stage[:, o, (4 * n + k) * P:(4 * n + k + 1) * P], cst["ident"][:, :])
                last.then_inc(s_turn, 1)
            pe.wait_ge(s_lo, 2 * KD)
            for b in range(NT):
                if 1 <= b and b + 1 < NT:
                    ln.turn(pe, cst["ident"][:, :], b + 1)
                if b >= 2:
                    pe.wait_ge(s_done, b - 1)
                ln.product(pe, b, w_hi, w_lo, [ps[4 + 2 * (b % 2)], ps[5 + 2 * (b % 2)]])


def spread_phase(nc, a, t, cst, X, ps, dinv, out):
    with Phase(nc) as ctx:
        def sb(name, shape, dt=F32):
            return ctx.enter_context(nc.sbuf_tensor("f_" + name, shape, dt))

        def sem(name):
            return ctx.sem("f_" + name)

        c = sb("c", [P, NT, NP], F32R)
        y_hi, y_lo = sb("y_hi", [P, NT, D], F32R), sb("y_lo", [P, NT, D], F32R)
        x3 = sb("x3", [P, 2, D])
        s_c = [sem(f"c_in{k}") for k in range(NT)]
        s_hi, s_lo = sem("y_hi_out"), sem("y_lo_out")
        s_x, s_mm, s_add, s_out = [sem("x_in0"), sem("x_in1")], sem("sums_done"), sem("x_added"), sem("out")
        block = ctx.enter_context(nc.Block())

        @block.gpsimd
        def _(pool):
            for k in range(NT):
                pool.dma_start(c[:, k, :], t["counts"][k * P:(k + 1) * P, :]).then_inc(s_c[k], 16)

        @block.scalar
        def _(act):
            for k in range(NT):
                nc.scalar.activation(y_hi[:, k, :], X[:, k, :], ACT.Copy).then_inc(s_hi, 1)

        @block.sync
        def _(sp):
            for b in range(NT + 1):
                if b < NT:
                    if b >= 2:
                        sp.wait_ge(s_out, 16 * (b - 1))
                    sp.dma_start(x3[:, b % 2, :], t["x3"][b * P:(b + 1) * P, :]).then_inc(s_x[b % 2], 16)
                if b >= 1:
                    q = b - 1
                    rows = P if q < NT - 1 else TAIL
                    sp.wait_ge(s_add, q + 1)
                    sp.dma_start(out[q * P:q * P + rows, :], x3[0:rows, q % 2, :]).then_inc(s_out, 16)
            sp.wait_ge(s_out, 16 * NT)

        @block.vector
        def _(dve):
            for k in range(NT):
                dve.wait_ge(s_hi, k + 1)
                nc.vector.tensor_tensor(y_lo[:, k, :], X[:, k, :], y_hi[:, k, :].bitcast(F32), ALU.subtract).then_inc(s_lo, 1)
            for b in range(NT):
                dve.wait_ge(s_x[b % 2], 16 * (b // 2 + 1))
                dve.wait_ge(s_mm, b + 1)
                for n in range(2):
                    cut = slice(n * HALF, (n + 1) * HALF)
                    last = nc.vector.scalar_tensor_tensor(out=x3[:, b % 2, cut], in0=ps[2 * (b % 4) + n][:, :], scalar=dinv[:, b:b + 1],
                                                          in1=x3[:, b % 2, cut], op0=ALU.mult, op1=ALU.add)
                last.then_inc(s_add, 1)

        @block.tensor
        def _(pe):
            def step(b, k):
                for y, f, e in ((y_hi, k == 0, False), (y_lo, False, k == NT - 1)):
                    for n in range(2):
                        last = nc.tensor.matmul(ps[2 * (b % 4) + n][:, :], c[:, k, b * P:(b + 1) * P], y[:, k, n * HALF:(n + 1) * HALF], start=f, stop=e)
                if k == NT - 1:
                    last.then_inc(s_mm, 1)

            for k in range(NT):
                pe.wait_ge(s_c[k], 16)
                pe.wait_ge(s_lo, k + 1)
                for b in range(4):
                    step(b, k)
            for b in range(4, NT):
                pe.wait_ge(s_add, b - 3)
                for k in range(NT):
                    step(b, k)


def constants(nc, cst):
    with Phase(nc) as ctx:
        s_set, s_sel = (ctx.sem(n) for n in ("cst_set", "cst_selected"))
        block = ctx.enter_context(nc.Block())

        @block.gpsimd
        def _(pool):
            nc.gpsimd.memset(cst["ident"][:, :], 0.0).then_inc(s_set, 1)
            nc.gpsimd.memset(cst["tri"][:, :], 1.0).then_inc(s_set, 1)
            pool.wait_ge(s_set, 2)
            nc.gpsimd.affine_select(out=cst["ident"][:, :], in_=cst["ident"][:, :], compare_op=ALU.not_equal, fill=1.0,
                                    base=0, pattern=[[-1, P]], channel_multiplier=1).then_inc(s_sel, 1)
            nc.gpsimd.affine_select(out=cst["tri"][:, :], in_=cst["tri"][:, :], compare_op=ALU.is_gt, fill=0.0,
                                    base=0, pattern=[[1, P]], channel_multiplier=-1).then_inc(s_sel, 1)
            pool.wait_ge(s_sel, 2)

        @block.vector
        def _(dve):
            nc.vector.memset(cst["weigh"][:, 0:1], 1.0)
            nc.vector.memset(cst["weigh"][:, 1:2], 1.0 + LATER)
            nc.vector.memset(cst["weigh"][:, 2:3], LATER)
            nc.vector.memset(cst["ones"][:, :], 1.0)
            nc.vector.memset(cst["ones16"][:, :], 1.0)


def gnn_kernel(nc, a, out, stop=None):
    t = {"xl": nc.dram_tensor("t_xl", [NP, HL], F32, kind="Internal").ap(),
         "xr": nc.dram_tensor("t_xr", [NP, HL], F32, kind="Internal").ap(),
         "pairs": nc.dram_tensor("t_pairs", [NP * NP + CE, PAY], F32, kind="Internal").ap(),
         "typed": nc.dram_tensor("t_typed", [R * NP * NP + CE, 1], F32, kind="Internal").ap(),
         "counts": nc.dram_tensor("t_counts", [NP, NP], F32, kind="Internal").ap()}
    for n in ("x2", "x3", "h2", "zx"):
        t[n] = nc.dram_tensor("t_" + n, [NP, D], F32, kind="Internal").ap()

    with Phase(nc) as ctx:
        def sb(name, shape, dt=F32):
            return ctx.enter_context(nc.sbuf_tensor(name, shape, dt))

        ps = [ctx.enter_context(nc.psum_tensor(f"bank{i}", [P, HALF], F32)) for i in range(8)]
        cst = {"ident": sb("ident", [P, P]), "tri": sb("tri", [P, P], F16), "weigh": sb("weigh", [P, 4], F16),
               "ones": sb("ones", [P, 2]), "ones16": sb("ones16", [P, 2], F16)}
        X = sb("x", [P, NT, D])
        al, ar, dinv = sb("al", [P, NT]), sb("ar", [P, NT]), sb("dinv", [P, NT])
        constants(nc, cst)
        st = Norm(nc, sb)
        keep = {"mult8": sb("mult8", [P, EC]), "idx8": sb("idx8", [P, EC], I32)}
        with ExitStack() as part:
            def keep_sb(name, shape, dt=F32):
                return part.enter_context(nc.sbuf_tensor(name, shape, dt))
            keep["xl"] = keep_sb("keep_xl", [P, NT, H, DH + 2])
            edge_phase(nc, a, t, cst, X, ps, keep, st)
            pair_phase(nc, a, t, cst, X, ps, keep, st)
        with nc.sbuf_tensor("h1", [P, NT, D], F32) as h1:
            attention_phase(nc, a, t, cst, X, ps, st, h1, al, ar, keep)
        neighbour_phase(nc, a, t, cst, X, ps, st, h1, al, ar, dinv, keep)
        with ExitStack() as part:
            h16 = part.enter_context(nc.sbuf_tensor("h16", [P, 2, NT, D], F16))
            gate_x_phase(nc, a, t, cst, X, ps, st, h16)
            root_phase(nc, a, t, cst, X, ps, st)
            relation_phase(nc, a, t, cst, X, ps, h16)
        gate_phase(nc, a, t, cst, X, ps, st)
        linear_phase(nc, a, t, cst, X, ps, st, dinv)
        spread_phase(nc, a, t, cst, X, ps, dinv, out)


_INS = ["x", "src", "dst", "edge_type_8", "L0_gnn_rms_w", "L0_gnn_W_down", "L0_gnn_Wl", "L0_gnn_Wr", "L0_gnn_att", "L0_gnn_W_up",
        "L1_gnn_W", "L1_gnn_a", "L2_gnn_weight", "L2_gnn_root", "L2_gnn_bias", "L2_gnn_w_gate", "L2_gnn_b_gate", "L3_gnn_W", "L3_gnn_b"]


def kernel(**inputs):
    import numpy as _np
    import concourse.bacc as _bacc
    from concourse import mybir as _mybir
    from concourse.bass_utils import run_bass_kernel_spmd as _run

    nc = _bacc.Bacc("TRN2", target_bir_lowering=False, num_devices=1)
    arrays, args = {}, {}
    for name in _INS:
        x = _np.ascontiguousarray(inputs[name])
        arrays[f"in_{name}_dram"] = x
        args[name] = nc.dram_tensor(f"in_{name}_dram", x.shape, _mybir.dt.from_np(x.dtype), kind="ExternalInput").ap()
    out = nc.dram_tensor("out_0_dram", (N, D), _mybir.dt.float32, kind="ExternalOutput").ap()
    gnn_kernel(nc, args, out)
    r = _run(nc, [arrays], core_ids=[0])
    return r.results[0]["out_0_dram"]
```
